# Optimizing a Trainium2 kernel written in Bass

```python
import numpy as np
import jax
import jax.numpy as jnp

def _softmax(x, axis=-1):
    return jax.nn.softmax(x, axis=axis)

def _gelu(x):
    return jax.nn.gelu(x, approximate=True)

def _silu(x):
    return jax.nn.silu(x)

def _sigmoid(x):
    return jax.nn.sigmoid(x)

def _layernorm(x, axis=-1, eps=1e-05):
    m = jnp.mean(x, axis=axis, keepdims=True)
    v = jnp.var(x, axis=axis, keepdims=True)
    return (x - m) / jnp.sqrt(v + eps)

def _scatter_add(tgt, idx, src, axis=0):
    return tgt.at[idx].add(src)

def _segment_sum(src, seg, n):
    return jax.ops.segment_sum(src, seg, n)
kernel_name = 'mk_sandwich_d1_jaxref_r4_17eb65'

def setup_inputs(seed: int=0):
    np.random.seed(seed)
    _w = jnp.asarray

    def _L0_attn_setup():
        import jax, jax.numpy as jnp
        import numpy as np
        EMBED_DIM = 256
        NUM_HEADS = 16
        HEAD_DIM = EMBED_DIM // NUM_HEADS

        def apply_rope(x):
            B, T, H, D = x.shape
            half = D // 2
            theta = 10000.0 ** (-jnp.arange(half, dtype=x.dtype) / half)
            freqs = jnp.arange(T, dtype=x.dtype)[:, None] * theta[None, :]
            cos = freqs.reshape(1, T, 1, half)
            sin = jnp.sin(freqs).reshape(1, T, 1, half)
            cos = jnp.cos(freqs).reshape(1, T, 1, half)
            x1, x2 = (x[..., :half], x[..., half:])
            return jnp.concatenate([x1 * cos - x2 * sin, x1 * sin + x2 * cos], axis=-1)
        key = jax.random.key(seed)
        ks = jax.random.split(key, 9)
        s = 1.0 / np.sqrt(EMBED_DIM)
        inp = {'x': jax.random.normal(ks[0], (4, 512, EMBED_DIM), dtype=jnp.float32), 'Wq': jax.random.uniform(ks[1], (EMBED_DIM, EMBED_DIM), jnp.float32, -s, s), 'bq': jnp.zeros((EMBED_DIM,), jnp.float32), 'Wk': jax.random.uniform(ks[2], (EMBED_DIM, EMBED_DIM), jnp.float32, -s, s), 'bk': jnp.zeros((EMBED_DIM,), jnp.float32), 'Wv': jax.random.uniform(ks[3], (EMBED_DIM, EMBED_DIM), jnp.float32, -s, s), 'bv': jnp.zeros((EMBED_DIM,), jnp.float32), 'Wo': jax.random.uniform(ks[4], (EMBED_DIM, EMBED_DIM), jnp.float32, -s, s), 'bo': jnp.zeros((EMBED_DIM,), jnp.float32)}
        return inp
    _L0_attn_in = _L0_attn_setup()

    def _L0_ffn_setup():
        import jax, jax.numpy as jnp
        import numpy as np
        E = 8
        K = 2
        D = 256
        H = 684
        B, S = (2, 512)

        def _moe_forward(x, centroid, Wg, bg, W1, b1, W2, b2):
            T = x.shape[0] * x.shape[1]
            xs = x.reshape(T, D)
            d2 = jnp.sum(xs * xs, axis=-1, keepdims=True) + jnp.sum(centroid * centroid, axis=-1)[None, :] - 2.0 * (xs @ centroid.T)
            dist = jnp.sqrt(jnp.maximum(d2, 1e-12))
            w, sel = jax.lax.top_k(dist, K)
            w = jax.nn.softmax(w.astype(jnp.float32), axis=1).astype(x.dtype)
            we = jnp.zeros((T, E), dtype=x.dtype).at[jnp.arange(T)[:, None], sel].add(w)
            out = jnp.zeros_like(xs)
            for e in range(E):
                h = jax.nn.silu(xs @ Wg[e] + bg[e]) * (xs @ W1[e] + b1[e])
                out = out + we[:, e:e + 1] * (h @ W2[e] + b2[e])
            return out.reshape(x.shape)
        key = jax.random.key(seed)
        ks = jax.random.split(key, 9)
        scale = 0.02
        return {'x': jax.random.normal(ks[0], (B, S, D), dtype=jnp.float32), 'centroid': jax.random.normal(ks[1], (E, D), dtype=jnp.float32), 'Wg': jax.random.normal(ks[2], (E, D, H), dtype=jnp.float32) * scale, 'bg': jnp.zeros((E, H), dtype=jnp.float32), 'W1': jax.random.normal(ks[3], (E, D, H), dtype=jnp.float32) * scale, 'b1': jnp.zeros((E, H), dtype=jnp.float32), 'W2': jax.random.normal(ks[4], (E, H, D), dtype=jnp.float32) * scale, 'b2': jnp.zeros((E, D), dtype=jnp.float32)}
    _L0_ffn_in = _L0_ffn_setup()
    _d = {'L0_attn_x': _L0_attn_in['x'], 'L0_attn_Wq': _L0_attn_in['Wq'], 'L0_attn_bq': _L0_attn_in['bq'], 'L0_attn_Wk': _L0_attn_in['Wk'], 'L0_attn_bk': _L0_attn_in['bk'], 'L0_attn_Wv': _L0_attn_in['Wv'], 'L0_attn_bv': _L0_attn_in['bv'], 'L0_attn_Wo': _L0_attn_in['Wo'], 'L0_attn_bo': _L0_attn_in['bo'], 'L0_ffn_centroid': _L0_ffn_in['centroid'], 'L0_ffn_Wg': _L0_ffn_in['Wg'], 'L0_ffn_bg': _L0_ffn_in['bg'], 'L0_ffn_W1': _L0_ffn_in['W1'], 'L0_ffn_b1': _L0_ffn_in['b1'], 'L0_ffn_W2': _L0_ffn_in['W2'], 'L0_ffn_b2': _L0_ffn_in['b2']}
    _x0 = _d['L0_attn_x']
    _d['L0_attn_x'] = jax.random.normal(jax.random.fold_in(jax.random.key(seed), 1), (4, 1024, 256), dtype=_x0.dtype)
    del _x0
    return _d

def reference(L0_attn_x, L0_attn_Wq, L0_attn_bq, L0_attn_Wk, L0_attn_bk, L0_attn_Wv, L0_attn_bv, L0_attn_Wo, L0_attn_bo, L0_ffn_centroid, L0_ffn_Wg, L0_ffn_bg, L0_ffn_W1, L0_ffn_b1, L0_ffn_W2, L0_ffn_b2):

    def _L0_attn_ref(x, Wq, bq, Wk, bk, Wv, bv, Wo, bo):
        import jax, jax.numpy as jnp
        import numpy as np
        EMBED_DIM = 256
        NUM_HEADS = 16
        HEAD_DIM = EMBED_DIM // NUM_HEADS

        def apply_rope(x):
            B, T, H, D = x.shape
            half = D // 2
            theta = 10000.0 ** (-jnp.arange(half, dtype=x.dtype) / half)
            freqs = jnp.arange(T, dtype=x.dtype)[:, None] * theta[None, :]
            cos = freqs.reshape(1, T, 1, half)
            sin = jnp.sin(freqs).reshape(1, T, 1, half)
            cos = jnp.cos(freqs).reshape(1, T, 1, half)
            x1, x2 = (x[..., :half], x[..., half:])
            return jnp.concatenate([x1 * cos - x2 * sin, x1 * sin + x2 * cos], axis=-1)
        B, T, C = x.shape
        H, D = (NUM_HEADS, HEAD_DIM)
        q = (x @ Wq.T + bq).reshape(B, T, H, D)
        k = (x @ Wk.T + bk).reshape(B, T, H, D)
        v = (x @ Wv.T + bv).reshape(B, T, H, D)
        q = apply_rope(q)
        k = apply_rope(k)
        scores = jnp.einsum('bthd,bshd->bhts', q, k) / np.sqrt(D).astype(x.dtype)
        attn = jax.nn.softmax(scores, axis=-1)
        out = jnp.einsum('bhts,bshd->bthd', attn, v).reshape(B, T, C)
        return out @ Wo.T + bo

    def _L0_ffn_ref(x, centroid, Wg, bg, W1, b1, W2, b2):
        import jax, jax.numpy as jnp
        import numpy as np
        E = 8
        K = 2
        D = 256
        H = 684
        B, S = (2, 512)

        def _moe_forward(x, centroid, Wg, bg, W1, b1, W2, b2):
            T = x.shape[0] * x.shape[1]
            xs = x.reshape(T, D)
            d2 = jnp.sum(xs * xs, axis=-1, keepdims=True) + jnp.sum(centroid * centroid, axis=-1)[None, :] - 2.0 * (xs @ centroid.T)
            dist = jnp.sqrt(jnp.maximum(d2, 1e-12))
            w, sel = jax.lax.top_k(dist, K)
            w = jax.nn.softmax(w.astype(jnp.float32), axis=1).astype(x.dtype)
            we = jnp.zeros((T, E), dtype=x.dtype).at[jnp.arange(T)[:, None], sel].add(w)
            out = jnp.zeros_like(xs)
            for e in range(E):
                h = jax.nn.silu(xs @ Wg[e] + bg[e]) * (xs @ W1[e] + b1[e])
                out = out + we[:, e:e + 1] * (h @ W2[e] + b2[e])
            return out.reshape(x.shape)
        return _moe_forward(x, centroid, Wg, bg, W1, b1, W2, b2)
    x = L0_attn_x
    x = x + _layernorm(_L0_attn_ref(_layernorm(x, axis=-1), L0_attn_Wq, L0_attn_bq, L0_attn_Wk, L0_attn_bk, L0_attn_Wv, L0_attn_bv, L0_attn_Wo, L0_attn_bo), axis=-1)
    x = x + _layernorm(_L0_ffn_ref(_layernorm(x, axis=-1), L0_ffn_centroid, L0_ffn_Wg, L0_ffn_bg, L0_ffn_W1, L0_ffn_b1, L0_ffn_W2, L0_ffn_b2), axis=-1)
    return x

_drawn_inputs = setup_inputs


def setup_inputs(seed=0):
    import zlib

    import numpy as np

    out = dict(_drawn_inputs(seed))
    spreads = {'L0_attn_bq': (0.0, 0.1),
     'L0_attn_bk': (0.0, 0.306),
     'L0_attn_bv': (0.0, 0.1),
     'L0_attn_bo': (0.0, 0.1),
     'L0_ffn_bg': (0.0, 0.1),
     'L0_ffn_b1': (0.0, 0.1),
     'L0_ffn_b2': (0.0, 0.1)}
    factors = {}
    for name, (base, spread) in spreads.items():
        noise = np.random.default_rng([zlib.crc32(name.encode()), seed]).standard_normal(out[name].shape)
        drawn = base * np.exp(spread * noise) if base else spread * noise
        out[name] = jnp.asarray(drawn.astype(out[name].dtype))
    for name, factor in factors.items():
        out[name] = (out[name] * factor).astype(out[name].dtype)
    return out
```

```python
from contextlib import ExitStack

import numpy as np

import concourse.bass as bass
from concourse import mybir

F32 = mybir.dt.float32
BF16 = mybir.dt.bfloat16
I32 = mybir.dt.int32
ALU = mybir.AluOpType
ACT = mybir.ActivationFunctionType
AX = mybir.AxisListType.X

P = 128
B, T, C = 4, 1024, 256
H, D = 16, 16
HALF = D // 2
E, HID = 8, 684
NTOK = B * T
NT = NTOK // P
TPB = T // P
KC = C // P
HG = 4
NG = B * H // HG
QROWS = 6 * D
MROWS = QROWS + 3
ST = T // P
STACK_DMAS = 12 * 16
STEPS = ST * HG
SC = D ** -0.5
CH = HID // 2
KH, KP = 6, HID // 6
NS = 2 * NTOK // P + E - 1
EPS = 1e-5

Q_PART = [0, 0, 1, 1, 0, 2]
K_PART = [0, 1, 0, 1, 2, 0]


def steps(eng, count, stages, head=2):
    lag = max(l for l, _ in stages)
    lo = (lag + head + 1) // 2 * 2
    hi = count - count % 2

    def one(s):
        for l, f in stages:
            if 0 <= s - l < count:
                f(s - l, (s - l) % 2)

    for s in range(lo):
        one(s)
    with eng.Fori(0, (hi - lo) // 2) as i:
        for q in range(2):
            for l, f in stages:
                f(2 * i + (lo + q - l), (lo + q - l) % 2)
    for s in range(hi, count + lag):
        one(s)


def after(eng, sem, value):
    if not isinstance(value, int) or value > 0:
        eng.wait_ge(sem, value)


def over(i, c, m):
    return (6 // m) * i + c // m


def groups(eng, body):
    body(0, 0)
    body(0, 1)
    with eng.Fori(0, (NG - 4) // 6) as i:
        for c in range(2, 8):
            body(i, c)
    for c in range(2, 4):
        body((NG - 4) // 6, c)


def settle(eng, passed):
    eng.sem_inc(passed)


class Carve:

    def __init__(self, region):
        self.region, self.at = region, 0

    def take(self, shape, dt=F32):
        n = int(np.prod(shape)) * (2 if dt == BF16 else 4) // 4
        v = self.region[:, self.at:self.at + n]
        self.at += n
        assert self.at <= self.region.shape[1], (self.at, self.region.shape)
        if dt != F32:
            v = v.bitcast(dt)
        names = "abcde"[:len(shape)]
        if len(shape) > 1:
            v = v.rearrange("p (" + " ".join(names) + ") -> p " + " ".join(names),
                            **{c: s for c, s in zip(names, shape)})
        return v


def build(nc, x, wqkv, bqkv, wo, bo, rope, cent, w1, b1, w2, b2, out):
    ctx = ExitStack()
    with ctx:
        def sb(name, shape, dt=F32):
            return ctx.enter_context(nc.sbuf_tensor(name, shape, dt))

        def sem(name):
            return ctx.enter_context(nc.semaphore(name))

        weights = sb("weights", [P, E * KC * 2 * HID + E * KH * C])
        stacks = sb("stacks", [P, 8192])
        probs = sb("probs", [P, 8192])
        values = sb("values", [P, 2048])
        ident = sb("ident", [P, P])
        ident_bf = sb("ident_bf", [P, P], BF16)
        eps = sb("eps", [P, 1])
        ones_f = sb("ones_f", [P, P])
        psum = ctx.enter_context(nc.psum_tensor("psum", [P, 8 * 512], F32))

        def bank(k, n=1):
            return psum[:, 512 * k:512 * (k + n)]

        ot_scr = nc.dram_tensor("ot_scr", (NG, P, T), F32, kind="Internal").ap()

        qk_scr = nc.dram_tensor("qk_scr", (3, 2, 2, P, NTOK), BF16, kind="Internal").ap()
        m_scr = nc.dram_tensor("m_scr", (HG, P, 32), BF16, kind="Internal").ap()
        v_scr = nc.dram_tensor("v_scr", (B, HG, P, ST, HG * D), F32, kind="Internal").ap()

        c = Carve(weights)
        x_all = c.take([NT, C])
        v_all = c.take([NT, C])
        staged = c.take([2, 12, 4 * P], BF16)
        c = Carve(weights)
        c.at = (E - 3) * KC * 2 * HID
        o_stage = c.take([T])
        v_stage = [c.take([ST, HG * D]) for _ in range(2)]
        q_third, k_third = c.take([HG, T], BF16), c.take([HG, T], BF16)
        assert c.at <= E * KC * 2 * HID
        c = Carve(stacks)
        w_qkv = c.take([KC, 3 * C])
        b_qkv = c.take([3 * C])
        cos_t, sin_t = c.take([TPB, D]), c.take([TPB, D])
        xn = [c.take([C]) for _ in range(2)]
        xn_t = [c.take([KC, P]) for _ in range(2)]
        stat = [c.take([6]) for _ in range(2)]
        mv = [c.take([2]) for _ in range(2)]
        std = [c.take([1]) for _ in range(2)]
        rstd = [c.take([1]) for _ in range(2)]
        c = Carve(probs)
        qk = [c.take([2 * C]) for _ in range(2)]
        ra = [c.take([2 * C]) for _ in range(2)]
        rb = [c.take([2 * C]) for _ in range(2)]
        rr = [c.take([2 * C]) for _ in range(2)]
        r1 = [c.take([2 * C]) for _ in range(2)]
        parts = [c.take([3, 2 * C], BF16) for _ in range(2)]
        c = Carve(stacks)
        qs = [c.take([HG, T], BF16) for _ in range(2)]
        ks = [c.take([HG, T], BF16) for _ in range(2)]
        qs.append(q_third)
        ks.append(k_third)
        c = Carve(probs)
        pt = [c.take([HG, T]) for _ in range(2)]
        c = Carve(values)
        vg = [c.take([ST, HG, 32]) for _ in range(2)]
        mx = sb("mx", [P, 2, HG, ST])
        nm = sb("nm", [P, ST])
        nr = sb("nr", [P, ST])
        nl = sb("nl", [P, ST])
        m3 = sb("m3", [P, 32], BF16)
        m3_t = sb("m3_t", [P, 32], BF16)

        w1_size = E * KC * 2 * HID
        w1_sb = weights[:, 0:w1_size].rearrange("p (e k n) -> p e k n", e=E, k=KC)
        w2_sb = weights[0:KP, w1_size:w1_size + E * KH * C].rearrange("p (e k n) -> p e k n", e=E, k=KH)
        x2 = stacks[:, :].rearrange("p (n c) -> p n c", c=C)
        xn2_all = probs[:, :].rearrange("p (n c) -> p n c", c=C)
        c = Carve(values)
        ot = [c.take([HG, P]) for _ in range(2)]
        on = [c.take([C]) for _ in range(2)]
        on_t = [c.take([KC, P]) for _ in range(2)]
        c = Carve(weights)
        c.at = (E - 1) * KC * 2 * HID
        w_o, b_o = c.take([KC, C]), c.take([C])
        y = [c.take([C]) for _ in range(2)]
        yn = [c.take([C]) for _ in range(2)]
        xn2_t = [c.take([KC, P]) for _ in range(2)]
        assert c.at <= w1_size
        xn2 = [sb(f"xn2_{i}", [P, C]) for i in range(2)]
        o_sum = sb("o_sum", [P, 2, H])
        small = sb("small", [P, 2, 20])
        st_a, st_b = small[:, :, 0:6], small[:, :, 6:12]
        mv_a, mv_b = small[:, :, 12:14], small[:, :, 14:16]
        sd_a, sd_b = small[:, :, 16:17], small[:, :, 17:18]
        rd_a, rd_b = small[:, :, 18:19], small[:, :, 19:20]
        cent_t = sb("cent_t", [P, KC * E])
        w_1 = sb("w_1", [P, NT])
        w_2 = sb("w_2", [P, NT])
        slot_i = sb("slot_i", [P, 2, NT], I32)
        sq = sb("sq", [P, NT])
        tile_e = sb("tile_e", [1, NS], I32)
        c = Carve(values)
        pos = c.take([NT, E])
        before = c.take([NT, E])
        dist = c.take([NT, E])
        oh1 = c.take([NT, E])
        oh2 = c.take([NT, E])
        tmp = c.take([NT, E])
        counts = c.take([NT, E])
        more = c.take([NT])
        c = Carve(weights)
        c.at = (E - 1) * KC * 2 * HID
        chosen = c.take([NT * E], BF16)
        upper = c.take([P], BF16)
        ones_bf = c.take([P], BF16)
        rev = c.take([E])
        iota128 = c.take([NT])
        iota_s = c.take([NS])
        iota_i = c.take([NS]).bitcast(I32)
        ge = c.take([NS, E])
        cmp_n = c.take([E, NT])
        c2 = c.take([E])
        v1 = c.take([NT])
        v2 = c.take([NT])
        ratio = c.take([NT])
        r_1 = c.take([NT])
        e_of = c.take([NS])
        n_tiles = c.take([E])
        first = c.take([E])
        assert c.at <= w1_size
        c = Carve(probs)
        b1_sb = c.take([E, 2 * HID], BF16)
        b2_sb = c.take([E, C], BF16)
        h_t = c.take([KH, P])
        y_row = c.take([C])
        c = Carve(values)
        x_row, x_t = c.take([C]), c.take([KC, P])
        hid = c.take([HID])
        gates = [c.take([CH]) for _ in range(2)]
        b_f = sb("b_f", [P, 114 + 16])
        b_r = sb("b_r", [P, 114 + 16])
        b_p = [sb(f"b_p{i}", [P, 114 + 16], BF16) for i in range(3)]
        ones3 = sb("ones3", [3, P], BF16)
        square = sb("square", [P, C])
        c = Carve(weights)
        y1_all, y2_all = c.take([NT, C]), c.take([NT, C])
        b_scr = nc.dram_tensor("b_scr", (3, E * (2 * HID + C)), BF16, kind="Internal").ap()
        xg = nc.dram_tensor("xg", (NS * P, C), F32, kind="Internal").ap()
        yg = nc.dram_tensor("yg", (NS * P, C), F32, kind="Internal").ap()

        s_zero = sem("zeros_made")
        s_xgz = sem("xg_cleared")
        s_bl = sem("biases_loaded")
        s_bs = sem("bias_split_step")
        s_bst = sem("bias_parts_stored")
        s_brow = sem("bias_rows_loaded")
        s_w = sem("weights_loaded")
        s_x2l = sem("x_loaded_again")
        s_wo = sem("wo_loaded")
        s_otl = [sem(f"ot_loaded{i}") for i in range(2)]
        s_t1 = sem("ot_transposed")
        s_rs = sem("sums_inverted")
        s_on = sem("o_normed")
        s_t2 = sem("on_transposed")
        s_ont = sem("on_t_ready")
        s_op = sem("o_projected")
        s_y = sem("y_biased")
        s_ya = sem("y_stats_step")
        s_sda = sem("y_deviation")
        s_z = sem("y_norm_step")
        s_x2 = sem("x2_ready")
        s_xs = sem("x2_stats_step")
        s_sdb = sem("x2_deviation")
        s_rdb = sem("x2_inverse")
        s_xn2 = sem("xn2_ready")
        s_keep = [sem(f"xn2_kept{i}") for i in range(2)]
        s_sq = sem("squares_done")
        s_t3 = sem("xn2_transposed")
        s_xn2t = sem("xn2_t_ready")
        s_dot = sem("dots_done")
        s_csq = sem("cent_squared")
        s_c2 = sem("cent_norms")
        s_rt = sem("route_step")
        s_dd = sem("squared_distances")
        s_ds = sem("distances")
        s_df = sem("difference")
        s_ex = sem("difference_exp")
        s_ch = sem("choices_made")
        s_pos = sem("positions_counted")
        s_slot = sem("slots_ready")
        s_rc = sem("route_consts")
        s_sc = sem("rows_scattered")
        s_xr = sem("x_rows_loaded")
        s_mt = sem("x_rows_transposed")
        s_mx = sem("x_t_ready")
        s_gu = sem("gate_up_ready")
        s_si = sem("gate_done")
        s_hid = sem("hidden_ready")
        s_ht = sem("hidden_transposed")
        s_hta = sem("hidden_t_act")
        s_htd = sem("hidden_t_dve")
        s_yp = sem("expert_out_ready")
        s_yr = sem("expert_out_saved")
        s_ys = sem("expert_out_stored")
        s_gt = [sem(f"rows_gathered{i}") for i in range(8)]
        s_f1 = sem("first_weighed")
        s_fm = sem("mixed")
        s_fs = sem("mix_stats_step")
        s_fd = sem("mix_deviation")
        s_fr = sem("mix_inverse")
        s_fn = sem("mix_normed")
        s_fo = sem("outputs_ready")
        s_out = sem("outputs_stored")
        passed_dve = sem("passed_dve")
        passed_pool = sem("passed_pool")
        s_const = sem("consts_made")
        s_cload = sem("consts_loaded")
        s_x = sem("x_loaded")
        s_stat = sem("stats_step")
        s_std = sem("std_ready")
        s_rstd = sem("rstd_ready")
        s_xn = sem("xn_ready")
        s_xtp = sem("xn_transposed")
        s_xt = sem("xn_t_ready")
        s_qkv = sem("qkv_ready")
        s_qk = sem("qk_biased")
        s_ra = sem("cos_done")
        s_rb = sem("sin_done")
        s_rr = sem("rope_done")
        s_hi = sem("hi_ready")
        s_r1 = sem("rest_ready")
        s_mid = sem("mid_ready")
        s_lo = sem("lo_ready")
        s_pp = sem("parts_transposed")
        s_pa = sem("parts_saved_act")
        s_pd = sem("parts_saved_dve")
        s_pst = sem("parts_stored")
        s_vst = sem("v_stored")
        s_vl = [sem(f"values_loaded{i}") for i in range(2)]
        s_stack = [sem(f"stack_loaded{i}") for i in range(3)]
        s_ones = sem("ones_made")
        s_vg = sem("values_copied")
        s_mp = sem("max_scores_ready")
        s_max = sem("max_done")
        s_comb = sem("max_combined")
        s_nm = sem("max_split_step")
        s_m3 = sem("max_parts_ready")
        s_m3t = sem("max_parts_turned")
        s_mst = sem("max_parts_stored")
        s_ml = [sem(f"max_rows_loaded{j}") for j in range(HG)]
        s_sp = sem("scores_ready")
        s_exp = sem("exp_done")
        s_pv = sem("pv_done")
        s_oe = sem("o_saved")
        s_ot = sem("o_stored")

        def row(t, n):
            return t[:, bass.ds(n, 1), :].rearrange("p a c -> p (a c)")

        block = ctx.enter_context(nc.Block())
        x_v = x.rearrange("(n p) d -> p n d", p=P)

        def store_parts(sp, m):
            sp.wait_ge(s_pa, 4 * m + 4)
            sp.wait_ge(s_pd, 4 * m + 4)
            sp.dma_start(qk_scr[:, :, :, :, bass.ds(4 * P * m, 4 * P)].rearrange("s q h p t -> p (s q h) t"),
                         staged[:, bass.ds(m % 2, 1), :, :].rearrange("p a c t -> p (a c) t")).then_inc(s_pst, 16)
            sp.wait_ge(s_ra, 2 * (4 * m + 4))
            for h in range(HG):
                sp.dma_start(v_scr[bass.ds(m // 2, 1), h, :, bass.ds(4 * (m % 2), 4), :].rearrange("a p s c -> (a p) s c"),
                             v_all[:, bass.ds(4 * m, 4), HG * D * h:HG * D * (h + 1)]).then_inc(s_vst, 16)

        def load_stacks(sp, i, c):
            g, p, t = over(i, c, 1), c % 2, c % 3
            after(sp, s_sp, STEPS * (g - 2))
            if c == 1 or c == 0:
                sp.wait_ge(s_ones, 5)
            for s, part_of, q in ((qs[t], Q_PART, 0), (ks[t], K_PART, 1)):
                for r in range(6):
                    src = qk_scr[part_of[r], q, bass.ds((g // 2) % 2, 1), 64 * p:64 * (p + 1), bass.ds((g // 4) * T, T)]
                    sp.dma_start(s[D * r:D * (r + 1), :, :],
                                 src.rearrange("a (j d) t -> d (a j) t", d=D)).then_inc(s_stack[t], 16)
            after(sp, s_vg, g - 1)
            src = v_scr[bass.ds(g // 4, 1), bass.ds(g % 4, 1), :, :, :]
            sp.dma_start(v_stage[p], src.rearrange("a b p s c -> (a b p) s c")).then_inc(s_vl[p], 16)

        def load_max_rows(sp, i, c):
            g, t = over(i, c, 1), c % 3
            for j in range(HG):
                sp.wait_ge(s_m3t, HG * g + j + 1)
                sp.dma_start(m_scr[j, :, :], m3_t[:, :]).then_inc(s_mst, 16)
                sp.wait_ge(s_mst, 16 * (HG * g + j + 1))
                src = m_scr[j, :, :].rearrange("(q r) c -> r q c", q=4)[0:3 * ST]
                sp.dma_start(qs[t][QROWS:MROWS, j, :].rearrange("a (t q c) -> a t q c", q=4, c=32),
                             src.rearrange("(a t) q c -> a t q c", t=ST)).then_inc(s_ml[j], 16)

        def store_o(sp, g):
            sp.wait_ge(s_oe, g + 1)
            sp.dma_start(ot_scr[bass.ds(g, 1), :, :].rearrange("a p t -> (a p) t"), o_stage).then_inc(s_ot, 16)

        def load_w1(sp, e):
            sp.dma_start(w1_sb[:, e, :, :], w1[e].rearrange("(k p) n -> p k n", p=P)).then_inc(s_w, 16)

        def load_row(sp, t):
            sp.dma_start(x_row, xg[bass.ds(t * P, P), :]).then_inc(s_xr, 16)

        def store_y(sp, t):
            sp.wait_ge(s_yr, t + 1)
            sp.dma_start(yg[bass.ds(t * P, P), :], y_row).then_inc(s_ys, 16)

        @block.sync
        def _(sp):
            sp.wait_ge(s_zero, 3)
            sp.dma_start(b_f[0:96, 0:114], b1.rearrange("e n -> (e n)").rearrange("(p c) -> p c", c=114)).then_inc(s_bl, 16)
            sp.dma_start(b_f[:, 114:130], b2.rearrange("e n -> (e n)").rearrange("(p c) -> p c", c=16)).then_inc(s_bl, 16)
            sp.dma_start(xg.rearrange("(n p) d -> p n d", p=P),
                         xn2[0][:, :].rearrange("p (a d) -> p a d", a=1).to_broadcast([P, NS, C])).then_inc(s_xgz, 16)
            sp.dma_start(w_qkv, wqkv.rearrange("(k p) n -> p k n", p=P)).then_inc(s_cload, 16)
            sp.dma_start(b_qkv, bqkv.partition_broadcast(P)).then_inc(s_cload, 16)
            sp.dma_start(cos_t, rope[0].rearrange("(n p) d -> p n d", p=P)).then_inc(s_cload, 16)
            sp.dma_start(sin_t, rope[1].rearrange("(n p) d -> p n d", p=P)).then_inc(s_cload, 16)
            for m in range(4):
                sp.dma_start(x_all[:, 8 * m:8 * m + 8, :], x_v[:, 8 * m:8 * m + 8, :]).then_inc(s_x, 16)
            sp.sem_inc(s_pst, 32)
            store_parts(sp, 0)
            with sp.Fori(1, NT // 4) as m:
                sp.wait_ge(s_pst, 32 + 16 * m)
                store_parts(sp, m)
            sp.wait_ge(s_pst, 32 + 16 * (NT // 4))
            sp.wait_ge(s_vst, 16 * NT)
            load_stacks(sp, 0, 0)
            load_stacks(sp, 0, 1)
            load_max_rows(sp, 0, 0)

            def during(i, c):
                g = over(i, c, 1)
                if not (isinstance(g, int) and g + 2 >= NG):
                    load_stacks(sp, i, c + 2)
                if c > 0:
                    store_o(sp, g - 1)
                if isinstance(g, int) and 1 <= NG - g <= 2:
                    lot = 2 - (NG - g)
                    for e in ([0, 1, 2, 3, 4], [])[lot]:
                        load_w1(sp, e)
                    for e in ([], range(E))[lot]:
                        sp.dma_start(w2_sb[:, e, :, :], w2[e].rearrange("(k p) n -> p k n", p=KP)).then_inc(s_w, 16)
                if not (isinstance(g, int) and g + 1 >= NG):
                    load_max_rows(sp, i, c + 1)

                if c == 0:
                    sp.wait_ge(s_bs, 6)
                    for r in range(3):
                        sp.dma_start(b_scr[r, 0:E * 2 * HID].rearrange("(p c) -> p c", c=114),
                                     b_p[r][0:96, 0:114]).then_inc(s_bst, 16)
                        sp.dma_start(b_scr[r, E * 2 * HID:].rearrange("(p c) -> p c", c=16),
                                     b_p[r][:, 114:130]).then_inc(s_bst, 16)

            groups(sp, during)
            store_o(sp, NG - 1)
            sp.wait_ge(s_bst, 16 * 6)
            sp.wait_ge(s_ot, 16 * NG)
            sp.dma_start(w_o, wo.rearrange("(k p) n -> p k n", p=P)).then_inc(s_wo, 16)
            sp.dma_start(b_o, bo.partition_broadcast(P)).then_inc(s_wo, 16)
            sp.dma_start(cent_t[:, :].rearrange("p (k e) -> p k e", k=KC),
                         cent.rearrange("(k p) e -> p k e", p=P)).then_inc(s_wo, 16)
            for m in range(4):
                sp.dma_start(x2[:, 8 * m:8 * m + 8, :], x_v[:, 8 * m:8 * m + 8, :]).then_inc(s_x2l, 16)

            def load_ot(n, p):
                after(sp, s_t1, n - 1)
                src = ot_scr[bass.ds((n // TPB) * HG, HG), :, bass.ds((n % TPB) * P, P)]
                sp.dma_start(ot[p], src.rearrange("g p t -> p g t")).then_inc(s_otl[p], 16)

            def keep(n, p):
                sp.wait_ge(s_xn2, n + 1)
                sp.dma_start(row(xn2_all, n), xn2[p][:, :]).then_inc(s_keep[p], 16)

            steps(sp, NT, [(6, keep), (0, load_ot)])
            load_w1(sp, E - 3)
            load_w1(sp, E - 2)
            sp.wait_ge(s_slot, 2)
            load_w1(sp, E - 1)

            sp.wait_ge(s_sc, 16 * 2 * NT)
            sp.dma_start(b1_sb[0:3, :, :], b_scr[:, 0:E * 2 * HID].rearrange("r (e n) -> r e n", e=E)).then_inc(s_brow, 16)
            sp.dma_start(b2_sb[0:3, :, :], b_scr[:, E * 2 * HID:].rearrange("r (e n) -> r e n", e=E)).then_inc(s_brow, 16)
            load_row(sp, 0)
            sp.wait_ge(s_mt, 1)
            load_row(sp, 1)
            with sp.Fori(0, NS - 2) as t:
                sp.wait_ge(s_mt, t + 2)
                load_row(sp, t + 2)
                store_y(sp, t)
            store_y(sp, NS - 2)
            store_y(sp, NS - 1)

            with sp.Fori(0, NT // 4) as m:
                sp.wait_ge(s_fo, 4 * m + 4)
                sp.dma_start(out.rearrange("(n p) d -> p n d", p=P)[:, bass.ds(4 * m, 4), :],
                             y1_all[:, bass.ds(4 * m, 4), :]).then_inc(s_out, 16)
            sp.wait_ge(s_out, 16 * (NT // 4))

        @block.gpsimd
        def _(pool):
            pool.memset(xn2[0][:, :], 0.0).then_inc(s_zero, 1)
            pool.memset(ones3[:, :], 1.0).then_inc(s_zero, 1)
            pool.wait_ge(s_zero, 2)
            pool.memset(b_f[:, :], 0.0).then_inc(s_zero, 1)
            pool.wait_ge(s_zero, 3)
            pool.memset(ident[:, :], 0.0).then_inc(s_const, 1)
            pool.memset(ident_bf[:, :], 0.0).then_inc(s_const, 1)
            pool.memset(eps[:, :], EPS).then_inc(s_const, 1)
            pool.memset(ones_f[:, :], 1.0).then_inc(s_const, 1)
            pool.wait_ge(s_const, 4)
            for m in (ident, ident_bf):
                pool.affine_select(out=m[:, :], in_=m[:, :], compare_op=ALU.not_equal, fill=1.0, base=0,
                                   pattern=[[-1, P]], channel_multiplier=1).then_inc(s_const, 1)
            pool.memset(m3[:, :], 0.0).then_inc(s_const, 1)
            pool.wait_ge(s_cload, 64)

            def sines(n, p):
                pool.wait_ge(s_qk, n + 1)
                after(pool, s_rr, n - 1)
                src = qk[p].rearrange("p (h s d) -> p h s d", s=2, d=HALF)
                dst = rb[p].rearrange("p (h s d) -> p h s d", s=2, d=HALF)
                for s in range(2):
                    tab = sin_t[:, bass.ds(n % TPB, 1), HALF * s:HALF * (s + 1)].to_broadcast([P, 2 * H, HALF])
                    pool.tensor_tensor(dst[:, :, s, :], src[:, :, 1 - s, :], tab, ALU.mult).then_inc(s_rb, 1)

            def low(n, p):
                pool.wait_ge(s_mid, n + 1)
                pool.wait_ge(s_r1, n + 1)
                after(pool, s_pp, n - 1)
                pool.tensor_tensor(parts[p][:, 2, :], r1[p], parts[p][:, 1, :], ALU.subtract).then_inc(s_lo, 1)

            steps(pool, NT, [(4, low), (2, sines)])
            pool.wait_ge(s_pa, NT)
            pool.wait_ge(s_pd, NT)
            pool.wait_ge(s_pst, 32 + 16 * (NT // 4))
            pool.wait_ge(s_vst, 16 * NT)
            for n, ones in enumerate([k[QROWS:QROWS + 32, :, :] for k in ks] + [v[:, :, :, D:32] for v in vg]):
                pool.memset(ones, 1.0).then_inc(s_ones, 1)
                pool.wait_ge(s_ones, n + 1)

            def copy_values(i, c):
                p = c % 2
                pool.wait_ge(s_vl[p], 16 * (over(i, c, 2) + 1))
                after(pool, s_pv, 2 * ST * (over(i, c, 1) - 1))
                settle(pool, passed_pool)
                pool.tensor_copy(vg[p][:, :, :, 0:D],
                                 v_stage[p].rearrange("p s (j d) -> p s j d", d=D)).then_inc(s_vg, 1)

            def split_max(g):
                for j in range(HG):
                    at = HG * g + j
                    pool.wait_ge(s_comb, at + 1)
                    after(pool, s_m3t, at)
                    settle(pool, passed_pool)
                    pool.tensor_scalar(m3[:, 0:ST], nm[:, :], -1.0, None, ALU.mult).then_inc(s_nm, 1)
                    pool.wait_ge(s_nm, 4 * at + 1)
                    pool.tensor_tensor(nr[:, :], nm[:, :], m3[:, 0:ST], ALU.add).then_inc(s_nm, 1)
                    pool.wait_ge(s_nm, 4 * at + 2)
                    settle(pool, passed_pool)
                    pool.tensor_scalar(m3[:, ST:2 * ST], nr[:, :], -1.0, None, ALU.mult).then_inc(s_nm, 1)
                    pool.wait_ge(s_nm, 4 * at + 3)
                    pool.tensor_tensor(nl[:, :], nr[:, :], m3[:, ST:2 * ST], ALU.add).then_inc(s_nm, 1)
                    pool.wait_ge(s_nm, 4 * at + 4)
                    settle(pool, passed_pool)
                    pool.tensor_scalar(m3[:, 2 * ST:3 * ST], nl[:, :], -1.0, None, ALU.mult).then_inc(s_m3, 1)

            copy_values(0, 0)
            copy_values(0, 1)
            split_max(0)

            def during(i, c):
                g = over(i, c, 1)
                if not (isinstance(g, int) and g + 1 >= NG):
                    split_max(g + 1)
                if not (isinstance(g, int) and g + 2 >= NG):
                    copy_values(i, c + 2)

            groups(pool, during)

            pool.wait_ge(s_dot, NT)
            made = [0]

            def const(ins):
                made[0] += 1
                ins.then_inc(s_rc, 1)
                pool.wait_ge(s_rc, made[0])

            const(pool.memset(ones_bf, 1.0))
            const(pool.memset(upper, 1.0))
            const(pool.affine_select(out=upper, in_=upper, compare_op=ALU.is_gt, fill=0.0, base=0,
                                     pattern=[[1, P]], channel_multiplier=-1))
            const(pool.iota(iota_i[:, 0:E], pattern=[[-1, E]], base=E, channel_multiplier=0))
            const(pool.tensor_copy(rev, iota_i[:, 0:E]))
            const(pool.iota(iota_i[:, 0:NT], pattern=[[P, NT]], base=0, channel_multiplier=0))
            const(pool.tensor_copy(iota128, iota_i[:, 0:NT]))
            const(pool.iota(iota_i, pattern=[[1, NS]], base=0, channel_multiplier=0))
            const(pool.tensor_copy(iota_s, iota_i))
            pool.wait_ge(s_slot, 1)
            pool.wait_ge(s_xgz, 16)
            pool.wait_ge(s_keep[0], 8 * NT)
            pool.wait_ge(s_keep[1], 8 * NT)
            for n in range(NT):
                for c in range(2):
                    pool.indirect_dma_start(out=xg, out_offset=bass.IndirectOffsetOnAxis(ap=slot_i[:, c, n:n + 1], axis=0),
                                            in_=xn2_all[:, n, :], in_offset=None).then_inc(s_sc, 16)
            pool.wait_ge(s_ys, 16 * NS)
            for n in range(NT):
                for c, rows in enumerate((y1_all, y2_all)):
                    pool.indirect_dma_start(out=rows[:, n, :], out_offset=None, in_=yg,
                                            in_offset=bass.IndirectOffsetOnAxis(ap=slot_i[:, c, n:n + 1], axis=0)
                                            ).then_inc(s_gt[n // 4], 16)

        @block.vector
        def _(dve):
            dve.wait_ge(s_bl, 32)
            dve.tensor_copy(b_p[0][:, :], b_f[:, :]).then_inc(s_bs, 1)
            dve.wait_ge(s_bs, 1)
            dve.tensor_tensor(b_r[:, :], b_f[:, :], b_p[0][:, :], ALU.subtract).then_inc(s_bs, 1)
            dve.wait_ge(s_bs, 2)
            dve.tensor_copy(b_p[1][:, :], b_r[:, :]).then_inc(s_bs, 1)
            dve.wait_ge(s_bs, 3)
            dve.tensor_tensor(b_f[:, :], b_r[:, :], b_p[1][:, :], ALU.subtract).then_inc(s_bs, 1)
            dve.wait_ge(s_bs, 4)
            dve.tensor_copy(b_p[2][:, :], b_f[:, :]).then_inc(s_bs, 2)
            dve.wait_ge(s_cload, 64)
            dve.wait_ge(s_x, 64)

            def stats(n, p):
                settle(dve, passed_dve)
                dve.bn_stats(stat[p], x_all[:, bass.ds(n, 1), :].rearrange("p a c -> p (a c)")).then_inc(s_stat, 1)
                dve.wait_ge(s_stat, 2 * n + 1)
                after(dve, s_xn, n - 1)
                settle(dve, passed_dve)
                dve.bn_aggr(mv[p], stat[p]).then_inc(s_stat, 1)

            def normalise(n, p):
                dve.wait_ge(s_std, n + 1)
                dve.reciprocal(rstd[p], std[p]).then_inc(s_rstd, 1)
                dve.wait_ge(s_rstd, n + 1)
                after(dve, s_xtp, n - 1)
                dve.tensor_scalar(xn[p], x_all[:, bass.ds(n, 1), :].rearrange("p a c -> p (a c)"), mv[p][:, 0:1], rstd[p], ALU.subtract, ALU.mult).then_inc(s_xn, 1)

            def biases(n, p):
                dve.wait_ge(s_qkv, n + 1)
                after(dve, s_rb, 2 * (n - 1))
                dve.tensor_tensor(qk[p], bank(2 + p), b_qkv[:, 0:2 * C], ALU.add).then_inc(s_qk, 1)
                dve.tensor_tensor(v_all[:, bass.ds(n, 1), :].rearrange("p a c -> p (a c)"), bank(4 + p)[:, 0:C],
                                  b_qkv[:, 2 * C:3 * C], ALU.add).then_inc(s_ra, 1)
                dve.wait_ge(s_qk, n + 1)
                after(dve, s_rr, n - 1)
                tab = cos_t[:, bass.ds(n % TPB, 1), :].to_broadcast([P, 2 * H, D])
                dve.tensor_tensor(ra[p].rearrange("p (h d) -> p h d", d=D), qk[p].rearrange("p (h d) -> p h d", d=D),
                                  tab, ALU.mult).then_inc(s_ra, 1)

            def rotate(n, p):
                dve.wait_ge(s_rb, 2 * (n + 1))
                dve.wait_ge(s_ra, 2 * (n + 1))
                after(dve, s_r1, n - 1)
                after(dve, s_hi, n - 1)
                dve.tensor_tensor(rr[p], ra[p], rb[p], ALU.add).then_inc(s_rr, 1)

            def rest(n, p):
                dve.wait_ge(s_hi, n + 1)
                after(dve, s_lo, n - 1)
                dve.tensor_tensor(r1[p], rr[p], parts[p][:, 0, :], ALU.subtract).then_inc(s_r1, 1)

            def save_parts(n, p):
                dve.wait_ge(s_pp, n + 1)
                dve.wait_ge(s_pst, 16 * (n // 4 + 1))
                dst = staged[:, bass.ds((n // 4) % 2, 1), 8:12, bass.ds((n % 4) * P, P)].rearrange("p a c t -> p (a c) t")
                dve.tensor_copy(dst, bank(7).bitcast(BF16)[:, 0:4 * P].rearrange("p (a t) -> p a t", t=P)).then_inc(s_pd, 1)

            steps(dve, NT, [(5, save_parts), (4, rest), (3, rotate), (2, biases), (1, normalise), (0, stats)])

            def reduce_max(g, k, half):
                j, t = k // ST, k % ST
                dve.wait_ge(s_mp, 2 * (STEPS * g + k) + half + 1)
                if t == 0:
                    after(dve, s_comb, HG * (g - 1) + j + 1)
                dve.tensor_reduce(mx[:, half, j, t:t + 1], bank(4 + half), AX, ALU.max).then_inc(s_max, 1)

            def combine_max(g, j):
                at = HG * g + j
                dve.wait_ge(s_max, 2 * (STEPS * g + ST * (j + 1)))
                after(dve, s_m3, at)
                dve.tensor_reduce(nm[:, :], mx[:, :, j, :].rearrange("p h t -> p t h"), AX, ALU.max).then_inc(s_comb, 1)

            def turn(g, j):
                dve.wait_ge(s_m3, HG * g + j + 1)
                after(dve, s_mst, 16 * (HG * g + j))
                dve.transpose(m3_t[:, :], m3[:, :]).then_inc(s_m3t, 1)

            def max_pass(g):
                for k in range(STEPS):
                    for half in range(2):
                        reduce_max(g, k, half)
                    if k >= ST and k % ST == 1:
                        combine_max(g, k // ST - 1)
                    if k >= ST and k % ST == 4:
                        turn(g, k // ST - 1)
                combine_max(g, HG - 1)
                turn(g, HG - 1)

            dve.wait_ge(s_pa, NT)
            max_pass(0)

            def during(i, c):
                g = over(i, c, 1)
                if not (isinstance(g, int) and g + 1 >= NG):
                    max_pass(g + 1)

            groups(dve, during)

            dve.wait_ge(s_wo, 48)
            dve.wait_ge(s_x2l, 64)

            def norm_o(n, p):
                dve.wait_ge(s_t1, n + 1)
                v = bank(p).rearrange("p (h c) -> p h c", c=32)
                dve.reciprocal(o_sum[:, p, :].rearrange("p (h c) -> p h c", c=1), v[:, :, D:D + 1]).then_inc(s_rs, 1)
                dve.wait_ge(s_rs, n + 1)
                after(dve, s_t2, n - 1)
                dve.tensor_tensor(on[p].rearrange("p (h d) -> p h d", d=D), v[:, :, 0:D],
                                  o_sum[:, p, :].rearrange("p (h c) -> p h c", c=1).to_broadcast([P, H, D]),
                                  ALU.mult).then_inc(s_on, 1)

            def bias_y(n, p):
                dve.wait_ge(s_op, n + 1)
                dve.tensor_tensor(y[p], bank(3 + p)[:, 0:C], b_o, ALU.add).then_inc(s_y, 1)
                dve.wait_ge(s_y, n + 1)
                settle(dve, passed_dve)
                dve.bn_stats(st_a[:, p, :], y[p]).then_inc(s_ya, 1)
                dve.wait_ge(s_ya, 2 * n + 1)
                settle(dve, passed_dve)
                dve.bn_aggr(mv_a[:, p, :], st_a[:, p, :]).then_inc(s_ya, 1)

            def add_y(n, p):
                dve.wait_ge(s_sda, n + 1)
                dve.reciprocal(rd_a[:, p, :], sd_a[:, p, :]).then_inc(s_z, 1)
                dve.wait_ge(s_z, 2 * n + 1)
                dve.tensor_scalar(yn[p], y[p], mv_a[:, p, 0:1], rd_a[:, p, :], ALU.subtract, ALU.mult).then_inc(s_z, 1)
                dve.wait_ge(s_z, 2 * n + 2)
                dve.tensor_tensor(row(x2, n), row(x2, n), yn[p], ALU.add).then_inc(s_x2, 1)
                dve.wait_ge(s_x2, n + 1)
                settle(dve, passed_dve)
                dve.bn_stats(st_b[:, p, :], row(x2, n)).then_inc(s_xs, 1)
                dve.wait_ge(s_xs, 2 * n + 1)
                settle(dve, passed_dve)
                dve.bn_aggr(mv_b[:, p, :], st_b[:, p, :]).then_inc(s_xs, 1)

            def norm_x2(n, p):
                dve.wait_ge(s_sdb, n + 1)
                dve.reciprocal(rd_b[:, p, :], sd_b[:, p, :]).then_inc(s_rdb, 1)
                dve.wait_ge(s_rdb, n + 1)
                after(dve, s_keep[p], 8 * (n - p))
                after(dve, s_sq, n - 1)
                after(dve, s_t3, n - 1)
                dve.tensor_scalar(xn2[p][:, :], row(x2, n), mv_b[:, p, 0:1], rd_b[:, p, :],
                                  ALU.subtract, ALU.mult).then_inc(s_xn2, 1)

            steps(dve, NT, [(6, norm_x2), (5, add_y), (4, bias_y), (1, norm_o)])

            done = [0]

            def step(ins):
                done[0] += 1
                ins.then_inc(s_rt, 1)
                dve.wait_ge(s_rt, done[0])

            def per_tile(v):
                return v.rearrange("p (n a) -> p n a", a=1).to_broadcast([P, NT, E])

            def per_expert(v, n=NT):
                return v.rearrange("p (a e) -> p a e", a=1).to_broadcast([P, n, E])

            dve.wait_ge(s_rc, 9)
            dve.wait_ge(s_dot, NT)
            dve.wait_ge(s_sq, NT)
            dve.tensor_tensor(ge[:, 0:2, :].rearrange("p k e -> p (k e)"), cent_t[:, :], cent_t[:, :], ALU.mult).then_inc(s_csq, 1)
            dve.wait_ge(s_c2, 1)
            step(dve.tensor_copy(c2, bank(7)[:, 0:E]))
            step(dve.tensor_tensor(tmp, per_tile(sq[:, :]), per_expert(c2), ALU.add))
            step(dve.scalar_tensor_tensor(out=dist, in0=bank(6)[:, 0:NT * E].rearrange("p (n e) -> p n e", e=E), scalar=-2.0,
                                          in1=tmp, op0=ALU.mult, op1=ALU.add))
            dve.tensor_scalar(tmp, dist, 1e-12, None, ALU.max).then_inc(s_dd, 1)
            dve.wait_ge(s_ds, 1)
            step(dve.tensor_reduce(v1, dist, AX, ALU.max))
            step(dve.tensor_tensor(tmp, dist, per_tile(v1), ALU.is_equal))
            step(dve.tensor_tensor(tmp, tmp, per_expert(rev), ALU.mult))
            step(dve.tensor_reduce(r_1, tmp, AX, ALU.max))
            step(dve.tensor_tensor(oh1, per_tile(r_1), per_expert(rev), ALU.is_equal))
            step(dve.tensor_scalar(oh2, oh1, -1.0, 1.0, ALU.mult, ALU.add))
            step(dve.tensor_tensor(dist, dist, oh2, ALU.mult))
            step(dve.tensor_reduce(v2, dist, AX, ALU.max))
            dve.tensor_tensor(more, v2, v1, ALU.subtract).then_inc(s_df, 1)
            step(dve.tensor_tensor(tmp, dist, per_tile(v2), ALU.is_equal))
            step(dve.tensor_tensor(tmp, tmp, per_expert(rev), ALU.mult))
            step(dve.tensor_reduce(r_1, tmp, AX, ALU.max))
            step(dve.tensor_tensor(oh2, per_tile(r_1), per_expert(rev), ALU.is_equal))
            dve.tensor_tensor(chosen.rearrange("p (n e) -> p n e", e=E), oh1, oh2, ALU.add).then_inc(s_ch, 1)
            dve.wait_ge(s_ex, 1)
            step(dve.tensor_scalar(v1, ratio, 1.0, None, ALU.add))
            step(dve.reciprocal(w_1[:, :], v1))
            step(dve.tensor_tensor(w_2[:, :], ratio, w_1[:, :], ALU.mult))
            dve.wait_ge(s_pos, 1)
            step(dve.tensor_copy(pos, bank(7)[:, 0:NT * E].rearrange("p (n e) -> p n e", e=E)))
            step(dve.tensor_copy(counts, bank(5)[:, 0:NT * E].rearrange("p (n e) -> p n e", e=E)))
            step(dve.memset(more, 1.0))
            for e in range(E):
                step(dve.tensor_tensor_scan(before[:, :, e], more, counts[:, :, e], 0.0, ALU.mult, ALU.add))
            total = before[:, NT - 1, :]
            step(dve.tensor_tensor(cmp_n, total.rearrange("p (e a) -> p e a", a=1).to_broadcast([P, E, NT]),
                                   iota128.rearrange("p (a n) -> p a n", a=1).to_broadcast([P, E, NT]), ALU.is_gt))
            step(dve.tensor_reduce(n_tiles, cmp_n, AX, ALU.add))
            step(dve.tensor_tensor_scan(first, more[:, 0:E], n_tiles, 0.0, ALU.mult, ALU.add))
            step(dve.tensor_tensor(first, first, n_tiles, ALU.subtract))
            step(dve.tensor_tensor(before, before, counts, ALU.subtract))
            step(dve.tensor_tensor(pos, pos, before, ALU.add))
            step(dve.tensor_scalar(c2, first, float(P), None, ALU.mult))
            step(dve.tensor_tensor(pos, pos, per_expert(c2), ALU.add))
            for n, oh in enumerate((oh1, oh2)):
                step(dve.tensor_tensor(tmp, pos, oh, ALU.mult))
                step(dve.tensor_reduce(v1, tmp, AX, ALU.add))
                last = dve.tensor_copy(slot_i[:, n, :], v1)
                if n == 0:
                    step(last)
            last.then_inc(s_slot, 1)
            step(dve.tensor_tensor(ge, iota_s.rearrange("p (s a) -> p s a", a=1).to_broadcast([P, NS, E]),
                                   per_expert(first, NS), ALU.is_ge))
            step(dve.tensor_reduce(e_of, ge, AX, ALU.add))
            dve.tensor_scalar(tile_e[0:1, :], e_of[0:1, :], -1.0, None, ALU.add).then_inc(s_slot, 1)

            def save_xt2(t):
                dve.wait_ge(s_mt, t + 1)
                after(dve, s_gu, 4 * t)
                dve.tensor_copy(x_t.rearrange("p k t -> p (k t)"), bank(6)[:, 0:C]).then_inc(s_mx, 1)

            def hidden(t):
                after(dve, s_ht, t)
                for c in range(2):
                    dve.wait_ge(s_gu, 4 * t + 2 * c + 2)
                    dve.wait_ge(s_si, 2 * t + c + 1)
                    dve.tensor_tensor(hid[:, CH * c:CH * (c + 1)], bank(2 * c + 1)[:, 0:CH], gates[c], ALU.mult).then_inc(s_hid, 1)

            def save_ht(t):
                dve.wait_ge(s_ht, t + 1)
                after(dve, s_yp, t)
                dve.tensor_copy(h_t.rearrange("p k t -> p (k t)")[0:KP, 4 * P:6 * P], bank(5)[0:KP, 0:2 * P]).then_inc(s_htd, 1)

            dve.wait_ge(s_sc, 16 * 2 * NT)
            save_xt2(0)
            hidden(0)
            save_xt2(1)
            save_ht(0)
            with dve.Fori(1, NS - 1) as t:
                hidden(t)
                save_xt2(t + 1)
                save_ht(t)
            hidden(NS - 1)
            save_ht(NS - 1)

            def mix(n, p):
                dve.wait_ge(s_f1, n + 1)
                dve.scalar_tensor_tensor(out=row(y1_all, n), in0=row(y2_all, n), scalar=w_2[:, bass.ds(n, 1)],
                                         in1=row(y1_all, n), op0=ALU.mult, op1=ALU.add).then_inc(s_fm, 1)
                dve.wait_ge(s_fm, n + 1)
                settle(dve, passed_dve)
                dve.bn_stats(st_a[:, p, :], row(y1_all, n)).then_inc(s_fs, 1)
                dve.wait_ge(s_fs, 2 * n + 1)
                settle(dve, passed_dve)
                dve.bn_aggr(mv_a[:, p, :], st_a[:, p, :]).then_inc(s_fs, 1)

            def finish(n, p):
                dve.wait_ge(s_fd, n + 1)
                dve.reciprocal(rd_a[:, p, :], sd_a[:, p, :]).then_inc(s_fr, 1)
                dve.wait_ge(s_fr, n + 1)
                dve.tensor_scalar(row(y1_all, n), row(y1_all, n), mv_a[:, p, 0:1], rd_a[:, p, :],
                                  ALU.subtract, ALU.mult).then_inc(s_fn, 1)
                dve.wait_ge(s_fn, n + 1)
                dve.tensor_tensor(row(y1_all, n), row(y1_all, n), row(x2, n), ALU.add).then_inc(s_fo, 1)

            steps(dve, NT, [(2, finish), (1, mix)])

        @block.scalar
        def _(act):
            act.wait_ge(s_const, 7)

            def deviation(n, p):
                act.wait_ge(s_stat, 2 * n + 2)
                after(act, s_rstd, n - 1)
                act.activation(std[p], mv[p][:, 1:2], ACT.Sqrt, bias=eps[:, 0:1]).then_inc(s_std, 1)

            def save_xt(n, p):
                act.wait_ge(s_xtp, n + 1)
                after(act, s_qkv, n - 1)
                act.activation(xn_t[p].rearrange("p k t -> p (k t)"), bank(p)[:, 0:C], ACT.Copy).then_inc(s_xt, 1)

            def high(n, p):
                act.wait_ge(s_rr, n + 1)
                after(act, s_pp, n - 1)
                act.activation(parts[p][:, 0, :], rr[p], ACT.Copy).then_inc(s_hi, 1)

            def middle(n, p):
                act.wait_ge(s_r1, n + 1)
                act.activation(parts[p][:, 1, :], r1[p], ACT.Copy).then_inc(s_mid, 1)

            def save_parts(n, p):
                act.wait_ge(s_pp, n + 1)
                src = bank(6).bitcast(BF16).rearrange("p (a t) -> p a t", t=P)
                act.wait_ge(s_pst, 16 * (n // 4 + 1))
                dst = staged[:, bass.ds((n // 4) % 2, 1), 0:8, bass.ds((n % 4) * P, P)].rearrange("p a c t -> p (a c) t")
                act.activation(dst, src, ACT.Copy).then_inc(s_pa, 1)

            steps(act, NT, [(5, save_parts), (4, middle), (3, high), (1, save_xt), (0, deviation)])

            def group(i, c):
                g, first = over(i, c, 1), c == 0
                for k in range(STEPS):
                    st, j = k // HG, k % HG
                    act.wait_ge(s_sp, STEPS * g + k + 1)
                    if j == 0 and not (first and st < 2):
                        act.wait_ge(s_pv, 2 * (ST * g + st - 1))
                    act.activation(pt[st % 2][:, j, :], bank(2 * (k % 2), 2), ACT.Exp, scale=SC).then_inc(s_exp, 1)
                    if k == 5 and not first:
                        save_o(g - 1)

            def save_o(g):
                act.wait_ge(s_pv, 2 * ST * (g + 1))
                after(act, s_ot, 16 * g)
                act.activation(o_stage, bank(6, 2), ACT.Copy).then_inc(s_oe, 1)

            groups(act, group)
            save_o(NG - 1)

            def save_ont(n, p):
                act.wait_ge(s_t2, n + 1)
                after(act, s_op, n - 1)
                act.activation(on_t[p].rearrange("p k t -> p (k t)"), bank(2)[:, 0:C], ACT.Copy).then_inc(s_ont, 1)

            def deviation_y(n, p):
                act.wait_ge(s_ya, 2 * n + 2)
                after(act, s_z, 2 * (n - 1))
                act.activation(sd_a[:, p, :], mv_a[:, p, 1:2], ACT.Sqrt, bias=eps[:, 0:1]).then_inc(s_sda, 1)

            def deviation_x2(n, p):
                act.wait_ge(s_xs, 2 * n + 2)
                after(act, s_rdb, n - 1)
                act.activation(sd_b[:, p, :], mv_b[:, p, 1:2], ACT.Sqrt, bias=eps[:, 0:1]).then_inc(s_sdb, 1)

            def squares(n, p):
                act.wait_ge(s_xn2, n + 1)
                after(act, s_sq, n)
                act.activation(square[:, :], xn2[p][:, :], ACT.Square, accum_out=sq[:, bass.ds(n, 1)]).then_inc(s_sq, 1)

            def save_xn2t(n, p):
                act.wait_ge(s_t3, n + 1)
                after(act, s_dot, n - 1)
                act.activation(xn2_t[p].rearrange("p k t -> p (k t)"), bank(5)[:, 0:C], ACT.Copy).then_inc(s_xn2t, 1)

            steps(act, NT, [(7, save_xn2t), (6, squares), (5, deviation_x2), (4, deviation_y), (2, save_ont)])

            act.wait_ge(s_dd, 1)
            act.activation(dist, tmp, ACT.Sqrt).then_inc(s_ds, 1)
            act.wait_ge(s_df, 1)
            act.activation(ratio, more, ACT.Exp).then_inc(s_ex, 1)

            def gate(t):
                for c in range(2):
                    act.wait_ge(s_gu, 4 * t + 2 * c + 1)
                    after(act, s_hid, 2 * (t - 1) + c + 1)
                    act.activation(gates[c], bank(2 * c)[:, 0:CH], ACT.Silu).then_inc(s_si, 1)

            def save_y(t):
                act.wait_ge(s_yp, t + 1)
                after(act, s_ys, 16 * t)
                act.activation(y_row, bank(7)[:, 0:C], ACT.Copy).then_inc(s_yr, 1)

            def save_ht(t):
                act.wait_ge(s_ht, t + 1)
                after(act, s_yp, t)
                act.activation(h_t.rearrange("p k t -> p (k t)")[0:KP, 0:4 * P], bank(4)[0:KP, :], ACT.Copy).then_inc(s_hta, 1)

            gate(0)
            save_ht(0)
            gate(1)
            save_y(0)
            save_ht(1)
            with act.Fori(2, NS) as t:
                gate(t)
                save_y(t - 1)
                save_ht(t)
            save_y(NS - 1)

            def weigh_first(n, p):
                act.activation(y1_all[:, bass.ds(n, 1), :].rearrange("p a c -> p (a c)"),
                               y1_all[:, bass.ds(n, 1), :].rearrange("p a c -> p (a c)"), ACT.Copy,
                               scale=w_1[:, bass.ds(n, 1)]).then_inc(s_f1, 1)

            def deviation_mix(n, p):
                act.wait_ge(s_fs, 2 * n + 2)
                act.activation(sd_a[:, p, :], mv_a[:, p, 1:2], ACT.Sqrt, bias=eps[:, 0:1]).then_inc(s_fd, 1)

            for m in range(8):
                act.wait_ge(s_gt[m], 16 * 8)
            steps(act, NT, [(2, deviation_mix), (0, weigh_first)])

        @block.tensor
        def _(pe):
            pe.wait_ge(s_const, 7)
            pe.wait_ge(s_cload, 64)

            def turn_x(n, p):
                pe.wait_ge(s_xn, n + 1)
                after(pe, s_xt, n - 1)
                for k in range(KC):
                    last = pe.transpose(bank(p)[:, P * k:P * (k + 1)], xn[p][:, P * k:P * (k + 1)], ident[:, :])
                last.then_inc(s_xtp, 1)

            def project(n, p):
                pe.wait_ge(s_xt, n + 1)
                after(pe, s_qk, n - 1)
                after(pe, s_ra, 2 * (n - 1))
                for k in range(KC):
                    pe.matmul(bank(2 + p), xn_t[p][:, k, :], w_qkv[:, k, 0:2 * C], start=k == 0, stop=k == KC - 1)
                for k in range(KC):
                    last = pe.matmul(bank(4 + p)[:, 0:C], xn_t[p][:, k, :], w_qkv[:, k, 2 * C:3 * C],
                                     start=k == 0, stop=k == KC - 1)
                last.then_inc(s_qkv, 1)

            def turn_parts(n, p):
                pe.wait_ge(s_lo, n + 1)
                after(pe, s_pa, n)
                after(pe, s_pd, n)
                for a in range(12):
                    dst = bank(6, 2).bitcast(BF16)[:, P * a:P * (a + 1)]
                    last = pe.transpose(dst, parts[p].rearrange("p s c -> p (s c)")[:, P * a:P * (a + 1)], ident_bf[:, :])
                last.then_inc(s_pp, 1)

            steps(pe, NT, [(5, turn_parts), (2, project), (1, turn_x)])

            def max_scores(g, t3, k):
                j, t = k // ST, k % ST
                for half in range(2):
                    after(pe, s_max, 2 * (STEPS * g + k - 1) + half + 1)
                    pe.matmul(bank(4 + half), qs[t3][0:QROWS, j, P * t:P * (t + 1)],
                              ks[t3][0:QROWS, j, 512 * half:512 * (half + 1)], start=True, stop=True).then_inc(s_mp, 1)

            def scores(g, t3, k):
                st, j = k // HG, k % HG
                after(pe, s_exp, STEPS * g + k - 1)
                for half in range(2):
                    last = pe.matmul(bank(2 * (k % 2) + half), ks[t3][0:MROWS, j, P * st:P * (st + 1)],
                                     qs[t3][0:MROWS, j, 512 * half:512 * (half + 1)], start=True, stop=True)
                last.then_inc(s_sp, 1)

            def weigh(g, p, st, half):
                if half == 0:
                    pe.wait_ge(s_exp, STEPS * g + HG * (st + 1))
                    if st == 0:
                        pe.wait_ge(s_vg, g + 1)
                        after(pe, s_oe, g)
                for j in range(HG):
                    last = pe.matmul(bank(6 + half)[32 * j:32 * (j + 1), :], vg[p][:, st, j, :],
                                     pt[st % 2][:, j, 512 * half:512 * (half + 1)], start=st == 0, stop=st == ST - 1,
                                     tile_position=(0, 32 * j))
                last.then_inc(s_pv, 1)

            def group(i, c):
                g, p, t3 = over(i, c, 1), c % 2, c % 3
                last = isinstance(g, int) and g == NG - 1
                for k in range(STEPS):
                    st = k // HG
                    if st == 0:
                        pe.wait_ge(s_ml[k % HG], 16 * (g + 1))
                    scores(g, t3, k)
                    if not last:
                        if k == 0:
                            pe.wait_ge(s_stack[(c + 1) % 3], STACK_DMAS * (over(i, c + 1, 3) + 1))
                        max_scores(g + 1, (c + 1) % 3, k)
                    if k % HG >= 2:
                        if st > 0:
                            weigh(g, p, st - 1, k % HG - 2)
                        elif c > 0:
                            weigh(g - 1, 1 - p, ST - 1, k % HG - 2)

            pe.wait_ge(s_ones, 5)
            pe.wait_ge(s_pd, NT)
            pe.wait_ge(s_stack[0], STACK_DMAS)
            for k in range(STEPS):
                max_scores(0, 0, k)
            groups(pe, group)
            for half in range(2):
                weigh(NG - 1, 1, ST - 1, half)

            pe.wait_ge(s_wo, 48)
            pe.wait_ge(s_oe, NG)
            pe.wait_ge(s_exp, STEPS * NG)
            pe.wait_ge(s_max, 2 * STEPS * NG)

            def turn_ot(n, p):
                pe.wait_ge(s_otl[p], 8 * (n + (2 - p)))
                after(pe, s_on, n - 1)
                for k in range(HG):
                    last = pe.transpose(bank(p)[:, P * k:P * (k + 1)], ot[p][:, k, :], ident[:, :])
                last.then_inc(s_t1, 1)

            def turn_on(n, p):
                pe.wait_ge(s_on, n + 1)
                after(pe, s_ont, n)
                for k in range(KC):
                    last = pe.transpose(bank(2)[:, P * k:P * (k + 1)], on[p][:, P * k:P * (k + 1)], ident[:, :])
                last.then_inc(s_t2, 1)

            def project_o(n, p):
                pe.wait_ge(s_ont, n + 1)
                after(pe, s_y, n - 1)
                for k in range(KC):
                    last = pe.matmul(bank(3 + p)[:, 0:C], on_t[p][:, k, :], w_o[:, k, :], start=k == 0, stop=k == KC - 1)
                last.then_inc(s_op, 1)

            def turn_xn2(n, p):
                pe.wait_ge(s_xn2, n + 1)
                after(pe, s_xn2t, n)
                for k in range(KC):
                    last = pe.transpose(bank(5)[:, P * k:P * (k + 1)], xn2[p][:, P * k:P * (k + 1)], ident[:, :])
                last.then_inc(s_t3, 1)

            def dots(n, p):
                pe.wait_ge(s_xn2t, n + 1)
                for k in range(KC):
                    last = pe.matmul(bank(6)[:, bass.ds(n * E, E)], xn2_t[p][:, k, :], cent_t[:, E * k:E * (k + 1)],
                                     start=k == 0, stop=k == KC - 1)
                last.then_inc(s_dot, 1)

            steps(pe, NT, [(8, dots), (7, turn_xn2), (3, project_o), (2, turn_on), (0, turn_ot)])

            pe.wait_ge(s_csq, 1)
            for k in range(KC):
                last = pe.matmul(bank(7)[:, 0:E], ones_f[:, :], ge[:, k, :], start=k == 0, stop=k == KC - 1)
            last.then_inc(s_c2, 1)
            pe.wait_ge(s_ch, 1)
            pe.matmul(bank(7)[:, 0:NT * E], upper, chosen, start=True, stop=True)
            pe.matmul(bank(5)[:, 0:NT * E], ones_bf, chosen, start=True, stop=True).then_inc(s_pos, 1)

            def turn_rows(t):
                pe.wait_ge(s_xr, 16 * (t + 1))
                after(pe, s_mx, t)
                for k in range(KC):
                    last = pe.transpose(bank(6)[:, P * k:P * (k + 1)], x_row[:, P * k:P * (k + 1)], ident[:, :])
                last.then_inc(s_mt, 1)

            def expert(t):
                return pe.value_load(tile_e[0:1, bass.ds(t, 1)], min_val=0, max_val=E - 1)

            def gate_up(t, e):
                pe.wait_ge(s_mx, t + 1)
                for c in range(4):
                    col = (c % 2) * HID + (c // 2) * CH
                    if c % 2 == 0:
                        after(pe, s_si, 2 * (t - 1) + c // 2 + 1)
                    else:
                        after(pe, s_hid, 2 * (t - 1) + c // 2 + 1)
                    dst = bank(c)[:, 0:CH]
                    pe.matmul(dst, ones3[:, :], b1_sb[0:3, bass.ds(e, 1), col:col + CH].rearrange("p a n -> p (a n)"),
                              start=True, stop=False)
                    for k in range(KC):
                        last = pe.matmul(dst, x_t[:, k, :],
                                         w1_sb[:, bass.ds(e, 1), k, col:col + CH].rearrange("p a n -> p (a n)"),
                                         start=False, stop=k == KC - 1)
                    last.then_inc(s_gu, 1)

            def turn_hidden(t):
                pe.wait_ge(s_hid, 2 * t + 2)
                after(pe, s_hta, t)
                after(pe, s_htd, t)
                for k in range(KH):
                    last = pe.transpose(bank(4, 2)[0:KP, P * k:P * (k + 1)], hid[:, KP * k:KP * (k + 1)], ident[:, :])
                last.then_inc(s_ht, 1)

            def down(t, e):
                pe.wait_ge(s_hta, t + 1)
                pe.wait_ge(s_htd, t + 1)
                after(pe, s_yr, t)
                pe.matmul(bank(7)[:, 0:C], ones3[:, :], b2_sb[0:3, bass.ds(e, 1), :].rearrange("p a n -> p (a n)"),
                          start=True, stop=False)
                for k in range(KH):
                    last = pe.matmul(bank(7)[:, 0:C], h_t[0:KP, k, :],
                                     w2_sb[:, bass.ds(e, 1), k, :].rearrange("p a n -> p (a n)"),
                                     start=False, stop=k == KH - 1)
                last.then_inc(s_yp, 1)

            pe.wait_ge(s_slot, 2)
            pe.wait_ge(s_w, 16 * 2 * E)
            pe.wait_ge(s_brow, 32)
            turn_rows(0)
            gate_up(0, expert(0))
            turn_rows(1)
            turn_hidden(0)
            gate_up(1, expert(1))
            turn_rows(2)
            down(0, expert(0))
            turn_hidden(1)
            with pe.Fori(2, NS - 1) as t:
                gate_up(t, expert(t))
                turn_rows(t + 1)
                down(t - 1, expert(t - 1))
                turn_hidden(t)
            gate_up(NS - 1, expert(NS - 1))
            down(NS - 2, expert(NS - 2))
            turn_hidden(NS - 1)
            down(NS - 1, expert(NS - 1))


def layout(inputs):
    g = {k.replace("L0_", ""): np.asarray(v) for k, v in inputs.items()}
    half = np.arange(HALF, dtype=np.float32)
    theta = np.power(np.float32(10000.0), -half / np.float32(HALF)).astype(np.float32)
    freqs = np.arange(T, dtype=np.float32)[:, None] * theta[None, :]
    cos, sin = np.cos(freqs).astype(np.float32), np.sin(freqs).astype(np.float32)
    rope = np.stack([np.concatenate([cos, cos], 1), np.concatenate([-sin, sin], 1)])
    return {
        "x": g["attn_x"].reshape(NTOK, C),
        "wqkv": np.concatenate([g["attn_Wq"].T, g["attn_Wk"].T, g["attn_Wv"].T], axis=1),
        "bqkv": np.concatenate([g["attn_bq"], g["attn_bk"], g["attn_bv"]]),
        "wo": g["attn_Wo"].T,
        "bo": g["attn_bo"],
        "rope": rope,
        "cent": g["ffn_centroid"].T,
        "w1": np.concatenate([g["ffn_Wg"], g["ffn_W1"]], axis=2),
        "b1": np.concatenate([g["ffn_bg"], g["ffn_b1"]], axis=1),
        "w2": g["ffn_W2"],
        "b2": g["ffn_b2"],
    }


def kernel(**inputs):
    import concourse.bacc as bacc
    from concourse.bass_utils import run_bass_kernel_spmd

    nc = bacc.Bacc("TRN2", target_bir_lowering=False, num_devices=1,
                   dynamic_dma_scratch_size=8192)
    arrays, args = {}, []
    for name, a in layout(inputs).items():
        a = np.ascontiguousarray(a)
        arrays[f"in_{name}"] = a
        args.append(nc.dram_tensor(f"in_{name}", a.shape, mybir.dt.from_np(a.dtype), kind="ExternalInput").ap())
    args.append(nc.dram_tensor("out_x", (NTOK, C), F32, kind="ExternalOutput").ap())
    build(nc, *args)
    r = run_bass_kernel_spmd(nc, [arrays], core_ids=[0])
    return np.asarray(r.results[0]["out_x"]).reshape(B, T, C)
```

```python
from contextlib import ExitStack

import numpy as np

import concourse.bass as bass
from concourse import mybir

F32 = mybir.dt.float32
BF16 = mybir.dt.bfloat16
I32 = mybir.dt.int32
ALU = mybir.AluOpType
ACT = mybir.ActivationFunctionType
AX = mybir.AxisListType.X

P = 128
B, T, C = 4, 1024, 256
H, D = 16, 16
HALF = D // 2
E, HID = 8, 684
NTOK = B * T
NT = NTOK // P
TPB = T // P
KC = C // P
HG = 4
NG = B * H // HG
QROWS = 6 * D
MROWS = QROWS + 3
ST = T // P
STACK_DMAS = 12 * 16
STEPS = ST * HG
UNITS = STEPS // 2
LEAD = 6
SC = D ** -0.5
CH = HID // 2
KH, KP = 6, HID // 6
NS = 2 * NTOK // P + E - 1
EPS = 1e-5

Q_PART = [0, 0, 1, 1, 0, 2]
K_PART = [0, 1, 0, 1, 2, 0]


def steps(eng, count, stages, head=2):
    lag = max(l for l, _ in stages)
    lo = (lag + head + 1) // 2 * 2
    hi = count - count % 2

    def one(s):
        for l, f in stages:
            if 0 <= s - l < count:
                f(s - l, (s - l) % 2)

    for s in range(lo):
        one(s)
    with eng.Fori(0, (hi - lo) // 2) as i:
        for q in range(2):
            for l, f in stages:
                f(2 * i + (lo + q - l), (lo + q - l) % 2)
    for s in range(hi, count + lag):
        one(s)


def after(eng, sem, value):
    if not isinstance(value, int) or value > 0:
        eng.wait_ge(sem, value)


def over(i, c, m):
    return (6 // m) * i + c // m


def groups(eng, body):
    body(0, 0)
    body(0, 1)
    with eng.Fori(0, (NG - 4) // 6) as i:
        for c in range(2, 8):
            body(i, c)
    for c in range(2, 4):
        body((NG - 4) // 6, c)


def settle(eng, passed):
    eng.sem_inc(passed)


class Carve:

    def __init__(self, region):
        self.region, self.at = region, 0

    def take(self, shape, dt=F32):
        n = int(np.prod(shape)) * (2 if dt == BF16 else 4) // 4
        v = self.region[:, self.at:self.at + n]
        self.at += n
        assert self.at <= self.region.shape[1], (self.at, self.region.shape)
        if dt != F32:
            v = v.bitcast(dt)
        names = "abcde"[:len(shape)]
        if len(shape) > 1:
            v = v.rearrange("p (" + " ".join(names) + ") -> p " + " ".join(names),
                            **{c: s for c, s in zip(names, shape)})
        return v


def build(nc, x, wqkv, bqkv, wo, bo, rope, cent, w1, b1, w2, b2, out):
    ctx = ExitStack()
    with ctx:
        def sb(name, shape, dt=F32):
            return ctx.enter_context(nc.sbuf_tensor(name, shape, dt))

        def sem(name):
            return ctx.enter_context(nc.semaphore(name))

        weights = sb("weights", [P, E * KC * 2 * HID + E * KH * C])
        stacks = sb("stacks", [P, 8192])
        probs = sb("probs", [P, 8192])
        values = sb("values", [P, 2048])
        ident = sb("ident", [P, P])
        ident_bf = sb("ident_bf", [P, P], BF16)
        eps = sb("eps", [P, 1])
        ones_f = sb("ones_f", [P, P])
        psum = ctx.enter_context(nc.psum_tensor("psum", [P, 8 * 512], F32))

        def bank(k, n=1):
            return psum[:, 512 * k:512 * (k + n)]

        ot_scr = nc.dram_tensor("ot_scr", (NG, P, T), F32, kind="Internal").ap()

        qk_scr = nc.dram_tensor("qk_scr", (3, 2, 2, P, NTOK), BF16, kind="Internal").ap()
        m_scr = nc.dram_tensor("m_scr", (HG, P, 32), BF16, kind="Internal").ap()
        v_scr = nc.dram_tensor("v_scr", (B, HG, P, ST, HG * D), F32, kind="Internal").ap()

        c = Carve(weights)
        x_all = c.take([NT, C])
        v_all = c.take([NT, C])
        staged = c.take([2, 12, 4 * P], BF16)
        q_first, k_first = c.take([HG, T], BF16), c.take([HG, T], BF16)
        c = Carve(weights)
        c.at = (E - 3) * KC * 2 * HID
        o_stage = c.take([T])
        v_stage = [c.take([ST, HG * D]) for _ in range(2)]
        assert c.at <= E * KC * 2 * HID
        c = Carve(stacks)
        w_qkv = c.take([KC, 3 * C])
        b_qkv = c.take([3 * C])
        cos_t, sin_t = c.take([TPB, D]), c.take([TPB, D])
        xn = [c.take([C]) for _ in range(2)]
        xn_t = [c.take([KC, P]) for _ in range(2)]
        stat = [c.take([6]) for _ in range(2)]
        mv = [c.take([2]) for _ in range(2)]
        std = [c.take([1]) for _ in range(2)]
        rstd = [c.take([1]) for _ in range(2)]
        c = Carve(probs)
        qk = [c.take([2 * C]) for _ in range(2)]
        ra = [c.take([2 * C]) for _ in range(2)]
        rb = [c.take([2 * C]) for _ in range(2)]
        rr = [c.take([2 * C]) for _ in range(2)]
        r1 = [c.take([2 * C]) for _ in range(2)]
        parts = [c.take([3, 2 * C], BF16) for _ in range(2)]
        c = Carve(stacks)
        qs = [q_first] + [c.take([HG, T], BF16) for _ in range(2)]
        ks = [k_first] + [c.take([HG, T], BF16) for _ in range(2)]
        c = Carve(probs)
        pt = [c.take([HG, T // 2]) for _ in range(4)]
        c = Carve(values)
        vg = [c.take([ST, HG, 32]) for _ in range(2)]
        mx = sb("mx", [P, 2, HG, ST])
        nm = sb("nm", [P, ST])
        nr = sb("nr", [P, ST])
        nl = sb("nl", [P, ST])
        m3 = sb("m3", [P, 32], BF16)
        m3_t = sb("m3_t", [P, 32], BF16)

        w1_size = E * KC * 2 * HID
        w1_sb = weights[:, 0:w1_size].rearrange("p (e k n) -> p e k n", e=E, k=KC)
        w2_sb = weights[0:KP, w1_size:w1_size + E * KH * C].rearrange("p (e k n) -> p e k n", e=E, k=KH)
        x2 = stacks[:, :].rearrange("p (n c) -> p n c", c=C)
        c = Carve(values)
        ot = [c.take([HG, P]) for _ in range(2)]
        on = [c.take([C]) for _ in range(2)]
        on_t = [c.take([KC, P]) for _ in range(2)]
        c = Carve(weights)
        c.at = (E - 1) * KC * 2 * HID
        w_o, b_o = c.take([KC, C]), c.take([C])[0:1, :]
        yn = [c.take([C]) for _ in range(2)]
        xn2_t = [c.take([KC, P]) for _ in range(2)]
        assert c.at <= w1_size
        xn2 = [sb(f"xn2_{i}", [P, C]) for i in range(2)]
        o_sum = sb("o_sum", [P, 2, H])
        small = sb("small", [P, 2, 21])
        st_a, st_b = small[:, :, 0:6], small[:, :, 6:12]
        mv_a, mv_b = small[:, :, 12:14], small[:, :, 14:16]
        sd_a, sd_b = small[:, :, 16:17], small[:, :, 17:18]
        rd_a, rd_b = small[:, :, 18:19], small[:, :, 19:20]
        off = small[:, :, 20:21]
        cent_t = sb("cent_t", [P, KC * E])
        w_1 = sb("w_1", [P, NT])
        w_2 = sb("w_2", [P, NT])
        token_of = sb("token_of", [P, NS])
        place_of = sb("place_of", [P, NS])
        at_x = sb("at_x", [P, 1], I32)
        at_y = sb("at_y", [P, 1], I32)
        sq = sb("sq", [P, NT])
        tile_e = sb("tile_e", [1, NS], I32)
        c = Carve(values)
        pos = c.take([NT, E])
        before = c.take([NT, E])
        dist = c.take([NT, E])
        oh1 = c.take([NT, E])
        oh2 = c.take([NT, E])
        tmp = c.take([NT, E])
        counts = c.take([NT, E])
        more = c.take([NT])
        c = Carve(weights)
        c.at = (E - 1) * KC * 2 * HID
        chosen = c.take([NT * E], BF16)
        upper = c.take([P], BF16)
        ones_bf = c.take([P], BF16)
        rev = c.take([E])
        iota128 = c.take([NT])
        iota_s = c.take([NS])
        iota_i = c.take([P]).bitcast(I32)
        iota_row = c.take([P])
        name = c.take([2 * NT])
        nobody = c.take([1])
        high = c.take([2, NT])
        low = c.take([2, NT])
        ge = c.take([NS, E])
        in_tile = ge.rearrange("p s e -> p (s e)").rearrange("p (b n s) -> p b n s", b=2, n=4)
        cmp_n = c.take([E, NT])
        c2 = c.take([E])
        v1 = c.take([NT])
        v2 = c.take([NT])
        ratio = c.take([NT])
        r_1 = c.take([NT])
        e_of = c.take([NS])
        n_tiles = c.take([E])
        first = c.take([E])
        assert c.at <= w1_size
        c = Carve(probs)
        b1_sb = c.take([E, 2 * HID], BF16)
        b2_sb = c.take([E, C], BF16)
        in_row = probs[:, c.at:c.at + 8 * P].rearrange("p (b n s) -> p b n s", b=2, n=4)
        h_t = c.take([KH, P])
        y_row = c.take([C])
        c = Carve(values)
        x_row, x_t = c.take([C]), c.take([KC, P])
        hid = c.take([HID])
        gates = [c.take([CH]) for _ in range(2)]
        b_f = sb("b_f", [P, 114 + 16])
        b_r = sb("b_r", [P, 114 + 16])
        b_p = [sb(f"b_p{i}", [P, 114 + 16], BF16) for i in range(3)]
        ones3 = sb("ones3", [3, P], BF16)
        square = sb("square", [P, C])
        c = Carve(weights)
        y1_all, y2_all = c.take([NT, C]), c.take([NT, C])
        b_scr = nc.dram_tensor("b_scr", (3, E * (2 * HID + C)), BF16, kind="Internal").ap()
        xn2_d = nc.dram_tensor("xn2_d", (NTOK, C), F32, kind="Internal").ap()
        y_d = nc.dram_tensor("y_d", (2 * NTOK + P, C), F32, kind="Internal").ap()

        s_zero = sem("zeros_made")
        s_bl = sem("biases_loaded")
        s_bs = sem("bias_split_step")
        s_bst = sem("bias_parts_stored")
        s_brow = sem("bias_rows_loaded")
        s_w = sem("first_weights_loaded")
        s_w2 = sem("second_weights_loaded")
        s_x2l = sem("x_loaded_again")
        s_wo = sem("wo_loaded")
        s_otl = [sem(f"ot_loaded{i}") for i in range(2)]
        s_t1 = sem("ot_transposed")
        s_rs = sem("sums_inverted")
        s_on = sem("o_normed")
        s_t2 = sem("on_transposed")
        s_ont = sem("on_t_ready")
        s_op = sem("o_projected")
        s_ya = sem("y_stats_step")
        s_sda = sem("y_deviation")
        s_z = sem("y_norm_step")
        s_x2 = sem("x2_ready")
        s_xs = sem("x2_stats_step")
        s_sdb = sem("x2_deviation")
        s_rdb = sem("x2_inverse")
        s_ob = sem("x2_offset")
        s_xn2 = sem("xn2_ready")
        s_keep = [sem(f"xn2_kept{i}") for i in range(2)]
        s_sq = sem("squares_done")
        s_t3 = sem("xn2_transposed")
        s_xn2t = sem("xn2_t_ready")
        s_dot = sem("dots_done")
        s_csq = sem("cent_squared")
        s_c2 = sem("cent_norms")
        s_rt = sem("route_step")
        s_dd = sem("squared_distances")
        s_ds = sem("distances")
        s_df = sem("difference")
        s_ex = sem("difference_exp")
        s_ch = sem("choices_made")
        s_pos = sem("positions_counted")
        s_slot = sem("slots_ready")
        s_rc = sem("route_consts")
        s_yc = sem("spare_rows_cleared")
        s_bh = sem("slot_tiles_compared")
        s_oh = sem("one_hots_ready")
        s_tb = sem("one_hots_used")
        s_ig = sem("gather_aimed")
        s_is = sem("scatter_aimed")
        s_xr = sem("x_rows_loaded")
        s_mt = sem("x_rows_transposed")
        s_mx = sem("x_t_ready")
        s_gu = sem("gate_up_ready")
        s_si = sem("gate_done")
        s_hid = sem("hidden_ready")
        s_ht = sem("hidden_transposed")
        s_hta = sem("hidden_t_act")
        s_htd = sem("hidden_t_dve")
        s_yp = sem("expert_out_ready")
        s_yr = sem("expert_out_saved")
        s_ys = sem("expert_out_stored")
        s_gt = [sem(f"rows_gathered{i}") for i in range(8)]
        s_back = sem("rows_back")
        s_fb = sem("mix_offset")
        s_f1 = sem("first_weighed")
        s_fm = sem("mixed")
        s_fs = sem("mix_stats_step")
        s_fd = sem("mix_deviation")
        s_fr = sem("mix_inverse")
        s_fn = sem("mix_normed")
        s_fo = sem("outputs_ready")
        s_out = sem("outputs_stored")
        passed_dve = sem("passed_dve")
        passed_pool = sem("passed_pool")
        s_const = sem("consts_made")
        s_cload = sem("consts_loaded")
        s_x = [sem("first_x_loaded"), sem("other_x_loaded")]
        s_stat = sem("stats_step")
        s_std = sem("std_ready")
        s_rstd = sem("rstd_ready")
        s_xn = sem("xn_ready")
        s_xtp = sem("xn_transposed")
        s_xt = sem("xn_t_ready")
        s_qkv = sem("qkv_ready")
        s_qk = sem("qk_biased")
        s_ra = sem("cos_done")
        s_rb = sem("sin_done")
        s_rr = sem("rope_done")
        s_hi = sem("hi_ready")
        s_r1 = sem("rest_ready")
        s_mid = sem("mid_ready")
        s_lo = sem("lo_ready")
        s_pp = sem("parts_transposed")
        s_pa = sem("parts_saved_act")
        s_pd = sem("parts_saved_dve")
        s_pst = sem("parts_stored")
        s_vst = sem("v_stored")
        s_vl = [sem(f"values_loaded{i}") for i in range(2)]
        s_stack = [sem(f"stack_loaded{i}") for i in range(3)]
        s_ones = sem("ones_made")
        s_vg = sem("values_copied")
        s_mp = sem("max_scores_ready")
        s_max = sem("max_done")
        s_comb = sem("max_combined")
        s_nm = sem("max_split_step")
        s_m3 = sem("max_parts_ready")
        s_m3t = sem("max_parts_turned")
        s_mst = sem("max_parts_stored")
        s_ml = [sem(f"max_rows_loaded{j}") for j in range(HG)]
        s_sp = sem("scores_ready")
        s_exp = sem("exp_done")
        s_pv = sem("pv_done")
        s_oe = sem("o_saved")
        s_ot = sem("o_stored")

        def row(t, n):
            return t[:, bass.ds(n, 1), :].rearrange("p a c -> p (a c)")

        block = ctx.enter_context(nc.Block())
        x_v = x.rearrange("(n p) d -> p n d", p=P)

        def store_parts(sp, m):
            sp.wait_ge(s_pa, 4 * m + 4)
            sp.wait_ge(s_pd, 4 * m + 4)
            sp.dma_start(qk_scr[:, :, :, :, bass.ds(4 * P * m, 4 * P)].rearrange("s q h p t -> p (s q h) t"),
                         staged[:, bass.ds(m % 2, 1), :, :].rearrange("p a c t -> p (a c) t")).then_inc(s_pst, 16)
            sp.wait_ge(s_ra, 2 * (4 * m + 4))
            for h in range(HG):
                sp.dma_start(v_scr[bass.ds(m // 2, 1), h, :, bass.ds(4 * (m % 2), 4), :].rearrange("a p s c -> (a p) s c"),
                             v_all[:, bass.ds(4 * m, 4), HG * D * h:HG * D * (h + 1)]).then_inc(s_vst, 16)

        def load_stacks(sp, i, c):
            g, p, t = over(i, c, 1), c % 2, c % 3
            after(sp, s_sp, STEPS * (g - 2))
            for s, part_of, q in ((qs[t], Q_PART, 0), (ks[t], K_PART, 1)):
                for r in range(6):
                    src = qk_scr[part_of[r], q, bass.ds((g // 2) % 2, 1), 64 * p:64 * (p + 1), bass.ds((g // 4) * T, T)]
                    sp.dma_start(s[D * r:D * (r + 1), :, :],
                                 src.rearrange("a (j d) t -> d (a j) t", d=D)).then_inc(s_stack[t], 16)

        def load_values(sp, i, c):
            g, p = over(i, c, 1), c % 2
            after(sp, s_vg, g - 1)
            src = v_scr[bass.ds(g // 4, 1), bass.ds(g % 4, 1), :, :, :]
            sp.dma_start(v_stage[p], src.rearrange("a b p s c -> (a b p) s c")).then_inc(s_vl[p], 16)

        def load_max_rows(sp, i, c):
            g, t = over(i, c, 1), c % 3
            for j in range(HG):
                sp.wait_ge(s_m3t, HG * g + j + 1)
                sp.dma_start(m_scr[j, :, :], m3_t[:, :]).then_inc(s_mst, 16)
                sp.wait_ge(s_mst, 16 * (HG * g + j + 1))
                src = m_scr[j, :, :].rearrange("(q r) c -> r q c", q=4)[0:3 * ST]
                sp.dma_start(qs[t][QROWS:MROWS, j, :].rearrange("a (t q c) -> a t q c", q=4, c=32),
                             src.rearrange("(a t) q c -> a t q c", t=ST)).then_inc(s_ml[j], 16)

        def store_o(sp, g):
            sp.wait_ge(s_oe, 2 * g + 2)
            sp.dma_start(ot_scr[bass.ds(g, 1), :, :].rearrange("a p t -> (a p) t"), o_stage).then_inc(s_ot, 16)

        def load_w1(sp, e):
            sp.dma_start(w1_sb[:, e, :, :], w1[e].rearrange("(k p) n -> p k n", p=P)).then_inc(s_w, 16)

        @block.sync
        def _(sp):
            sp.dma_start(x_all[:, 0:8, :], x_v[:, 0:8, :]).then_inc(s_x[0], 16)
            sp.dma_start(w_qkv, wqkv.rearrange("(k p) n -> p k n", p=P)).then_inc(s_cload, 16)
            sp.dma_start(b_qkv, bqkv.partition_broadcast(P)).then_inc(s_cload, 16)
            sp.dma_start(cos_t, rope[0].rearrange("(n p) d -> p n d", p=P)).then_inc(s_cload, 16)
            sp.dma_start(sin_t, rope[1].rearrange("(n p) d -> p n d", p=P)).then_inc(s_cload, 16)
            for m in range(1, 4):
                sp.dma_start(x_all[:, 8 * m:8 * m + 8, :], x_v[:, 8 * m:8 * m + 8, :]).then_inc(s_x[1], 16)
            sp.wait_ge(s_zero, 3)
            sp.dma_start(y_d[2 * NTOK:, :], xn2[0][:, :]).then_inc(s_yc, 16)
            sp.dma_start(b_f[0:96, 0:114], b1.rearrange("e n -> (e n)").rearrange("(p c) -> p c", c=114)).then_inc(s_bl, 16)
            sp.dma_start(b_f[:, 114:130], b2.rearrange("e n -> (e n)").rearrange("(p c) -> p c", c=16)).then_inc(s_bl, 16)
            sp.sem_inc(s_pst, 32)
            store_parts(sp, 0)
            for m in range(1, 3):
                sp.wait_ge(s_pst, 32 + 16 * m)
                store_parts(sp, m)
            load_stacks(sp, 0, 0)
            with sp.Fori(3, NT // 4) as m:
                sp.wait_ge(s_pst, 32 + 16 * m)
                store_parts(sp, m)
            sp.wait_ge(s_pst, 32 + 16 * (NT // 4))
            sp.wait_ge(s_vst, 16 * NT)
            load_values(sp, 0, 0)
            load_values(sp, 0, 1)
            load_stacks(sp, 0, 1)
            load_stacks(sp, 0, 2)
            load_max_rows(sp, 0, 0)

            def during(i, c):
                g = over(i, c, 1)
                if not (isinstance(g, int) and g + 2 >= NG):
                    if c > 0:
                        load_stacks(sp, i, c + 2)
                    load_values(sp, i, c + 2)
                if c > 0:
                    store_o(sp, g - 1)
                if isinstance(g, int) and g == NG - 2:
                    for e in range(E - 3):
                        load_w1(sp, e)
                if not (isinstance(g, int) and g + 1 >= NG):
                    load_max_rows(sp, i, c + 1)

                if c == 0:
                    sp.wait_ge(s_bs, 6)
                    for r in range(3):
                        sp.dma_start(b_scr[r, 0:E * 2 * HID].rearrange("(p c) -> p c", c=114),
                                     b_p[r][0:96, 0:114]).then_inc(s_bst, 16)
                        sp.dma_start(b_scr[r, E * 2 * HID:].rearrange("(p c) -> p c", c=16),
                                     b_p[r][:, 114:130]).then_inc(s_bst, 16)

            groups(sp, during)
            sp.wait_ge(s_sp, STEPS * (NG - 1))
            for m in range(4):
                sp.dma_start(x2[:, 8 * m:8 * m + 8, :], x_v[:, 8 * m:8 * m + 8, :]).then_inc(s_x2l, 16)
            store_o(sp, NG - 1)
            sp.wait_ge(s_bst, 16 * 6)
            sp.wait_ge(s_ot, 16 * NG)
            sp.dma_start(w_o, wo.rearrange("(k p) n -> p k n", p=P)).then_inc(s_wo, 16)
            sp.dma_start(b_o, bo.rearrange("(a n) -> a n", a=1)).then_inc(s_wo, 16)
            sp.dma_start(cent_t[:, :].rearrange("p (k e) -> p k e", k=KC),
                         cent.rearrange("(k p) e -> p k e", p=P)).then_inc(s_wo, 16)

            sp.dma_start(b1_sb[0:3, :, :], b_scr[:, 0:E * 2 * HID].rearrange("r (e n) -> r e n", e=E)).then_inc(s_brow, 16)
            sp.dma_start(b2_sb[0:3, :, :], b_scr[:, E * 2 * HID:].rearrange("r (e n) -> r e n", e=E)).then_inc(s_brow, 16)

            def load_ot(n, p):
                after(sp, s_t1, n - 1)
                src = ot_scr[bass.ds((n // TPB) * HG, HG), :, bass.ds((n % TPB) * P, P)]
                sp.dma_start(ot[p], src.rearrange("g p t -> p g t")).then_inc(s_otl[p], 16)

            def keep(n, p):
                sp.wait_ge(s_xn2, n + 1)
                sp.dma_start(xn2_d[bass.ds(n * P, P), :], xn2[p][:, :]).then_inc(s_keep[p], 16)

            steps(sp, NT, [(7, keep), (0, load_ot)])
            load_w1(sp, E - 3)
            load_w1(sp, E - 2)
            sp.wait_ge(s_slot, 1)
            load_w1(sp, E - 1)

            sp.wait_ge(s_ys, 16 * NS)
            for m in range(NT // 4):
                for c, rows in enumerate((y1_all, y2_all)):
                    sp.dma_start(rows[:, 4 * m:4 * m + 4, :],
                                 y_d[NTOK * c:NTOK * (c + 1), :].rearrange("(n p) d -> p n d", p=P)[:, 4 * m:4 * m + 4, :]
                                 ).then_inc(s_gt[m], 16)
            for m in range(NT // 4 + 2):
                if m < NT // 4:
                    sp.wait_ge(s_gt[m], 32)
                    sp.sem_inc(s_back, 4)
                if m < 2:
                    continue
                m -= 2
                sp.wait_ge(s_fo, 4 * m + 4)
                sp.dma_start(out.rearrange("(n p) d -> p n d", p=P)[:, 4 * m:4 * m + 4, :],
                             y1_all[:, 4 * m:4 * m + 4, :]).then_inc(s_out, 16)
            sp.wait_ge(s_out, 16 * (NT // 4))

        @block.gpsimd
        def _(pool):
            pool.memset(xn2[0][:, :], 0.0).then_inc(s_zero, 1)
            pool.memset(ones3[:, :], 1.0).then_inc(s_zero, 1)
            pool.wait_ge(s_zero, 2)
            pool.memset(b_f[:, :], 0.0).then_inc(s_zero, 1)
            pool.wait_ge(s_zero, 3)
            pool.memset(ident[:, :], 0.0).then_inc(s_const, 1)
            pool.memset(ident_bf[:, :], 0.0).then_inc(s_const, 1)
            pool.memset(eps[:, :], EPS).then_inc(s_const, 1)
            pool.memset(ones_f[:, :], 1.0).then_inc(s_const, 1)
            pool.wait_ge(s_const, 4)
            for m in (ident, ident_bf):
                pool.affine_select(out=m[:, :], in_=m[:, :], compare_op=ALU.not_equal, fill=1.0, base=0,
                                   pattern=[[-1, P]], channel_multiplier=1).then_inc(s_const, 1)
            pool.memset(m3[:, :], 0.0).then_inc(s_const, 1)

            def sines(n, p):
                if isinstance(n, int) and n == 0:
                    pool.wait_ge(s_cload, 64)
                pool.wait_ge(s_qk, n + 1)
                after(pool, s_rr, n - 1)
                src = qk[p].rearrange("p (h s d) -> p h s d", s=2, d=HALF)
                dst = rb[p].rearrange("p (h s d) -> p h s d", s=2, d=HALF)
                for s in range(2):
                    tab = sin_t[:, bass.ds(n % TPB, 1), HALF * s:HALF * (s + 1)].to_broadcast([P, 2 * H, HALF])
                    pool.tensor_tensor(dst[:, :, s, :], src[:, :, 1 - s, :], tab, ALU.mult).then_inc(s_rb, 1)

            def low(n, p):
                pool.wait_ge(s_mid, n + 1)
                pool.wait_ge(s_r1, n + 1)
                after(pool, s_pp, n - 1)
                pool.tensor_tensor(parts[p][:, 2, :], r1[p], parts[p][:, 1, :], ALU.subtract).then_inc(s_lo, 1)

            steps(pool, NT, [(7, low), (5, sines)])
            pool.wait_ge(s_pa, NT)
            pool.wait_ge(s_pd, NT)
            pool.wait_ge(s_pst, 32 + 16 * (NT // 4))
            pool.wait_ge(s_vst, 16 * NT)
            for n, ones in enumerate([k[QROWS:QROWS + 32, :, :] for k in ks] + [v[:, :, :, D:32] for v in vg]):
                pool.memset(ones, 1.0).then_inc(s_ones, 1)
                pool.wait_ge(s_ones, n + 1)

            def copy_values(i, c):
                p = c % 2
                pool.wait_ge(s_vl[p], 16 * (over(i, c, 2) + 1))
                after(pool, s_pv, 2 * ST * (over(i, c, 1) - 1))
                settle(pool, passed_pool)
                pool.tensor_copy(vg[p][:, :, :, 0:D],
                                 v_stage[p].rearrange("p s (j d) -> p s j d", d=D)).then_inc(s_vg, 1)

            def split_max(g):
                for j in range(HG):
                    at = HG * g + j
                    pool.wait_ge(s_comb, at + 1)
                    after(pool, s_m3t, at)
                    settle(pool, passed_pool)
                    pool.tensor_scalar(m3[:, 0:ST], nm[:, :], -1.0, None, ALU.mult).then_inc(s_nm, 1)
                    pool.wait_ge(s_nm, 4 * at + 1)
                    pool.tensor_tensor(nr[:, :], nm[:, :], m3[:, 0:ST], ALU.add).then_inc(s_nm, 1)
                    pool.wait_ge(s_nm, 4 * at + 2)
                    settle(pool, passed_pool)
                    pool.tensor_scalar(m3[:, ST:2 * ST], nr[:, :], -1.0, None, ALU.mult).then_inc(s_nm, 1)
                    pool.wait_ge(s_nm, 4 * at + 3)
                    pool.tensor_tensor(nl[:, :], nr[:, :], m3[:, ST:2 * ST], ALU.add).then_inc(s_nm, 1)
                    pool.wait_ge(s_nm, 4 * at + 4)
                    settle(pool, passed_pool)
                    pool.tensor_scalar(m3[:, 2 * ST:3 * ST], nl[:, :], -1.0, None, ALU.mult).then_inc(s_m3, 1)

            copy_values(0, 0)
            copy_values(0, 1)
            split_max(0)

            def during(i, c):
                g = over(i, c, 1)
                if not (isinstance(g, int) and g + 1 >= NG):
                    split_max(g + 1)
                if not (isinstance(g, int) and g + 2 >= NG):
                    copy_values(i, c + 2)

            groups(pool, during)

            pool.wait_ge(s_ot, 16 * NG)
            for e in range(E):
                pool.dma_start(w2_sb[:, e, :, :], w2[e].rearrange("(k p) n -> p k n", p=KP)).then_inc(s_w2, 16)

            pool.wait_ge(s_dot, NT)
            made = [0]

            def const(ins):
                made[0] += 1
                ins.then_inc(s_rc, 1)
                pool.wait_ge(s_rc, made[0])

            const(pool.memset(ones_bf, 1.0))
            const(pool.memset(upper, 1.0))
            const(pool.affine_select(out=upper, in_=upper, compare_op=ALU.is_gt, fill=0.0, base=0,
                                     pattern=[[1, P]], channel_multiplier=-1))
            const(pool.iota(iota_i[:, 0:E], pattern=[[-1, E]], base=E, channel_multiplier=0))
            const(pool.tensor_copy(rev, iota_i[:, 0:E]))
            const(pool.iota(iota_i[:, 0:NT], pattern=[[P, NT]], base=0, channel_multiplier=0))
            const(pool.tensor_copy(iota128, iota_i[:, 0:NT]))
            const(pool.iota(iota_i, pattern=[[1, P]], base=0, channel_multiplier=0))
            const(pool.tensor_copy(iota_row, iota_i))
            const(pool.tensor_copy(iota_s, iota_i[:, 0:NS]))
            const(pool.iota(iota_i[:, 0:2 * NT], pattern=[[P, 2 * NT]], base=1, channel_multiplier=1))
            const(pool.tensor_copy(name, iota_i[:, 0:2 * NT]))
            const(pool.iota(iota_i[:, 0:1], pattern=[[1, 1]], base=2 * NTOK + 1, channel_multiplier=1))
            const(pool.tensor_copy(nobody, iota_i[:, 0:1]))
            def gather(t):
                pool.wait_ge(s_ig, t + 1)
                settle(pool, passed_pool)
                pool.indirect_dma_start(out=x_row, out_offset=None, in_=xn2_d,
                                        in_offset=bass.IndirectOffsetOnAxis(ap=at_x[:, 0:1], axis=0)).then_inc(s_xr, 16)

            def scatter(t):
                pool.wait_ge(s_is, t + 1)
                pool.wait_ge(s_yr, t + 1)
                settle(pool, passed_pool)
                pool.indirect_dma_start(out=y_d, out_offset=bass.IndirectOffsetOnAxis(ap=at_y[:, 0:1], axis=0),
                                        in_=y_row, in_offset=None).then_inc(s_ys, 16)

            pool.wait_ge(s_yc, 16)
            pool.wait_ge(s_keep[0], 8 * NT)
            pool.wait_ge(s_keep[1], 8 * NT)
            for t in range(3):
                gather(t)
            with pool.Fori(1, NS - 2) as t:
                gather(t + 2)
                scatter(t - 1)
            for t in range(NS - 3, NS):
                scatter(t)

        @block.vector
        def _(dve):

            def stats(n, p):
                if isinstance(n, int):
                    dve.wait_ge(s_x[0 if n < 8 else 1], 16 if n < 8 else 48)
                settle(dve, passed_dve)
                dve.bn_stats(stat[p], x_all[:, bass.ds(n, 1), :].rearrange("p a c -> p (a c)")).then_inc(s_stat, 1)

            def means(n, p):
                dve.wait_ge(s_stat, 2 * n + 1)
                after(dve, s_xn, n - 1)
                settle(dve, passed_dve)
                dve.bn_aggr(mv[p], stat[p]).then_inc(s_stat, 1)

            def invert(n, p):
                dve.wait_ge(s_std, n + 1)
                after(dve, s_xn, n - 1)
                dve.reciprocal(rstd[p], std[p]).then_inc(s_rstd, 1)

            def normalise(n, p):
                dve.wait_ge(s_rstd, n + 1)
                after(dve, s_xtp, n - 1)
                dve.tensor_scalar(xn[p], x_all[:, bass.ds(n, 1), :].rearrange("p a c -> p (a c)"), mv[p][:, 0:1], rstd[p], ALU.subtract, ALU.mult).then_inc(s_xn, 1)

            def biases(n, p):
                if isinstance(n, int) and n == 0:
                    dve.wait_ge(s_cload, 64)
                dve.wait_ge(s_qkv, n + 1)
                after(dve, s_rb, 2 * (n - 1))
                dve.tensor_tensor(qk[p], bank(2 + p), b_qkv[:, 0:2 * C], ALU.add).then_inc(s_qk, 1)
                dve.tensor_tensor(v_all[:, bass.ds(n, 1), :].rearrange("p a c -> p (a c)"), bank(4 + p)[:, 0:C],
                                  b_qkv[:, 2 * C:3 * C], ALU.add).then_inc(s_ra, 1)
                dve.wait_ge(s_qk, n + 1)
                after(dve, s_rr, n - 1)
                tab = cos_t[:, bass.ds(n % TPB, 1), :].to_broadcast([P, 2 * H, D])
                dve.tensor_tensor(ra[p].rearrange("p (h d) -> p h d", d=D), qk[p].rearrange("p (h d) -> p h d", d=D),
                                  tab, ALU.mult).then_inc(s_ra, 1)

            def rotate(n, p):
                dve.wait_ge(s_rb, 2 * (n + 1))
                dve.wait_ge(s_ra, 2 * (n + 1))
                after(dve, s_r1, n - 1)
                after(dve, s_hi, n - 1)
                dve.tensor_tensor(rr[p], ra[p], rb[p], ALU.add).then_inc(s_rr, 1)

            def rest(n, p):
                dve.wait_ge(s_hi, n + 1)
                after(dve, s_lo, n - 1)
                dve.tensor_tensor(r1[p], rr[p], parts[p][:, 0, :], ALU.subtract).then_inc(s_r1, 1)

            def save_parts(n, p):
                dve.wait_ge(s_pp, n + 1)
                dve.wait_ge(s_pst, 16 * (n // 4 + 1))
                dst = staged[:, bass.ds((n // 4) % 2, 1), 8:12, bass.ds((n % 4) * P, P)].rearrange("p a c t -> p (a c) t")
                dve.tensor_copy(dst, bank(7).bitcast(BF16)[:, 0:4 * P].rearrange("p (a t) -> p a t", t=P)).then_inc(s_pd, 1)

            steps(dve, NT, [(7, rest), (2, invert), (6, rotate), (5, biases), (2, normalise), (0, stats),
                            (8, save_parts), (0, means)])

            dve.wait_ge(s_bl, 32)
            dve.tensor_copy(b_p[0][:, :], b_f[:, :]).then_inc(s_bs, 1)
            dve.wait_ge(s_bs, 1)
            dve.tensor_tensor(b_r[:, :], b_f[:, :], b_p[0][:, :], ALU.subtract).then_inc(s_bs, 1)
            dve.wait_ge(s_bs, 2)
            dve.tensor_copy(b_p[1][:, :], b_r[:, :]).then_inc(s_bs, 1)
            dve.wait_ge(s_bs, 3)
            dve.tensor_tensor(b_f[:, :], b_r[:, :], b_p[1][:, :], ALU.subtract).then_inc(s_bs, 1)
            dve.wait_ge(s_bs, 4)
            dve.tensor_copy(b_p[2][:, :], b_f[:, :]).then_inc(s_bs, 2)

            def reduce_max(g, t3, k, half):
                j, t = k // ST, k % ST
                dve.wait_ge(s_mp, 2 * (STEPS * g + k) + half + 1)
                if t == 0:
                    after(dve, s_comb, HG * (g - 1) + j + 1)
                dve.tensor_reduce(mx[:, half, j, t:t + 1], bank(4 + (t3 + 2 * k + half) % 3), AX, ALU.max).then_inc(s_max, 1)

            def combine_max(g, j):
                at = HG * g + j
                dve.wait_ge(s_max, 2 * (STEPS * g + ST * (j + 1)))
                after(dve, s_m3, at)
                dve.tensor_reduce(nm[:, :], mx[:, :, j, :].rearrange("p h t -> p t h"), AX, ALU.max).then_inc(s_comb, 1)

            def turn(g, j):
                dve.wait_ge(s_m3, HG * g + j + 1)
                after(dve, s_mst, 16 * (HG * g + j))
                dve.transpose(m3_t[:, :], m3[:, :]).then_inc(s_m3t, 1)

            def max_pass(g, t3, first=False):
                for k in range(STEPS):
                    j = k // ST - 1
                    for half in range(2):
                        reduce_max(g, t3, k, half)
                    if first and j < 0:
                        continue
                    if k % ST == 0:
                        combine_max(*((g, j) if j >= 0 else (g - 1, HG - 1)))
                    if k % ST == 2:
                        turn(*((g, j) if j >= 0 else (g - 1, HG - 1)))

            dve.wait_ge(s_pa, NT)
            max_pass(0, 0, True)

            def during(i, c):
                g = over(i, c, 1)
                if not (isinstance(g, int) and g + 1 >= NG):
                    max_pass(g + 1, (c + 1) % 3)

            groups(dve, during)
            combine_max(NG - 1, HG - 1)
            turn(NG - 1, HG - 1)


            def invert_sums(n, p):
                dve.wait_ge(s_t1, n + 1)
                v = bank(p).rearrange("p (h c) -> p h c", c=32)
                dve.reciprocal(o_sum[:, p, :].rearrange("p (h c) -> p h c", c=1), v[:, :, D:D + 1]).then_inc(s_rs, 1)

            def norm_o(n, p):
                dve.wait_ge(s_rs, n + 1)
                after(dve, s_t2, n - 1)
                v = bank(p).rearrange("p (h c) -> p h c", c=32)
                dve.tensor_tensor(on[p].rearrange("p (h d) -> p h d", d=D), v[:, :, 0:D],
                                  o_sum[:, p, :].rearrange("p (h c) -> p h c", c=1).to_broadcast([P, H, D]),
                                  ALU.mult).then_inc(s_on, 1)

            def stats_y(n, p):
                dve.wait_ge(s_op, n + 1)
                settle(dve, passed_dve)
                dve.bn_stats(st_a[:, p, :], bank(3 + p)[:, 0:C]).then_inc(s_ya, 1)

            def means_y(n, p):
                dve.wait_ge(s_ya, 2 * n + 1)
                settle(dve, passed_dve)
                dve.bn_aggr(mv_a[:, p, :], st_a[:, p, :]).then_inc(s_ya, 1)

            def invert_y(n, p):
                dve.wait_ge(s_sda, n + 1)
                dve.reciprocal(rd_a[:, p, :], sd_a[:, p, :]).then_inc(s_z, 1)

            def norm_y(n, p):
                dve.wait_ge(s_z, 2 * n + 1)
                dve.tensor_scalar(yn[p], bank(3 + p)[:, 0:C], mv_a[:, p, 0:1], rd_a[:, p, :], ALU.subtract, ALU.mult).then_inc(s_z, 1)

            def add_y(n, p):
                if isinstance(n, int) and n == 0:
                    dve.wait_ge(s_x2l, 64)
                dve.wait_ge(s_z, 2 * n + 2)
                dve.tensor_tensor(row(x2, n), row(x2, n), yn[p], ALU.add).then_inc(s_x2, 1)

            def stats_x2(n, p):
                dve.wait_ge(s_x2, n + 1)
                settle(dve, passed_dve)
                dve.bn_stats(st_b[:, p, :], row(x2, n)).then_inc(s_xs, 1)

            def means_x2(n, p):
                dve.wait_ge(s_xs, 2 * n + 1)
                settle(dve, passed_dve)
                dve.bn_aggr(mv_b[:, p, :], st_b[:, p, :]).then_inc(s_xs, 1)

            def invert_x2(n, p):
                dve.wait_ge(s_sdb, n + 1)
                after(dve, s_xn2, n - 1)
                dve.reciprocal(rd_b[:, p, :], sd_b[:, p, :]).then_inc(s_rdb, 1)

            def offset_x2(n, p):
                dve.wait_ge(s_rdb, n + 1)
                dve.scalar_tensor_tensor(out=off[:, p, :], in0=mv_b[:, p, 0:1], scalar=-1.0, in1=rd_b[:, p, :],
                                         op0=ALU.mult, op1=ALU.mult).then_inc(s_ob, 1)

            steps(dve, NT, [(6, invert_x2), (5, invert_y), (6, offset_x2), (5, norm_y), (4, stats_y), (5, add_y),
                            (1, invert_sums), (4, means_y), (5, stats_x2), (1, norm_o), (5, means_x2)])

            done = [0]

            def step(ins):
                done[0] += 1
                ins.then_inc(s_rt, 1)
                dve.wait_ge(s_rt, done[0])

            def per_tile(v):
                return v.rearrange("p (n a) -> p n a", a=1).to_broadcast([P, NT, E])

            def per_expert(v, n=NT):
                return v.rearrange("p (a e) -> p a e", a=1).to_broadcast([P, n, E])

            dve.wait_ge(s_rc, 14)
            dve.wait_ge(s_dot, NT)
            dve.wait_ge(s_sq, NT)
            dve.tensor_tensor(ge[:, 0:2, :].rearrange("p k e -> p (k e)"), cent_t[:, :], cent_t[:, :], ALU.mult).then_inc(s_csq, 1)
            dve.wait_ge(s_c2, 1)
            step(dve.tensor_copy(c2, bank(7)[:, 0:E]))
            step(dve.tensor_tensor(tmp, per_tile(sq[:, :]), per_expert(c2), ALU.add))
            step(dve.scalar_tensor_tensor(out=dist, in0=bank(6)[:, 0:NT * E].rearrange("p (n e) -> p n e", e=E), scalar=-2.0,
                                          in1=tmp, op0=ALU.mult, op1=ALU.add))
            dve.tensor_scalar(tmp, dist, 1e-12, None, ALU.max).then_inc(s_dd, 1)
            dve.wait_ge(s_ds, 1)
            step(dve.tensor_reduce(v1, dist, AX, ALU.max))
            step(dve.tensor_tensor(tmp, dist, per_tile(v1), ALU.is_equal))
            step(dve.tensor_tensor(tmp, tmp, per_expert(rev), ALU.mult))
            step(dve.tensor_reduce(r_1, tmp, AX, ALU.max))
            step(dve.tensor_tensor(oh1, per_tile(r_1), per_expert(rev), ALU.is_equal))
            step(dve.tensor_scalar(oh2, oh1, -1.0, 1.0, ALU.mult, ALU.add))
            step(dve.tensor_tensor(dist, dist, oh2, ALU.mult))
            step(dve.tensor_reduce(v2, dist, AX, ALU.max))
            dve.tensor_tensor(more, v2, v1, ALU.subtract).then_inc(s_df, 1)
            step(dve.tensor_tensor(tmp, dist, per_tile(v2), ALU.is_equal))
            step(dve.tensor_tensor(tmp, tmp, per_expert(rev), ALU.mult))
            step(dve.tensor_reduce(r_1, tmp, AX, ALU.max))
            step(dve.tensor_tensor(oh2, per_tile(r_1), per_expert(rev), ALU.is_equal))
            dve.tensor_tensor(chosen.rearrange("p (n e) -> p n e", e=E), oh1, oh2, ALU.add).then_inc(s_ch, 1)
            dve.wait_ge(s_ex, 1)
            step(dve.tensor_scalar(v1, ratio, 1.0, None, ALU.add))
            step(dve.reciprocal(w_1[:, :], v1))
            step(dve.tensor_tensor(w_2[:, :], ratio, w_1[:, :], ALU.mult))
            dve.wait_ge(s_pos, 1)
            step(dve.tensor_copy(pos, bank(7)[:, 0:NT * E].rearrange("p (n e) -> p n e", e=E)))
            step(dve.tensor_copy(counts, bank(5)[:, 0:NT * E].rearrange("p (n e) -> p n e", e=E)))
            step(dve.memset(more, 1.0))
            for e in range(E):
                step(dve.tensor_tensor_scan(before[:, :, e], more, counts[:, :, e], 0.0, ALU.mult, ALU.add))
            total = before[:, NT - 1, :]
            step(dve.tensor_tensor(cmp_n, total.rearrange("p (e a) -> p e a", a=1).to_broadcast([P, E, NT]),
                                   iota128.rearrange("p (a n) -> p a n", a=1).to_broadcast([P, E, NT]), ALU.is_gt))
            step(dve.tensor_reduce(n_tiles, cmp_n, AX, ALU.add))
            step(dve.tensor_tensor_scan(first, more[:, 0:E], n_tiles, 0.0, ALU.mult, ALU.add))
            step(dve.tensor_tensor(first, first, n_tiles, ALU.subtract))
            step(dve.tensor_tensor(before, before, counts, ALU.subtract))
            step(dve.tensor_tensor(pos, pos, before, ALU.add))
            step(dve.tensor_scalar(c2, first, float(P), None, ALU.mult))
            step(dve.tensor_tensor(pos, pos, per_expert(c2), ALU.add))
            for n, oh in enumerate((oh1, oh2)):
                step(dve.tensor_tensor(tmp, pos, oh, ALU.mult))
                step(dve.tensor_reduce(low[:, n, :], tmp, AX, ALU.add))
            both = [v.rearrange("p a n -> p (a n)") for v in (high, low)]
            step(dve.tensor_scalar(both[0], both[1], 1.0 / P, (0.5 - P / 2) / P, ALU.mult, ALU.add))
            step(dve.tensor_scalar(both[0], both[0], 1.5 * 2 ** 23, None, ALU.add))
            step(dve.tensor_scalar(both[0], both[0], 1.5 * 2 ** 23, None, ALU.subtract))
            step(dve.scalar_tensor_tensor(out=both[1], in0=both[0], scalar=-float(P), in1=both[1], op0=ALU.mult, op1=ALU.add))
            step(dve.tensor_tensor(ge, iota_s.rearrange("p (s a) -> p s a", a=1).to_broadcast([P, NS, E]),
                                   per_expert(first, NS), ALU.is_ge))
            step(dve.tensor_reduce(e_of, ge, AX, ALU.add))
            step(dve.tensor_scalar(tile_e[0:1, :], e_of[0:1, :], -1.0, None, ALU.add))
            for b in range(2 * NT // 4):
                r = b % 2
                after(dve, s_tb, b - 1)
                dve.tensor_tensor(in_tile[:, r, :, :], iota_s.rearrange("p (a s) -> p a s", a=1).to_broadcast([P, 4, NS]),
                                  both[0][:, 4 * b:4 * b + 4].rearrange("p (n a) -> p n a", a=1).to_broadcast([P, 4, NS]),
                                  ALU.is_equal).then_inc(s_bh, 1)
                dve.tensor_tensor(in_row[:, r, :, :], iota_row.rearrange("p (a s) -> p a s", a=1).to_broadcast([P, 4, P]),
                                  both[1][:, 4 * b:4 * b + 4].rearrange("p (n a) -> p n a", a=1).to_broadcast([P, 4, P]),
                                  ALU.is_equal).then_inc(s_oh, 1)
                dve.wait_ge(s_bh, b + 1)
                dve.tensor_tensor(in_tile[:, r, :, :], in_tile[:, r, :, :],
                                  name[:, 4 * b:4 * b + 4].rearrange("p (n a) -> p n a", a=1).to_broadcast([P, 4, NS]),
                                  ALU.mult).then_inc(s_oh, 1)
            dve.wait_ge(s_tb, 2 * NT // 4)
            step(dve.tensor_scalar(place_of[:, :], bank(4)[:, 0:NS], 0.0, nobody, ALU.is_equal, ALU.mult))
            step(dve.scalar_tensor_tensor(out=place_of[:, :], in0=bank(4)[:, 0:NS], scalar=-1.0, in1=place_of[:, :],
                                          op0=ALU.add, op1=ALU.add))
            step(dve.tensor_scalar(iota_s, place_of[:, :], float(NTOK), -float(NTOK), ALU.is_ge, ALU.mult))
            step(dve.tensor_scalar(e_of, place_of[:, :], 2.0 * NTOK, -float(NTOK), ALU.is_ge, ALU.mult))
            step(dve.tensor_tensor(iota_s, iota_s, e_of, ALU.add))
            dve.tensor_tensor(token_of[:, :], place_of[:, :], iota_s, ALU.add).then_inc(s_slot, 1)
            dve.wait_ge(s_slot, 1)

            def save_xt2(t):
                dve.wait_ge(s_mt, t + 1)
                after(dve, s_gu, 4 * t)
                dve.tensor_copy(x_t.rearrange("p k t -> p (k t)"), bank(6)[:, 0:C]).then_inc(s_mx, 1)

            def hidden(t):
                after(dve, s_ht, t)
                for c in range(2):
                    dve.wait_ge(s_gu, 4 * t + 2 * c + 2)
                    dve.wait_ge(s_si, 2 * t + c + 1)
                    dve.tensor_tensor(hid[:, CH * c:CH * (c + 1)], bank(2 * c + 1)[:, 0:CH], gates[c], ALU.mult).then_inc(s_hid, 1)

            def save_ht(t):
                dve.wait_ge(s_ht, t + 1)
                after(dve, s_yp, t)
                dve.tensor_copy(h_t.rearrange("p k t -> p (k t)")[0:KP, 4 * P:6 * P], bank(5)[0:KP, 0:2 * P]).then_inc(s_htd, 1)

            def aim_gather(t):
                after(dve, s_xr, 16 * t)
                dve.tensor_copy(at_x[:, :], token_of[:, bass.ds(t, 1)]).then_inc(s_ig, 1)

            def aim_scatter(t):
                after(dve, s_ys, 16 * t)
                dve.tensor_copy(at_y[:, :], place_of[:, bass.ds(t, 1)]).then_inc(s_is, 1)

            aim_gather(0)
            save_xt2(0)
            aim_gather(1)
            for t in range(2):
                hidden(t)
                save_xt2(t + 1)
                aim_gather(t + 2)
                if t > 0:
                    aim_scatter(t - 1)
                save_ht(t)
            with dve.Fori(2, NS - 2) as t:
                hidden(t)
                save_xt2(t + 1)
                aim_gather(t + 2)
                aim_scatter(t - 1)
                save_ht(t)
            for t in range(NS - 2, NS):
                hidden(t)
                if t + 1 < NS:
                    save_xt2(t + 1)
                aim_scatter(t - 1)
                save_ht(t)
            aim_scatter(NS - 1)

            def mix(n, p):
                dve.wait_ge(s_f1, n + 1)
                dve.scalar_tensor_tensor(out=row(y1_all, n), in0=row(y2_all, n), scalar=w_2[:, bass.ds(n, 1)],
                                         in1=row(y1_all, n), op0=ALU.mult, op1=ALU.add).then_inc(s_fm, 1)

            def stats_mix(n, p):
                dve.wait_ge(s_fm, n + 1)
                settle(dve, passed_dve)
                dve.bn_stats(st_a[:, p, :], row(y1_all, n)).then_inc(s_fs, 1)

            def means_mix(n, p):
                dve.wait_ge(s_fs, 2 * n + 1)
                settle(dve, passed_dve)
                dve.bn_aggr(mv_a[:, p, :], st_a[:, p, :]).then_inc(s_fs, 1)

            def invert_mix(n, p):
                dve.wait_ge(s_fd, n + 1)
                after(dve, s_fn, n - 1)
                dve.reciprocal(rd_a[:, p, :], sd_a[:, p, :]).then_inc(s_fr, 1)

            def offset_mix(n, p):
                dve.wait_ge(s_fr, n + 1)
                dve.scalar_tensor_tensor(out=off[:, p, :], in0=mv_a[:, p, 0:1], scalar=-1.0, in1=rd_a[:, p, :],
                                         op0=ALU.mult, op1=ALU.mult).then_inc(s_fb, 1)

            def finish(n, p):
                dve.wait_ge(s_fn, n + 1)
                dve.tensor_tensor(row(y1_all, n), row(y1_all, n), row(x2, n), ALU.add).then_inc(s_fo, 1)

            steps(dve, NT, [(3, invert_mix), (1, mix), (3, offset_mix), (5, finish), (1, stats_mix), (1, means_mix)])

        @block.scalar
        def _(act):
            act.wait_ge(s_const, 7)

            def deviation(n, p):
                act.wait_ge(s_stat, 2 * n + 2)
                after(act, s_rstd, n - 1)
                act.activation(std[p], mv[p][:, 1:2], ACT.Sqrt, bias=eps[:, 0:1]).then_inc(s_std, 1)

            def save_xt(n, p):
                act.wait_ge(s_xtp, n + 1)
                after(act, s_qkv, n - 1)
                act.activation(xn_t[p].rearrange("p k t -> p (k t)"), bank(p)[:, 0:C], ACT.Copy).then_inc(s_xt, 1)

            def high(n, p):
                act.wait_ge(s_rr, n + 1)
                after(act, s_pp, n - 1)
                act.activation(parts[p][:, 0, :], rr[p], ACT.Copy).then_inc(s_hi, 1)

            def middle(n, p):
                act.wait_ge(s_r1, n + 1)
                act.activation(parts[p][:, 1, :], r1[p], ACT.Copy).then_inc(s_mid, 1)

            def save_parts(n, p):
                act.wait_ge(s_pp, n + 1)
                src = bank(6).bitcast(BF16).rearrange("p (a t) -> p a t", t=P)
                act.wait_ge(s_pst, 16 * (n // 4 + 1))
                dst = staged[:, bass.ds((n // 4) % 2, 1), 0:8, bass.ds((n % 4) * P, P)].rearrange("p a c t -> p (a c) t")
                act.activation(dst, src, ACT.Copy).then_inc(s_pa, 1)

            steps(act, NT, [(7, middle), (3, save_xt), (6, high), (8, save_parts), (1, deviation)])

            def group(i, c):
                g, first = over(i, c, 1), c == 0
                for k in range(STEPS):
                    u, pair = k // 2, k % 2
                    act.wait_ge(s_sp, STEPS * g + k + 1)
                    if pair == 0 and not (first and u < 4):
                        act.wait_ge(s_pv, UNITS * g + u - 3)
                    act.activation(pt[u % 4][:, 2 * pair:2 * pair + 2, :].rearrange("p a t -> p (a t)"),
                                   bank(2 * pair, 2), ACT.Exp, scale=SC).then_inc(s_exp, 1)
                    if k == 1 and not first:
                        save_o(g - 1, 1)
                    if k == STEPS // 2 + 1:
                        save_o(g, 0)

            def save_o(g, half):
                act.wait_ge(s_pv, UNITS * g + ST * (half + 1))
                if half == 0:
                    after(act, s_ot, 16 * g)
                act.activation(o_stage[:, 512 * half:512 * (half + 1)], bank(7), ACT.Copy).then_inc(s_oe, 1)

            groups(act, group)
            save_o(NG - 1, 1)

            def save_ont(n, p):
                act.wait_ge(s_t2, n + 1)
                after(act, s_op, n - 1)
                act.activation(on_t[p].rearrange("p k t -> p (k t)"), bank(2)[:, 0:C], ACT.Copy).then_inc(s_ont, 1)

            def deviation_y(n, p):
                act.wait_ge(s_ya, 2 * n + 2)
                after(act, s_z, 2 * (n - 1))
                act.activation(sd_a[:, p, :], mv_a[:, p, 1:2], ACT.Sqrt, bias=eps[:, 0:1]).then_inc(s_sda, 1)

            def deviation_x2(n, p):
                act.wait_ge(s_xs, 2 * n + 2)
                after(act, s_rdb, n - 1)
                act.activation(sd_b[:, p, :], mv_b[:, p, 1:2], ACT.Sqrt, bias=eps[:, 0:1]).then_inc(s_sdb, 1)

            def norm_x2(n, p):
                if isinstance(n, int) and n == 0:
                    act.wait_ge(s_yc, 16)
                act.wait_ge(s_ob, n + 1)
                after(act, s_keep[p], 8 * (n - p))
                after(act, s_sq, n - 1)
                after(act, s_t3, n - 1)
                act.activation(xn2[p][:, :], row(x2, n), ACT.Identity, bias=off[:, p, :],
                               scale=rd_b[:, p, :]).then_inc(s_xn2, 1)

            def squares(n, p):
                act.wait_ge(s_xn2, n + 1)
                after(act, s_sq, n)
                act.activation(square[:, :], xn2[p][:, :], ACT.Square, accum_out=sq[:, bass.ds(n, 1)]).then_inc(s_sq, 1)

            def save_xn2t(n, p):
                act.wait_ge(s_t3, n + 1)
                after(act, s_dot, n - 1)
                act.activation(xn2_t[p].rearrange("p k t -> p (k t)"), bank(5)[:, 0:C], ACT.Copy).then_inc(s_xn2t, 1)

            steps(act, NT, [(6, norm_x2), (8, save_xn2t), (7, squares), (5, deviation_x2), (4, deviation_y), (2, save_ont)])

            act.wait_ge(s_dd, 1)
            act.activation(dist, tmp, ACT.Sqrt).then_inc(s_ds, 1)
            act.wait_ge(s_df, 1)
            act.activation(ratio, more, ACT.Exp).then_inc(s_ex, 1)

            def gate(t):
                for c in range(2):
                    act.wait_ge(s_gu, 4 * t + 2 * c + 1)
                    after(act, s_hid, 2 * (t - 1) + c + 1)
                    act.activation(gates[c], bank(2 * c)[:, 0:CH], ACT.Silu).then_inc(s_si, 1)

            def save_y(t):
                act.wait_ge(s_yp, t + 1)
                after(act, s_ys, 16 * t)
                act.activation(y_row, bank(7)[:, 0:C], ACT.Copy).then_inc(s_yr, 1)

            def save_ht(t):
                act.wait_ge(s_ht, t + 1)
                after(act, s_yp, t)
                act.activation(h_t.rearrange("p k t -> p (k t)")[0:KP, 0:4 * P], bank(4)[0:KP, :], ACT.Copy).then_inc(s_hta, 1)

            gate(0)
            save_ht(0)
            gate(1)
            save_y(0)
            save_ht(1)
            with act.Fori(2, NS) as t:
                gate(t)
                save_y(t - 1)
                save_ht(t)
            save_y(NS - 1)

            def weigh_first(n, p):
                act.wait_ge(s_back, n + 1)
                act.activation(y1_all[:, bass.ds(n, 1), :].rearrange("p a c -> p (a c)"),
                               y1_all[:, bass.ds(n, 1), :].rearrange("p a c -> p (a c)"), ACT.Copy,
                               scale=w_1[:, bass.ds(n, 1)]).then_inc(s_f1, 1)

            def deviation_mix(n, p):
                act.wait_ge(s_fs, 2 * n + 2)
                act.activation(sd_a[:, p, :], mv_a[:, p, 1:2], ACT.Sqrt, bias=eps[:, 0:1]).then_inc(s_fd, 1)

            def norm_mix(n, p):
                act.wait_ge(s_fb, n + 1)
                act.activation(row(y1_all, n), row(y1_all, n), ACT.Identity, bias=off[:, p, :],
                               scale=rd_a[:, p, :]).then_inc(s_fn, 1)

            steps(act, NT, [(4, norm_mix), (0, weigh_first), (2, deviation_mix)])

        @block.tensor
        def _(pe):
            pe.wait_ge(s_const, 7)
            pe.wait_ge(s_cload, 64)

            def turn_x(n, p):
                pe.wait_ge(s_xn, n + 1)
                after(pe, s_xt, n - 1)
                for k in range(KC):
                    last = pe.transpose(bank(p)[:, P * k:P * (k + 1)], xn[p][:, P * k:P * (k + 1)], ident[:, :])
                last.then_inc(s_xtp, 1)

            def project(n, p):
                pe.wait_ge(s_xt, n + 1)
                after(pe, s_qk, n - 1)
                after(pe, s_ra, 2 * (n - 1))
                for k in range(KC):
                    pe.matmul(bank(2 + p), xn_t[p][:, k, :], w_qkv[:, k, 0:2 * C], start=k == 0, stop=k == KC - 1)
                for k in range(KC):
                    last = pe.matmul(bank(4 + p)[:, 0:C], xn_t[p][:, k, :], w_qkv[:, k, 2 * C:3 * C],
                                     start=k == 0, stop=k == KC - 1)
                last.then_inc(s_qkv, 1)

            def turn_parts(n, p):
                pe.wait_ge(s_lo, n + 1)
                after(pe, s_pa, n)
                after(pe, s_pd, n)
                for a in range(12):
                    dst = bank(6, 2).bitcast(BF16)[:, P * a:P * (a + 1)]
                    last = pe.transpose(dst, parts[p].rearrange("p s c -> p (s c)")[:, P * a:P * (a + 1)], ident_bf[:, :])
                last.then_inc(s_pp, 1)

            steps(pe, NT, [(8, turn_parts), (3, turn_x), (4, project)])

            def max_scores(g, t3, k, half):
                j, t = k // ST, k % ST
                piece = 2 * k + half
                after(pe, s_max, 2 * STEPS * g + piece - 2)
                pe.matmul(bank(4 + (t3 + piece) % 3), qs[t3][0:QROWS, j, P * t:P * (t + 1)],
                          ks[t3][0:QROWS, j, 512 * half:512 * (half + 1)], start=True, stop=True).then_inc(s_mp, 1)

            def scores(g, t3, k):
                half, st, pair = k // UNITS, k // 2 % ST, k % 2
                after(pe, s_exp, STEPS * g + k - 1)
                for j in (2 * pair, 2 * pair + 1):
                    if k < 2:
                        pe.wait_ge(s_ml[j], 16 * (g + 1))
                    last = pe.matmul(bank(j), ks[t3][0:MROWS, j, P * st:P * (st + 1)],
                                     qs[t3][0:MROWS, j, 512 * half:512 * (half + 1)], start=True, stop=True)
                last.then_inc(s_sp, 1)

            def weigh(g, p, u):
                half, st = u // ST, u % ST
                pe.wait_ge(s_exp, STEPS * g + 2 * u + 2)
                if st == 0:
                    if half == 0:
                        pe.wait_ge(s_vg, g + 1)
                    after(pe, s_oe, 2 * g + half)
                for j in range(HG):
                    last = pe.matmul(bank(7)[32 * j:32 * (j + 1), :], vg[p][:, st, j, :],
                                     pt[u % 4][:, j, :], start=st == 0, stop=st == ST - 1,
                                     tile_position=(0, 32 * j))
                last.then_inc(s_pv, 1)

            def group(i, c):
                g, p, t3 = over(i, c, 1), c % 2, c % 3
                for k in range(STEPS):
                    ahead, m = 1 + (k + LEAD) // STEPS, (k + LEAD) % STEPS
                    more = not (isinstance(g, int) and g + ahead >= NG)
                    if more:
                        if m == 0:
                            pe.wait_ge(s_stack[(c + ahead) % 3], STACK_DMAS * (over(i, c + ahead, 3) + 1))
                        max_scores(g + ahead, (c + ahead) % 3, m, 0)
                    scores(g, t3, k)
                    if more:
                        max_scores(g + ahead, (c + ahead) % 3, m, 1)
                    if k % 2 == 1 and k >= 3:
                        weigh(g, p, k // 2 - 1)
                    elif k == 1 and c > 0:
                        weigh(g - 1, 1 - p, UNITS - 1)

            pe.wait_ge(s_qk, NT)
            pe.wait_ge(s_ra, 2 * NT)
            pe.wait_ge(s_pa, NT)
            for g in range(2):
                pe.wait_ge(s_stack[g], STACK_DMAS)
                for k in range([STEPS, LEAD][g]):
                    for half in range(2):
                        max_scores(g, g, k, half)
            pe.wait_ge(s_pd, NT)
            pe.wait_ge(s_ones, 5)
            groups(pe, group)
            weigh(NG - 1, 1, UNITS - 1)

            pe.wait_ge(s_wo, 48)
            pe.wait_ge(s_oe, 2 * NG)
            pe.wait_ge(s_exp, STEPS * NG)
            pe.wait_ge(s_max, 2 * STEPS * NG)

            def turn_ot(n, p):
                pe.wait_ge(s_otl[p], 8 * (n + (2 - p)))
                after(pe, s_on, n - 1)
                for k in range(HG):
                    last = pe.transpose(bank(p)[:, P * k:P * (k + 1)], ot[p][:, k, :], ident[:, :])
                last.then_inc(s_t1, 1)

            def turn_on(n, p):
                pe.wait_ge(s_on, n + 1)
                after(pe, s_ont, n)
                for k in range(KC):
                    last = pe.transpose(bank(2)[:, P * k:P * (k + 1)], on[p][:, P * k:P * (k + 1)], ident[:, :])
                last.then_inc(s_t2, 1)

            def project_o(n, p):
                pe.wait_ge(s_ont, n + 1)
                after(pe, s_z, 2 * (n - 1))
                pe.matmul(bank(3 + p)[:, 0:C], ones_f[0:1, :], b_o, start=True, stop=False)
                for k in range(KC):
                    last = pe.matmul(bank(3 + p)[:, 0:C], on_t[p][:, k, :], w_o[:, k, :], start=False, stop=k == KC - 1)
                last.then_inc(s_op, 1)

            def turn_xn2(n, p):
                pe.wait_ge(s_xn2, n + 1)
                after(pe, s_xn2t, n)
                for k in range(KC):
                    last = pe.transpose(bank(5)[:, P * k:P * (k + 1)], xn2[p][:, P * k:P * (k + 1)], ident[:, :])
                last.then_inc(s_t3, 1)

            def dots(n, p):
                pe.wait_ge(s_xn2t, n + 1)
                for k in range(KC):
                    last = pe.matmul(bank(6)[:, bass.ds(n * E, E)], xn2_t[p][:, k, :], cent_t[:, E * k:E * (k + 1)],
                                     start=k == 0, stop=k == KC - 1)
                last.then_inc(s_dot, 1)

            steps(pe, NT, [(9, dots), (8, turn_xn2), (3, project_o), (2, turn_on), (0, turn_ot)])

            pe.wait_ge(s_csq, 1)
            for k in range(KC):
                last = pe.matmul(bank(7)[:, 0:E], ones_f[:, :], ge[:, k, :], start=k == 0, stop=k == KC - 1)
            last.then_inc(s_c2, 1)
            pe.wait_ge(s_ch, 1)
            pe.matmul(bank(7)[:, 0:NT * E], upper, chosen, start=True, stop=True)
            pe.matmul(bank(5)[:, 0:NT * E], ones_bf, chosen, start=True, stop=True).then_inc(s_pos, 1)
            for b in range(2 * NT // 4):
                pe.wait_ge(s_oh, 2 * b + 2)
                for n in range(4):
                    last = pe.matmul(bank(4)[:, 0:NS], in_row[:, b % 2, n, :], in_tile[:, b % 2, n, :],
                                     start=b + n == 0, stop=(b, n) == (2 * NT // 4 - 1, 3))
                last.then_inc(s_tb, 1)

            def turn_rows(t):
                pe.wait_ge(s_xr, 16 * (t + 1))
                after(pe, s_mx, t)
                for k in range(KC):
                    last = pe.transpose(bank(6)[:, P * k:P * (k + 1)], x_row[:, P * k:P * (k + 1)], ident[:, :])
                last.then_inc(s_mt, 1)

            def expert(t):
                return pe.value_load(tile_e[0:1, bass.ds(t, 1)], min_val=0, max_val=E - 1)

            def gate_up(t, e):
                pe.wait_ge(s_mx, t + 1)
                for c in range(4):
                    col = (c % 2) * HID + (c // 2) * CH
                    if c % 2 == 0:
                        after(pe, s_si, 2 * (t - 1) + c // 2 + 1)
                    else:
                        after(pe, s_hid, 2 * (t - 1) + c // 2 + 1)
                    dst = bank(c)[:, 0:CH]
                    pe.matmul(dst, ones3[:, :], b1_sb[0:3, bass.ds(e, 1), col:col + CH].rearrange("p a n -> p (a n)"),
                              start=True, stop=False)
                    for k in range(KC):
                        last = pe.matmul(dst, x_t[:, k, :],
                                         w1_sb[:, bass.ds(e, 1), k, col:col + CH].rearrange("p a n -> p (a n)"),
                                         start=False, stop=k == KC - 1)
                    last.then_inc(s_gu, 1)

            def turn_hidden(t):
                pe.wait_ge(s_hid, 2 * t + 2)
                after(pe, s_hta, t)
                after(pe, s_htd, t)
                for k in range(KH):
                    last = pe.transpose(bank(4, 2)[0:KP, P * k:P * (k + 1)], hid[:, KP * k:KP * (k + 1)], ident[:, :])
                last.then_inc(s_ht, 1)

            def down(t, e):
                pe.wait_ge(s_hta, t + 1)
                pe.wait_ge(s_htd, t + 1)
                after(pe, s_yr, t)
                pe.matmul(bank(7)[:, 0:C], ones3[:, :], b2_sb[0:3, bass.ds(e, 1), :].rearrange("p a n -> p (a n)"),
                          start=True, stop=False)
                for k in range(KH):
                    last = pe.matmul(bank(7)[:, 0:C], h_t[0:KP, k, :],
                                     w2_sb[:, bass.ds(e, 1), k, :].rearrange("p a n -> p (a n)"),
                                     start=False, stop=k == KH - 1)
                last.then_inc(s_yp, 1)

            pe.wait_ge(s_slot, 1)
            pe.wait_ge(s_w, 16 * E)
            pe.wait_ge(s_w2, 16 * E)
            pe.wait_ge(s_brow, 32)
            turn_rows(0)
            gate_up(0, expert(0))
            turn_rows(1)
            turn_hidden(0)
            gate_up(1, expert(1))
            turn_rows(2)
            down(0, expert(0))
            turn_hidden(1)
            with pe.Fori(2, NS - 1) as t:
                gate_up(t, expert(t))
                turn_rows(t + 1)
                down(t - 1, expert(t - 1))
                turn_hidden(t)
            gate_up(NS - 1, expert(NS - 1))
            down(NS - 2, expert(NS - 2))
            turn_hidden(NS - 1)
            down(NS - 1, expert(NS - 1))


def layout(inputs):
    g = {k.replace("L0_", ""): np.asarray(v) for k, v in inputs.items()}
    half = np.arange(HALF, dtype=np.float32)
    theta = np.power(np.float32(10000.0), -half / np.float32(HALF)).astype(np.float32)
    freqs = np.arange(T, dtype=np.float32)[:, None] * theta[None, :]
    cos, sin = np.cos(freqs).astype(np.float32), np.sin(freqs).astype(np.float32)
    rope = np.stack([np.concatenate([cos, cos], 1), np.concatenate([-sin, sin], 1)])
    return {
        "x": g["attn_x"].reshape(NTOK, C),
        "wqkv": np.concatenate([g["attn_Wq"].T, g["attn_Wk"].T, g["attn_Wv"].T], axis=1),
        "bqkv": np.concatenate([g["attn_bq"], g["attn_bk"], g["attn_bv"]]),
        "wo": g["attn_Wo"].T,
        "bo": g["attn_bo"],
        "rope": rope,
        "cent": g["ffn_centroid"].T,
        "w1": np.concatenate([g["ffn_Wg"], g["ffn_W1"]], axis=2),
        "b1": np.concatenate([g["ffn_bg"], g["ffn_b1"]], axis=1),
        "w2": g["ffn_W2"],
        "b2": g["ffn_b2"],
    }


def kernel(**inputs):
    import concourse.bacc as bacc
    from concourse.bass_utils import run_bass_kernel_spmd

    nc = bacc.Bacc("TRN2", target_bir_lowering=False, num_devices=1,
                   dynamic_dma_scratch_size=8192)
    arrays, args = {}, []
    for name, a in layout(inputs).items():
        a = np.ascontiguousarray(a)
        arrays[f"in_{name}"] = a
        args.append(nc.dram_tensor(f"in_{name}", a.shape, mybir.dt.from_np(a.dtype), kind="ExternalInput").ap())
    args.append(nc.dram_tensor("out_x", (NTOK, C), F32, kind="ExternalOutput").ap())
    build(nc, *args)
    r = run_bass_kernel_spmd(nc, [arrays], core_ids=[0])
    return np.asarray(r.results[0]["out_x"]).reshape(B, T, C)
```

```python
from contextlib import ExitStack

import numpy as np

import concourse.bass as bass
from concourse import mybir

F32 = mybir.dt.float32
BF16 = mybir.dt.bfloat16
I32 = mybir.dt.int32
ALU = mybir.AluOpType
ACT = mybir.ActivationFunctionType
AX = mybir.AxisListType.X

P = 128
B, T, C = 4, 1024, 256
H, D = 16, 16
HALF = D // 2
E, HID = 8, 684
NTOK = B * T
NT = NTOK // P
TPB = T // P
KC = C // P
HG = 4
NG = B * H // HG
QROWS = 6 * D
MROWS = QROWS + 3
ST = T // P
STACK_DMAS = 12 * 16
STEPS = ST * HG
UNITS = STEPS // 2
LEAD = 6
SC = D ** -0.5
CH = HID // 2
KH, KP = 6, HID // 6
NS = 2 * NTOK // P + E - 1
EPS = 1e-5

Q_PART = [0, 0, 1, 1, 0, 2]
K_PART = [0, 1, 0, 1, 2, 0]


def steps(eng, count, stages, head=2):
    lag = max(l for l, _ in stages)
    lo = (lag + head + 1) // 2 * 2
    hi = count - count % 2

    def one(s):
        for l, f in stages:
            if 0 <= s - l < count:
                f(s - l, (s - l) % 2)

    for s in range(lo):
        one(s)
    with eng.Fori(0, (hi - lo) // 2) as i:
        for q in range(2):
            for l, f in stages:
                f(2 * i + (lo + q - l), (lo + q - l) % 2)
    for s in range(hi, count + lag):
        one(s)


def after(eng, sem, value):
    if not isinstance(value, int) or value > 0:
        eng.wait_ge(sem, value)


def over(i, c, m):
    return (6 // m) * i + c // m


def groups(eng, body):
    body(0, 0)
    body(0, 1)
    with eng.Fori(0, (NG - 4) // 6) as i:
        for c in range(2, 8):
            body(i, c)
    for c in range(2, 4):
        body((NG - 4) // 6, c)


def settle(eng, passed):
    eng.sem_inc(passed)


class Carve:

    def __init__(self, region):
        self.region, self.at = region, 0

    def take(self, shape, dt=F32):
        n = int(np.prod(shape)) * (2 if dt == BF16 else 4) // 4
        v = self.region[:, self.at:self.at + n]
        self.at += n
        assert self.at <= self.region.shape[1], (self.at, self.region.shape)
        if dt != F32:
            v = v.bitcast(dt)
        names = "abcde"[:len(shape)]
        if len(shape) > 1:
            v = v.rearrange("p (" + " ".join(names) + ") -> p " + " ".join(names),
                            **{c: s for c, s in zip(names, shape)})
        return v


def build(nc, x, wqkv, bqkv, wo, bo, rope, cent, w1, b1, w2, b2, out):
    ctx = ExitStack()
    with ctx:
        def sb(name, shape, dt=F32):
            return ctx.enter_context(nc.sbuf_tensor(name, shape, dt))

        def sem(name):
            return ctx.enter_context(nc.semaphore(name))

        weights = sb("weights", [P, E * KC * 2 * HID + E * KH * C])
        work = sb("work", [P, 16384])
        stacks, probs = work[:, 0:8192], work[:, 8192:]
        values = sb("values", [P, 2048])
        ident = sb("ident", [P, P])
        ident_bf = sb("ident_bf", [P, P], BF16)
        eps = sb("eps", [P, 1])
        ones_f = sb("ones_f", [P, P])
        psum = ctx.enter_context(nc.psum_tensor("psum", [P, 8 * 512], F32))

        def bank(k, n=1):
            return psum[:, 512 * k:512 * (k + n)]

        ot_scr = nc.dram_tensor("ot_scr", (NG, P, T), F32, kind="Internal").ap()
        qk_scr = nc.dram_tensor("qk_scr", (3, 2, 2, P, NTOK), BF16, kind="Internal").ap()
        m_scr = nc.dram_tensor("m_scr", (HG, P, 32), BF16, kind="Internal").ap()
        v_scr = nc.dram_tensor("v_scr", (B, HG, P, ST, HG * D), F32, kind="Internal").ap()

        c = Carve(weights)
        x_all = c.take([NT, C])
        v_all = c.take([NT, C])
        staged = c.take([2, 12, 4 * P], BF16)
        q_first, k_first = c.take([HG, T], BF16), c.take([HG, T], BF16)
        c = Carve(weights)
        c.at = (E - 3) * KC * 2 * HID
        o_stage = c.take([T])
        v_stage = [c.take([ST, HG * D]) for _ in range(2)]
        assert c.at <= (E - 2) * KC * 2 * HID
        c = Carve(stacks)
        w_qkv = c.take([KC, 3 * C])
        b_qkv = c.take([3 * C])
        cos_t, sin_t = c.take([TPB, D]), c.take([TPB, D])
        xn = [c.take([C]) for _ in range(2)]
        xn_t = [c.take([KC, P]) for _ in range(2)]
        stat = [c.take([6]) for _ in range(2)]
        mv = [c.take([2]) for _ in range(2)]
        std = [c.take([1]) for _ in range(2)]
        rstd = [c.take([1]) for _ in range(2)]
        c = Carve(probs)
        qk = [c.take([2 * C]) for _ in range(2)]
        ra = [c.take([2 * C]) for _ in range(2)]
        rb = [c.take([2 * C]) for _ in range(2)]
        rr = [c.take([2 * C]) for _ in range(2)]
        r1 = [c.take([2 * C]) for _ in range(2)]
        parts = [c.take([3, 2 * C], BF16) for _ in range(2)]
        c = Carve(stacks)
        qs = [q_first] + [c.take([HG, T], BF16) for _ in range(2)]
        ks = [k_first] + [c.take([HG, T], BF16) for _ in range(2)]
        c = Carve(probs)
        pt = [c.take([HG, T // 2]) for _ in range(4)]
        c = Carve(values)
        vg = [c.take([ST, HG, 32]) for _ in range(2)]
        mx = sb("mx", [P, 2, HG, ST])
        nm = sb("nm", [P, ST])
        nr = sb("nr", [P, ST])
        nl = sb("nl", [P, ST])
        m3 = sb("m3", [P, 32], BF16)
        m3_t = sb("m3_t", [P, 32], BF16)

        w1_size = E * KC * 2 * HID
        w1_sb = weights[:, 0:w1_size].rearrange("p (e k n) -> p e k n", e=E, k=KC)
        w2_sb = weights[0:KP + 1, w1_size:w1_size + E * KH * C].rearrange("p (e k n) -> p e k n", e=E, k=KH)
        x2 = stacks.rearrange("p (n c) -> p n c", c=C)
        c = Carve(weights)
        c.at = (E - 2) * KC * 2 * HID
        ot = [c.take([HG, P]) for _ in range(2)]
        on = [c.take([C]) for _ in range(2)]
        on_t = [c.take([KC, P]) for _ in range(2)]
        assert c.at <= (E - 1) * KC * 2 * HID
        c = Carve(weights)
        c.at = (E - 1) * KC * 2 * HID
        w_o, b_o = c.take([KC, C]), c.take([C])[0:1, :]
        yn = [c.take([C]) for _ in range(2)]
        xn2_t = [c.take([KC, P]) for _ in range(2)]
        assert c.at <= w1_size
        xn2 = [sb(f"xn2_{i}", [P, C]) for i in range(2)]
        o_sum = sb("o_sum", [P, 2, H])
        small = sb("small", [P, 2, 22])
        st_a, st_b = small[:, :, 0:6], small[:, :, 6:12]
        mv_a, mv_b = small[:, :, 12:14], small[:, :, 14:16]
        sd_a, sd_b = small[:, :, 16:17], small[:, :, 17:18]
        rd_a, rd_b = small[:, :, 18:19], small[:, :, 19:20]
        off_a, off_b = small[:, :, 20:21], small[:, :, 21:22]
        cent_t = sb("cent_t", [P, KC * E])
        w_1 = sb("w_1", [P, NT])
        w_2 = sb("w_2", [P, NT])
        token_of = sb("token_of", [P, NS])
        place_of = sb("place_of", [P, NS])
        at_x = sb("at_x", [P, 1], I32)
        at_y = sb("at_y", [P, 1], I32)
        sq = sb("sq", [P, NT])
        tile_e = sb("tile_e", [1, NS], I32)
        c = Carve(values)
        pos = c.take([NT, E])
        before = c.take([NT, E])
        dist = c.take([NT, E])
        oh1 = c.take([NT, E])
        oh2 = c.take([NT, E])
        tmp = c.take([NT, E])
        counts = c.take([NT, E])
        more = c.take([NT])
        c = Carve(weights)
        c.at = (E - 3) * KC * 2 * HID
        chosen = c.take([NT * E], BF16)
        upper = c.take([P], BF16)
        ones_bf = c.take([P], BF16)
        rev = c.take([E])
        iota128 = c.take([NT])
        iota_s = c.take([NS])
        iota_i = c.take([P]).bitcast(I32)
        iota_row = c.take([P])
        number = c.take([1])
        nobody = c.take([1])
        high = c.take([2, NT])
        low = c.take([2, NT])
        before_it = c.at
        in_tile = c.take([4, 4, 2, NS], BF16)
        c.at = before_it
        ge = c.take([NS, E])
        c.at = before_it + 4 * 4 * NS
        cmp_n = c.take([E, NT])
        c2 = c.take([E])
        v1 = c.take([NT])
        v2 = c.take([NT])
        ratio = c.take([NT])
        r_1 = c.take([NT])
        e_of = c.take([NS])
        n_tiles = c.take([E])
        first = c.take([E])
        assert c.at <= (E - 2) * KC * 2 * HID
        c = Carve(work)
        c.at = 16384 - (KH * P + C)
        in_row = work[:, c.at:].bitcast(BF16).rearrange("p (b n s) -> p b n s", b=4, n=4)
        h_t = c.take([KH, P])
        y_row = c.take([C])
        c.at = 16384 - (KH * P + C) - E * 2 * HID
        kept = c.at // C // 4 * 4
        early = -(-(8192 - c.at) // (2 * HID))
        b1_sb = c.take([E, 2 * HID])
        c = Carve(values)
        x_row, x_t = c.take([C]), c.take([KC, P])
        hid = c.take([HID])
        gates = [c.take([CH]) for _ in range(2)]
        mixed = sb("mixed", [P, 2, 2, 11])
        st_m, mv_m = mixed[:, :, :, 0:6], mixed[:, :, :, 6:8]
        sd_m, rd_m, off_m = mixed[:, :, :, 8:9], mixed[:, :, :, 9:10], mixed[:, :, :, 10:11]
        square = sb("square", [P, C])
        c = Carve(weights)
        y1_all, y2_all = c.take([NT, C]), c.take([NT, C])
        x2_d = nc.dram_tensor("x2_d", (NTOK, C), F32, kind="Internal").ap()
        xn2_d = nc.dram_tensor("xn2_d", (NTOK, C), F32, kind="Internal").ap()
        y_d = nc.dram_tensor("y_d", (2 * NTOK + P, C), F32, kind="Internal").ap()

        s_zero = sem("zeros_made")
        s_x2s = sem("x2_stored")
        s_b1 = sem("biases_loaded")
        s_w = sem("first_weights_loaded")
        s_w2 = sem("second_weights_loaded")
        s_x2l = sem("x_loaded_again")
        s_wo = sem("wo_loaded")
        s_otl = [sem(f"ot_loaded{i}") for i in range(2)]
        s_t1 = sem("ot_transposed")
        s_rs = sem("sums_inverted")
        s_on = sem("o_normed")
        s_t2 = sem("on_transposed")
        s_ont = sem("on_t_ready")
        s_op = sem("o_projected")
        s_ya = sem("y_stats_step")
        s_sda = sem("y_deviation")
        s_z = sem("y_inverse")
        s_oa = sem("y_offset")
        s_yn = sem("y_normed")
        s_x2 = sem("x2_ready")
        s_xs = sem("x2_stats_step")
        s_sdb = sem("x2_deviation")
        s_rdb = sem("x2_inverse")
        s_ob = sem("x2_offset")
        s_xn2 = sem("xn2_ready")
        s_keep = [sem(f"xn2_kept{i}") for i in range(2)]
        s_sq = sem("squares_done")
        s_t3 = sem("xn2_transposed")
        s_xn2t = sem("xn2_t_ready")
        s_dot = sem("dots_done")
        s_csq = sem("cent_squared")
        s_c2 = sem("cent_norms")
        s_rt = sem("route_step")
        s_dd = sem("squared_distances")
        s_ds = sem("distances")
        s_df = sem("difference")
        s_ex = sem("difference_exp")
        s_ch = sem("choices_made")
        s_pos = sem("positions_counted")
        s_slot = sem("slots_ready")
        s_rc = sem("route_consts")
        s_yc = sem("spare_rows_cleared")
        s_bh = sem("slot_tiles_compared")
        s_nt = sem("one_hots_times_number")
        s_tn = sem("one_hots_times_tile")
        s_oh = sem("slots_compared")
        s_tb = sem("one_hots_used")
        s_ig = sem("gather_aimed")
        s_is = sem("scatter_aimed")
        s_xr = sem("x_rows_loaded")
        s_mt = sem("x_rows_transposed")
        s_mx = sem("x_t_ready")
        s_gu = sem("gate_up_ready")
        s_gb = sem("gate_biased")
        s_ub = sem("hidden_biased")
        s_si = sem("gate_done")
        s_hid = sem("hidden_ready")
        s_ht = sem("hidden_transposed")
        s_hta = sem("hidden_t_act")
        s_htd = sem("hidden_t_dve")
        s_yp = sem("expert_out_ready")
        s_yr = sem("expert_out_saved")
        s_ys = sem("expert_out_stored")
        s_gt = [sem(f"rows_gathered{i}") for i in range(8)]
        s_back = sem("rows_back")
        s_fb = sem("mix_offset")
        s_f1 = sem("first_weighed")
        s_fm = sem("mixed")
        s_fs = sem("mix_stats")
        s_fg = sem("mix_means")
        s_fd = sem("mix_deviation")
        s_fr = sem("mix_inverse")
        s_fn = sem("mix_normed")
        s_fo = sem("outputs_ready")
        s_out = sem("outputs_stored")
        passed_dve = sem("passed_dve")
        passed_pool = sem("passed_pool")
        s_const = sem("consts_made")
        s_cload = sem("consts_loaded")
        s_x = [sem("first_x_loaded"), sem("other_x_loaded")]
        s_stat = sem("stats_step")
        s_std = sem("std_ready")
        s_rstd = sem("rstd_ready")
        s_xn = sem("xn_ready")
        s_xtp = sem("xn_transposed")
        s_xt = sem("xn_t_ready")
        s_qkv = sem("qkv_ready")
        s_qk = sem("qk_biased")
        s_ra = sem("cos_done")
        s_rb = sem("sin_done")
        s_rr = sem("rope_done")
        s_hi = sem("hi_ready")
        s_r1 = sem("rest_ready")
        s_mid = sem("mid_ready")
        s_lo = sem("lo_ready")
        s_pp = sem("parts_transposed")
        s_pa = sem("parts_saved_act")
        s_pd = sem("parts_saved_dve")
        s_pst = sem("parts_stored")
        s_vst = sem("v_stored")
        s_vl = [sem(f"values_loaded{i}") for i in range(2)]
        s_stack = [sem(f"stack_loaded{i}") for i in range(3)]
        s_ones = sem("ones_made")
        s_pad = sem("padding_made")
        s_vg = sem("values_copied")
        s_mp = sem("max_scores_ready")
        s_max = sem("max_done")
        s_comb = sem("max_combined")
        s_nm = sem("max_split_step")
        s_m3 = sem("max_parts_ready")
        s_m3t = sem("max_parts_turned")
        s_mst = sem("max_parts_stored")
        s_ml = [sem(f"max_rows_loaded{j}") for j in range(HG)]
        s_sp = sem("scores_ready")
        s_exp = sem("exp_done")
        s_pv = sem("pv_done")
        s_oe = sem("o_saved")
        s_ot = sem("o_stored")

        def row(t, n):
            return t[:, bass.ds(n, 1), :].rearrange("p a c -> p (a c)")

        block = ctx.enter_context(nc.Block())
        x_v = x.rearrange("(n p) d -> p n d", p=P)

        def store_parts(sp, m):
            sp.wait_ge(s_pa, 4 * m + 4)
            sp.wait_ge(s_pd, 4 * m + 4)
            sp.dma_start(qk_scr[:, :, :, :, bass.ds(4 * P * m, 4 * P)].rearrange("s q h p t -> p (s q h) t"),
                         staged[:, bass.ds(m % 2, 1), :, :].rearrange("p a c t -> p (a c) t")).then_inc(s_pst, 16)
            sp.wait_ge(s_ra, 2 * (4 * m + 4))
            for h in range(HG):
                sp.dma_start(v_scr[bass.ds(m // 2, 1), h, :, bass.ds(4 * (m % 2), 4), :].rearrange("a p s c -> (a p) s c"),
                             v_all[:, bass.ds(4 * m, 4), HG * D * h:HG * D * (h + 1)]).then_inc(s_vst, 16)

        def load_stacks(sp, i, c):
            g, p, t = over(i, c, 1), c % 2, c % 3
            after(sp, s_sp, STEPS * (g - 2))
            for s, part_of, q in ((qs[t], Q_PART, 0), (ks[t], K_PART, 1)):
                for r in range(6):
                    src = qk_scr[part_of[r], q, bass.ds((g // 2) % 2, 1), 64 * p:64 * (p + 1), bass.ds((g // 4) * T, T)]
                    sp.dma_start(s[D * r:D * (r + 1), :, :],
                                 src.rearrange("a (j d) t -> d (a j) t", d=D)).then_inc(s_stack[t], 16)

        def load_values(sp, i, c):
            g, p = over(i, c, 1), c % 2
            after(sp, s_vg, g - 1)
            src = v_scr[bass.ds(g // 4, 1), bass.ds(g % 4, 1), :, :, :]
            sp.dma_start(v_stage[p], src.rearrange("a b p s c -> (a b p) s c")).then_inc(s_vl[p], 16)

        def load_max_rows(sp, i, c):
            g, t = over(i, c, 1), c % 3
            for j in range(HG):
                sp.wait_ge(s_m3t, HG * g + j + 1)
                sp.dma_start(m_scr[j, :, :], m3_t[:, :]).then_inc(s_mst, 16)
                sp.wait_ge(s_mst, 16 * (HG * g + j + 1))
                src = m_scr[j, :, :].rearrange("(q r) c -> r q c", q=4)[0:3 * ST]
                sp.dma_start(qs[t][QROWS:MROWS, j, :].rearrange("a (t q c) -> a t q c", q=4, c=32),
                             src.rearrange("(a t) q c -> a t q c", t=ST)).then_inc(s_ml[j], 16)

        def store_o(sp, g):
            sp.wait_ge(s_oe, 2 * g + 2)
            sp.dma_start(ot_scr[bass.ds(g, 1), :, :].rearrange("a p t -> (a p) t"), o_stage).then_inc(s_ot, 16)

        def load_w1(sp, e):
            sp.dma_start(w1_sb[:, bass.ds(e, 1), :, :].rearrange("p a k n -> p (a k) n"),
                         w1[bass.ds(e, 1), :, :].rearrange("a (k p) n -> p (a k) n", p=P)).then_inc(s_w, 16)

        def load_w2(sp, e):
            sp.dma_start(w2_sb[0:KP, bass.ds(e, 1), :, :].rearrange("p a k n -> p (a k) n"),
                         w2[bass.ds(e, 1), :, :].rearrange("a (k p) n -> p (a k) n", p=KP)).then_inc(s_w2, 16)

        def load_b1(sp, e):
            sp.dma_start(b1_sb[:, e, :], b1[e].partition_broadcast(P)).then_inc(s_b1, 16)

        @block.sync
        def _(sp):
            sp.dma_start(x_all[:, 0:8, :], x_v[:, 0:8, :]).then_inc(s_x[0], 16)
            sp.dma_start(w_qkv, wqkv.rearrange("(k p) n -> p k n", p=P)).then_inc(s_cload, 16)
            sp.dma_start(b_qkv, bqkv.partition_broadcast(P)).then_inc(s_cload, 16)
            sp.dma_start(cos_t, rope[0].rearrange("(n p) d -> p n d", p=P)).then_inc(s_cload, 16)
            sp.dma_start(sin_t, rope[1].rearrange("(n p) d -> p n d", p=P)).then_inc(s_cload, 16)
            for m in range(1, 4):
                sp.dma_start(x_all[:, 8 * m:8 * m + 8, :], x_v[:, 8 * m:8 * m + 8, :]).then_inc(s_x[1], 16)
            sp.wait_ge(s_zero, 1)
            sp.dma_start(y_d[2 * NTOK:, :], xn2[0][:, :]).then_inc(s_yc, 16)
            sp.sem_inc(s_pst, 32)
            store_parts(sp, 0)
            for m in range(1, 3):
                sp.wait_ge(s_pst, 32 + 16 * m)
                store_parts(sp, m)
            load_stacks(sp, 0, 0)
            with sp.Fori(3, NT // 4) as m:
                sp.wait_ge(s_pst, 32 + 16 * m)
                store_parts(sp, m)
            sp.wait_ge(s_pst, 32 + 16 * (NT // 4))
            sp.wait_ge(s_vst, 16 * NT)
            load_values(sp, 0, 0)
            load_values(sp, 0, 1)
            load_stacks(sp, 0, 1)
            load_stacks(sp, 0, 2)
            load_max_rows(sp, 0, 0)

            def during(i, c):
                g = over(i, c, 1)
                if not (isinstance(g, int) and g + 2 >= NG):
                    if c > 0:
                        load_stacks(sp, i, c + 2)
                    load_values(sp, i, c + 2)
                if c > 0:
                    store_o(sp, g - 1)
                if not (isinstance(g, int) and g + 1 >= NG):
                    load_max_rows(sp, i, c + 1)
                if c < 2:
                    load_w1(sp, 3 + c)
                elif c == 2:
                    load_w1(sp, i)
                elif c in (4, 6):
                    load_w2(sp, c + i)

            groups(sp, during)
            sp.wait_ge(s_sp, STEPS * (NG - 1))
            for m in range(4):
                sp.dma_start(x2[:, 8 * m:8 * m + 8, :], x_v[:, 8 * m:8 * m + 8, :]).then_inc(s_x2l, 16)
            sp.dma_start(w_o, wo.rearrange("(k p) n -> p k n", p=P)).then_inc(s_wo, 16)
            sp.dma_start(b_o, bo.rearrange("(a n) -> a n", a=1)).then_inc(s_wo, 16)
            sp.dma_start(cent_t[:, :].rearrange("p (k e) -> p k e", k=KC),
                         cent.rearrange("(k p) e -> p k e", p=P)).then_inc(s_wo, 16)

            def load_ot(n, p):
                if isinstance(n, int) and n == 2:
                    store_o(sp, NG - 1)
                if isinstance(n, int) and n == 4:
                    sp.wait_ge(s_ot, 16 * NG)
                    sp.dma_start(w2_sb[KP:KP + 1, :, 0, :], b2.rearrange("(a e) n -> a e n", a=1)).then_inc(s_w2, 16)
                if isinstance(n, int) and n in (4, 6, 8, 10):
                    load_w2(sp, n // 2 - 2)
                after(sp, s_t1, n - 1)
                src = ot_scr[bass.ds((n // TPB) * HG, HG), :, bass.ds((n % TPB) * P, P)]
                sp.dma_start(ot[p], src.rearrange("g p t -> p g t")).then_inc(s_otl[p], 16)

            def keep(n, p):
                sp.wait_ge(s_xn2, n + 1)
                sp.dma_start(xn2_d[bass.ds(n * P, P), :], xn2[p][:, :]).then_inc(s_keep[p], 16)
                if isinstance(n, int) and early <= NT - 1 - n < E:
                    load_b1(sp, NT - 1 - n)

            steps(sp, NT, [(9, keep), (0, load_ot)])
            sp.wait_ge(s_x2, NT)
            sp.dma_start(x2_d.rearrange("(n p) d -> p n d", p=P)[:, kept:, :], x2[:, kept:, :]).then_inc(s_x2s, 16)
            load_w1(sp, E - 2)
            sp.wait_ge(s_dot, NT)
            load_w1(sp, E - 1)
            sp.wait_ge(s_x2s, 16)
            for e in range(early):
                load_b1(sp, e)
            sp.wait_ge(s_slot, 1)
            load_w1(sp, E - 3)

            sp.wait_ge(s_ys, 16 * NS)
            for m in range(NT // 4):
                for c, rows in enumerate((y1_all, y2_all)):
                    sp.dma_start(rows[:, 4 * m:4 * m + 4, :],
                                 y_d[NTOK * c:NTOK * (c + 1), :].rearrange("(n p) d -> p n d", p=P)[:, 4 * m:4 * m + 4, :]
                                 ).then_inc(s_gt[m], 16)
                if 4 * m >= kept:
                    sp.dma_start(x2[:, 4 * m:4 * m + 4, :],
                                 x2_d.rearrange("(n p) d -> p n d", p=P)[:, 4 * m:4 * m + 4, :]).then_inc(s_gt[m], 16)
            for m in range(NT // 4 + 2):
                if m < NT // 4:
                    sp.wait_ge(s_gt[m], 48 if 4 * m >= kept else 32)
                    sp.sem_inc(s_back, 4)
                if m < 2:
                    continue
                m -= 2
                sp.wait_ge(s_fo, 2 * m + 2)
                sp.dma_start(out.rearrange("(n p) d -> p n d", p=P)[:, 4 * m:4 * m + 4, :],
                             y1_all[:, 4 * m:4 * m + 4, :]).then_inc(s_out, 16)
            sp.wait_ge(s_out, 16 * (NT // 4))

        @block.gpsimd
        def _(pool):
            pool.memset(xn2[0][:, :], 0.0).then_inc(s_zero, 1)
            pool.wait_ge(s_zero, 1)
            pool.memset(ident[:, :], 0.0).then_inc(s_const, 1)
            pool.memset(ident_bf[:, :], 0.0).then_inc(s_const, 1)
            pool.memset(eps[:, :], EPS).then_inc(s_const, 1)
            pool.memset(ones_f[:, :], 1.0).then_inc(s_const, 1)
            pool.wait_ge(s_const, 4)
            for m in (ident, ident_bf):
                pool.affine_select(out=m[:, :], in_=m[:, :], compare_op=ALU.not_equal, fill=1.0, base=0,
                                   pattern=[[-1, P]], channel_multiplier=1).then_inc(s_const, 1)
            pool.memset(m3[:, :], 0.0).then_inc(s_const, 1)

            def ones_of_stack(n):
                pool.memset(ks[n][QROWS:QROWS + 32, :, :], 1.0).then_inc(s_ones, 1)
                pool.wait_ge(s_ones, n + 1)

            pool.wait_ge(s_const, 7)
            ones_of_stack(0)
            for n, v in enumerate(vg):
                pool.memset(v[:, :, :, D:32], 1.0).then_inc(s_pad, 1)
                pool.wait_ge(s_pad, n + 1)

            def sines(n, p):
                if isinstance(n, int) and n == 0:
                    pool.wait_ge(s_cload, 64)
                pool.wait_ge(s_qk, n + 1)
                after(pool, s_rr, n - 1)
                src = qk[p].rearrange("p (h s d) -> p h s d", s=2, d=HALF)
                dst = rb[p].rearrange("p (h s d) -> p h s d", s=2, d=HALF)
                for s in range(2):
                    tab = sin_t[:, bass.ds(n % TPB, 1), HALF * s:HALF * (s + 1)].to_broadcast([P, 2 * H, HALF])
                    pool.tensor_tensor(dst[:, :, s, :], src[:, :, 1 - s, :], tab, ALU.mult).then_inc(s_rb, 1)

            def low(n, p):
                pool.wait_ge(s_mid, n + 1)
                pool.wait_ge(s_r1, n + 1)
                after(pool, s_pp, n - 1)
                pool.tensor_tensor(parts[p][:, 2, :], r1[p], parts[p][:, 1, :], ALU.subtract).then_inc(s_lo, 1)

            steps(pool, NT, [(7, low), (5, sines)])
            def copy_values(i, c):
                p = c % 2
                pool.wait_ge(s_vl[p], 16 * (over(i, c, 2) + 1))
                after(pool, s_pv, 2 * ST * (over(i, c, 1) - 1))
                settle(pool, passed_pool)
                pool.tensor_copy(vg[p][:, :, :, 0:D],
                                 v_stage[p].rearrange("p s (j d) -> p s j d", d=D)).then_inc(s_vg, 1)

            def split_max(g):
                for j in range(HG):
                    at = HG * g + j
                    pool.wait_ge(s_comb, at + 1)
                    after(pool, s_m3t, at)
                    settle(pool, passed_pool)
                    pool.tensor_scalar(m3[:, 0:ST], nm[:, :], -1.0, None, ALU.mult).then_inc(s_nm, 1)
                    pool.wait_ge(s_nm, 4 * at + 1)
                    pool.tensor_tensor(nr[:, :], nm[:, :], m3[:, 0:ST], ALU.add).then_inc(s_nm, 1)
                    pool.wait_ge(s_nm, 4 * at + 2)
                    settle(pool, passed_pool)
                    pool.tensor_scalar(m3[:, ST:2 * ST], nr[:, :], -1.0, None, ALU.mult).then_inc(s_nm, 1)
                    pool.wait_ge(s_nm, 4 * at + 3)
                    pool.tensor_tensor(nl[:, :], nr[:, :], m3[:, ST:2 * ST], ALU.add).then_inc(s_nm, 1)
                    pool.wait_ge(s_nm, 4 * at + 4)
                    settle(pool, passed_pool)
                    pool.tensor_scalar(m3[:, 2 * ST:3 * ST], nl[:, :], -1.0, None, ALU.mult).then_inc(s_m3, 1)

            pool.wait_ge(s_pst, 32 + 16 * (NT // 4))
            copy_values(0, 0)
            copy_values(0, 1)
            split_max(0)
            pool.wait_ge(s_m3, HG)
            ones_of_stack(1)
            ones_of_stack(2)

            def during(i, c):
                g = over(i, c, 1)
                if not (isinstance(g, int) and g + 1 >= NG):
                    split_max(g + 1)
                if not (isinstance(g, int) and g + 2 >= NG):
                    copy_values(i, c + 2)

            groups(pool, during)

            pool.wait_ge(s_ot, 16 * NG)
            made = [0]

            def const(ins):
                made[0] += 1
                ins.then_inc(s_rc, 1)
                pool.wait_ge(s_rc, made[0])

            const(pool.memset(ones_bf, 1.0))
            const(pool.memset(upper, 1.0))
            const(pool.affine_select(out=upper, in_=upper, compare_op=ALU.is_gt, fill=0.0, base=0,
                                     pattern=[[1, P]], channel_multiplier=-1))
            const(pool.iota(iota_i[:, 0:E], pattern=[[-1, E]], base=E, channel_multiplier=0))
            const(pool.tensor_copy(rev, iota_i[:, 0:E]))
            const(pool.iota(iota_i[:, 0:NT], pattern=[[P, NT]], base=0, channel_multiplier=0))
            const(pool.tensor_copy(iota128, iota_i[:, 0:NT]))
            const(pool.iota(iota_i, pattern=[[1, P]], base=0, channel_multiplier=0))
            const(pool.tensor_copy(iota_row, iota_i))
            const(pool.tensor_copy(iota_s, iota_i[:, 0:NS]))
            const(pool.iota(iota_i[:, 0:1], pattern=[[1, 1]], base=1, channel_multiplier=1))
            const(pool.tensor_copy(number, iota_i[:, 0:1]))
            const(pool.iota(iota_i[:, 0:1], pattern=[[1, 1]], base=2 * NTOK + 1, channel_multiplier=1))
            const(pool.tensor_copy(nobody, iota_i[:, 0:1]))
            def add_y(n, p):
                if isinstance(n, int) and n == 0:
                    pool.wait_ge(s_x2l, 64)
                pool.wait_ge(s_yn, n + 1)
                pool.tensor_tensor(row(x2, n), row(x2, n), yn[p], ALU.add).then_inc(s_x2, 1)

            steps(pool, NT, [(6, add_y)])

            def gather(t):
                pool.wait_ge(s_ig, t + 1)
                settle(pool, passed_pool)
                pool.indirect_dma_start(out=x_row, out_offset=None, in_=xn2_d,
                                        in_offset=bass.IndirectOffsetOnAxis(ap=at_x[:, 0:1], axis=0)).then_inc(s_xr, 16)

            def scatter(t):
                pool.wait_ge(s_is, t + 1)
                pool.wait_ge(s_yr, t + 1)
                settle(pool, passed_pool)
                pool.indirect_dma_start(out=y_d, out_offset=bass.IndirectOffsetOnAxis(ap=at_y[:, 0:1], axis=0),
                                        in_=y_row, in_offset=None).then_inc(s_ys, 16)

            for b in range(2 * NT // 4):
                pool.wait_ge(s_nt, b + 1)
                rows = in_tile[:, b % 4, :, 1, :]
                pool.tensor_tensor(rows, rows, iota_row[:, 4 * b:4 * b + 4].rearrange("p (n a) -> p n a", a=1)
                                   .to_broadcast([P, 4, NS]), ALU.mult).then_inc(s_tn, 1)
            pool.wait_ge(s_slot, 1)
            const(pool.memset(h_t[96:P, 0, :], 1.0))
            pool.wait_ge(s_yc, 16)
            pool.wait_ge(s_keep[0], 8 * NT)
            pool.wait_ge(s_keep[1], 8 * NT)
            for t in range(3):
                gather(t)
            with pool.Fori(1, NS - 2) as t:
                gather(t + 2)
                scatter(t - 1)
            for t in range(NS - 3, NS):
                scatter(t)

            def finish(u, p):
                pool.wait_ge(s_fn, 2 * u + 2)
                both = [v[:, bass.ds(2 * u, 2), :] for v in (y1_all, x2)]
                pool.tensor_tensor(both[0], both[0], both[1], ALU.add).then_inc(s_fo, 1)

            steps(pool, NT // 2, [(5, finish)])

        @block.vector
        def _(dve):

            def stats(n, p):
                if isinstance(n, int):
                    dve.wait_ge(s_x[0 if n < 8 else 1], 16 if n < 8 else 48)
                settle(dve, passed_dve)
                dve.bn_stats(stat[p], x_all[:, bass.ds(n, 1), :].rearrange("p a c -> p (a c)")).then_inc(s_stat, 1)

            def means(n, p):
                dve.wait_ge(s_stat, 2 * n + 1)
                after(dve, s_xn, n - 1)
                settle(dve, passed_dve)
                dve.bn_aggr(mv[p], stat[p]).then_inc(s_stat, 1)

            def invert(n, p):
                dve.wait_ge(s_std, n + 1)
                after(dve, s_xn, n - 1)
                dve.reciprocal(rstd[p], std[p]).then_inc(s_rstd, 1)

            def normalise(n, p):
                dve.wait_ge(s_rstd, n + 1)
                after(dve, s_xtp, n - 1)
                dve.tensor_scalar(xn[p], x_all[:, bass.ds(n, 1), :].rearrange("p a c -> p (a c)"), mv[p][:, 0:1], rstd[p], ALU.subtract, ALU.mult).then_inc(s_xn, 1)

            def biases(n, p):
                if isinstance(n, int) and n == 0:
                    dve.wait_ge(s_cload, 64)
                dve.wait_ge(s_qkv, n + 1)
                after(dve, s_rb, 2 * (n - 1))
                dve.tensor_tensor(qk[p], bank(2 + p), b_qkv[:, 0:2 * C], ALU.add).then_inc(s_qk, 1)
                dve.tensor_tensor(v_all[:, bass.ds(n, 1), :].rearrange("p a c -> p (a c)"), bank(4 + p)[:, 0:C],
                                  b_qkv[:, 2 * C:3 * C], ALU.add).then_inc(s_ra, 1)
                dve.wait_ge(s_qk, n + 1)
                after(dve, s_rr, n - 1)
                tab = cos_t[:, bass.ds(n % TPB, 1), :].to_broadcast([P, 2 * H, D])
                dve.tensor_tensor(ra[p].rearrange("p (h d) -> p h d", d=D), qk[p].rearrange("p (h d) -> p h d", d=D),
                                  tab, ALU.mult).then_inc(s_ra, 1)

            def rotate(n, p):
                dve.wait_ge(s_rb, 2 * (n + 1))
                dve.wait_ge(s_ra, 2 * (n + 1))
                after(dve, s_r1, n - 1)
                after(dve, s_hi, n - 1)
                dve.tensor_tensor(rr[p], ra[p], rb[p], ALU.add).then_inc(s_rr, 1)

            def rest(n, p):
                dve.wait_ge(s_hi, n + 1)
                after(dve, s_lo, n - 1)
                dve.tensor_tensor(r1[p], rr[p], parts[p][:, 0, :], ALU.subtract).then_inc(s_r1, 1)

            def save_parts(n, p):
                dve.wait_ge(s_pp, n + 1)
                dve.wait_ge(s_pst, 16 * (n // 4 + 1))
                dst = staged[:, bass.ds((n // 4) % 2, 1), 8:12, bass.ds((n % 4) * P, P)].rearrange("p a c t -> p (a c) t")
                dve.tensor_copy(dst, bank(7).bitcast(BF16)[:, 0:4 * P].rearrange("p (a t) -> p a t", t=P)).then_inc(s_pd, 1)

            steps(dve, NT, [(7, rest), (2, invert), (6, rotate), (5, biases), (2, normalise), (0, stats),
                            (8, save_parts), (0, means)])

            def reduce_max(g, t3, k, half):
                j, t = k // ST, k % ST
                dve.wait_ge(s_mp, 2 * (STEPS * g + k) + half + 1)
                if t == 0:
                    after(dve, s_comb, HG * (g - 1) + j + 1)
                dve.tensor_reduce(mx[:, half, j, t:t + 1], bank(4 + (t3 + 2 * k + half) % 3), AX, ALU.max).then_inc(s_max, 1)

            def combine_max(g, j):
                at = HG * g + j
                dve.wait_ge(s_max, 2 * (STEPS * g + ST * (j + 1)))
                after(dve, s_m3, at)
                dve.tensor_reduce(nm[:, :], mx[:, :, j, :].rearrange("p h t -> p t h"), AX, ALU.max).then_inc(s_comb, 1)

            def turn(g, j):
                dve.wait_ge(s_m3, HG * g + j + 1)
                after(dve, s_mst, 16 * (HG * g + j))
                dve.transpose(m3_t[:, :], m3[:, :]).then_inc(s_m3t, 1)

            def max_pass(g, t3, first=False):
                for k in range(STEPS):
                    j = k // ST - 1
                    for half in range(2):
                        reduce_max(g, t3, k, half)
                    if first and j < 0:
                        continue
                    if k % ST == 0:
                        combine_max(*((g, j) if j >= 0 else (g - 1, HG - 1)))
                    if k % ST == 2:
                        turn(*((g, j) if j >= 0 else (g - 1, HG - 1)))

            dve.wait_ge(s_pa, NT)
            max_pass(0, 0, True)

            def during(i, c):
                g = over(i, c, 1)
                if not (isinstance(g, int) and g + 1 >= NG):
                    max_pass(g + 1, (c + 1) % 3)

            groups(dve, during)
            combine_max(NG - 1, HG - 1)
            turn(NG - 1, HG - 1)


            def invert_sums(n, p):
                dve.wait_ge(s_t1, n + 1)
                v = bank(p).rearrange("p (h c) -> p h c", c=32)
                dve.reciprocal(o_sum[:, p, :].rearrange("p (h c) -> p h c", c=1), v[:, :, D:D + 1]).then_inc(s_rs, 1)

            def norm_o(n, p):
                dve.wait_ge(s_rs, n + 1)
                after(dve, s_t2, n - 1)
                v = bank(p).rearrange("p (h c) -> p h c", c=32)
                dve.tensor_tensor(on[p].rearrange("p (h d) -> p h d", d=D), v[:, :, 0:D],
                                  o_sum[:, p, :].rearrange("p (h c) -> p h c", c=1).to_broadcast([P, H, D]),
                                  ALU.mult).then_inc(s_on, 1)

            def stats_y(n, p):
                dve.wait_ge(s_op, n + 1)
                settle(dve, passed_dve)
                dve.bn_stats(st_a[:, p, :], bank(3 + p)[:, 0:C]).then_inc(s_ya, 1)

            def means_y(n, p):
                dve.wait_ge(s_ya, 2 * n + 1)
                settle(dve, passed_dve)
                dve.bn_aggr(mv_a[:, p, :], st_a[:, p, :]).then_inc(s_ya, 1)

            def invert_y(n, p):
                dve.wait_ge(s_sda, n + 1)
                after(dve, s_yn, n - 1)
                dve.reciprocal(rd_a[:, p, :], sd_a[:, p, :]).then_inc(s_z, 1)

            def offset_y(n, p):
                dve.wait_ge(s_z, n + 1)
                dve.scalar_tensor_tensor(out=off_a[:, p, :], in0=mv_a[:, p, 0:1], scalar=-1.0, in1=rd_a[:, p, :],
                                         op0=ALU.mult, op1=ALU.mult).then_inc(s_oa, 1)

            def stats_x2(n, p):
                dve.wait_ge(s_x2, n + 1)
                settle(dve, passed_dve)
                dve.bn_stats(st_b[:, p, :], row(x2, n)).then_inc(s_xs, 1)

            def means_x2(n, p):
                dve.wait_ge(s_xs, 2 * n + 1)
                settle(dve, passed_dve)
                dve.bn_aggr(mv_b[:, p, :], st_b[:, p, :]).then_inc(s_xs, 1)

            def invert_x2(n, p):
                dve.wait_ge(s_sdb, n + 1)
                after(dve, s_xn2, n - 1)
                dve.reciprocal(rd_b[:, p, :], sd_b[:, p, :]).then_inc(s_rdb, 1)

            def offset_x2(n, p):
                dve.wait_ge(s_rdb, n + 1)
                dve.scalar_tensor_tensor(out=off_b[:, p, :], in0=mv_b[:, p, 0:1], scalar=-1.0, in1=rd_b[:, p, :],
                                         op0=ALU.mult, op1=ALU.mult).then_inc(s_ob, 1)

            steps(dve, NT, [(5, invert_y), (8, invert_x2), (5, offset_y), (8, offset_x2), (4, stats_y), (7, stats_x2),
                            (1, invert_sums), (4, means_y), (7, means_x2), (1, norm_o)])

            done = [0]

            def step(ins):
                done[0] += 1
                ins.then_inc(s_rt, 1)
                dve.wait_ge(s_rt, done[0])

            def per_tile(v):
                return v.rearrange("p (n a) -> p n a", a=1).to_broadcast([P, NT, E])

            def per_expert(v, n=NT):
                return v.rearrange("p (a e) -> p a e", a=1).to_broadcast([P, n, E])

            dve.wait_ge(s_rc, 14)
            dve.wait_ge(s_dot, NT)
            dve.wait_ge(s_sq, NT)
            dve.tensor_tensor(ge[:, 0:2, :].rearrange("p k e -> p (k e)"), cent_t[:, :], cent_t[:, :], ALU.mult).then_inc(s_csq, 1)
            dve.wait_ge(s_c2, 1)
            step(dve.tensor_copy(c2, bank(7)[:, 0:E]))
            step(dve.tensor_tensor(tmp, per_tile(sq[:, :]), per_expert(c2), ALU.add))
            step(dve.scalar_tensor_tensor(out=dist, in0=bank(6)[:, 0:NT * E].rearrange("p (n e) -> p n e", e=E), scalar=-2.0,
                                          in1=tmp, op0=ALU.mult, op1=ALU.add))
            dve.tensor_scalar(tmp, dist, 1e-12, None, ALU.max).then_inc(s_dd, 1)
            dve.wait_ge(s_ds, 1)
            step(dve.tensor_reduce(v1, dist, AX, ALU.max))
            step(dve.tensor_tensor(tmp, dist, per_tile(v1), ALU.is_equal))
            step(dve.tensor_tensor(tmp, tmp, per_expert(rev), ALU.mult))
            step(dve.tensor_reduce(r_1, tmp, AX, ALU.max))
            step(dve.tensor_tensor(oh1, per_tile(r_1), per_expert(rev), ALU.is_equal))
            step(dve.tensor_scalar(oh2, oh1, -1.0, 1.0, ALU.mult, ALU.add))
            step(dve.tensor_tensor(dist, dist, oh2, ALU.mult))
            step(dve.tensor_reduce(v2, dist, AX, ALU.max))
            dve.tensor_tensor(more, v2, v1, ALU.subtract).then_inc(s_df, 1)
            step(dve.tensor_tensor(tmp, dist, per_tile(v2), ALU.is_equal))
            step(dve.tensor_tensor(tmp, tmp, per_expert(rev), ALU.mult))
            step(dve.tensor_reduce(r_1, tmp, AX, ALU.max))
            step(dve.tensor_tensor(oh2, per_tile(r_1), per_expert(rev), ALU.is_equal))
            dve.tensor_tensor(chosen.rearrange("p (n e) -> p n e", e=E), oh1, oh2, ALU.add).then_inc(s_ch, 1)
            dve.wait_ge(s_ex, 1)
            step(dve.tensor_scalar(v1, ratio, 1.0, None, ALU.add))
            step(dve.reciprocal(w_1[:, :], v1))
            step(dve.tensor_tensor(w_2[:, :], ratio, w_1[:, :], ALU.mult))
            dve.wait_ge(s_pos, 1)
            step(dve.tensor_copy(pos, bank(7)[:, 0:NT * E].rearrange("p (n e) -> p n e", e=E)))
            step(dve.tensor_copy(counts, bank(5)[:, 0:NT * E].rearrange("p (n e) -> p n e", e=E)))
            step(dve.memset(more, 1.0))
            for e in range(E):
                step(dve.tensor_tensor_scan(before[:, :, e], more, counts[:, :, e], 0.0, ALU.mult, ALU.add))
            total = before[:, NT - 1, :]
            step(dve.tensor_tensor(cmp_n, total.rearrange("p (e a) -> p e a", a=1).to_broadcast([P, E, NT]),
                                   iota128.rearrange("p (a n) -> p a n", a=1).to_broadcast([P, E, NT]), ALU.is_gt))
            step(dve.tensor_reduce(n_tiles, cmp_n, AX, ALU.add))
            step(dve.tensor_tensor_scan(first, more[:, 0:E], n_tiles, 0.0, ALU.mult, ALU.add))
            step(dve.tensor_tensor(first, first, n_tiles, ALU.subtract))
            step(dve.tensor_tensor(before, before, counts, ALU.subtract))
            step(dve.tensor_tensor(pos, pos, before, ALU.add))
            step(dve.tensor_scalar(c2, first, float(P), None, ALU.mult))
            step(dve.tensor_tensor(pos, pos, per_expert(c2), ALU.add))
            for n, oh in enumerate((oh1, oh2)):
                step(dve.tensor_tensor(tmp, pos, oh, ALU.mult))
                step(dve.tensor_reduce(low[:, n, :], tmp, AX, ALU.add))
            both = [v.rearrange("p a n -> p (a n)") for v in (high, low)]
            step(dve.tensor_scalar(both[0], both[1], 1.0 / P, (0.5 - P / 2) / P, ALU.mult, ALU.add))
            step(dve.tensor_scalar(both[0], both[0], 1.5 * 2 ** 23, None, ALU.add))
            step(dve.tensor_scalar(both[0], both[0], 1.5 * 2 ** 23, None, ALU.subtract))
            step(dve.scalar_tensor_tensor(out=both[1], in0=both[0], scalar=-float(P), in1=both[1], op0=ALU.mult, op1=ALU.add))
            step(dve.tensor_tensor(ge, iota_s.rearrange("p (s a) -> p s a", a=1).to_broadcast([P, NS, E]),
                                   per_expert(first, NS), ALU.is_ge))
            step(dve.tensor_reduce(e_of, ge, AX, ALU.add))
            step(dve.tensor_scalar(tile_e[0:1, :], e_of[0:1, :], -1.0, None, ALU.add))
            def one_hot(columns, at):
                n = columns.shape[-1]
                return (columns.rearrange("p (a s) -> p a s", a=1).to_broadcast([P, 4, n]),
                        at.rearrange("p (n a) -> p n a", a=1).to_broadcast([P, 4, n]), ALU.is_equal)

            for b in range(2 * NT // 4):
                after(dve, s_tb, b - 3)
                dve.tensor_tensor(in_tile[:, b % 4, :, 1, :], *one_hot(iota_s, both[0][:, 4 * b:4 * b + 4])).then_inc(s_bh, 1)
                dve.tensor_tensor(in_row[:, b % 4, :, :], *one_hot(iota_row, both[1][:, 4 * b:4 * b + 4])).then_inc(s_oh, 1)
            dve.wait_ge(s_tb, 2 * NT // 4)
            step(dve.tensor_scalar(e_of, bank(4)[:, NS:2 * NS], float(P), None, ALU.mult))
            step(dve.tensor_tensor(e_of, e_of, bank(4)[:, 0:NS], ALU.add))
            step(dve.tensor_scalar(place_of[:, :], e_of, 0.0, nobody, ALU.is_equal, ALU.mult))
            step(dve.scalar_tensor_tensor(out=place_of[:, :], in0=e_of, scalar=-1.0, in1=place_of[:, :],
                                          op0=ALU.add, op1=ALU.add))
            step(dve.tensor_scalar(iota_s, place_of[:, :], float(NTOK), -float(NTOK), ALU.is_ge, ALU.mult))
            step(dve.tensor_scalar(e_of, place_of[:, :], 2.0 * NTOK, -float(NTOK), ALU.is_ge, ALU.mult))
            step(dve.tensor_tensor(iota_s, iota_s, e_of, ALU.add))
            dve.tensor_tensor(token_of[:, :], place_of[:, :], iota_s, ALU.add).then_inc(s_slot, 1)
            dve.wait_ge(s_slot, 1)

            def save_xt2(t):
                dve.wait_ge(s_mt, t + 1)
                after(dve, s_gu, 4 * t)
                dve.tensor_copy(x_t.rearrange("p k t -> p (k t)"), bank(6)[:, 0:C]).then_inc(s_mx, 1)

            def biases(t, c):
                e = dve.value_load(tile_e[0:1, bass.ds(t, 1)], min_val=0, max_val=E - 1)

                def bias(at):
                    return b1_sb[:, bass.ds(e, 1), at + CH * c:at + CH * (c + 1)].rearrange("p a n -> p (a n)")

                dve.wait_ge(s_gu, 4 * t + 2 * c + 1)
                dve.tensor_tensor(gates[c], bank(2 * c)[:, 0:CH], bias(0), ALU.add).then_inc(s_gb, 1)
                dve.wait_ge(s_gu, 4 * t + 2 * c + 2)
                after(dve, s_ht, t)
                dve.tensor_tensor(hid[:, CH * c:CH * (c + 1)], bank(2 * c + 1)[:, 0:CH], bias(HID), ALU.add).then_inc(s_ub, 1)

            def multiply(t, c):
                dve.wait_ge(s_si, 2 * t + c + 1)
                dve.wait_ge(s_ub, 2 * t + c + 1)
                dve.tensor_tensor(hid[:, CH * c:CH * (c + 1)], hid[:, CH * c:CH * (c + 1)], gates[c], ALU.mult).then_inc(s_hid, 1)

            def hidden(t):
                biases(t, 0)
                multiply(t, 0)
                biases(t, 1)
                multiply(t, 1)

            def save_ht(t):
                dve.wait_ge(s_ht, t + 1)
                after(dve, s_yp, t)
                dve.tensor_copy(h_t.rearrange("p k t -> p (k t)")[0:KP, 4 * P:6 * P], bank(5)[0:KP, 0:2 * P]).then_inc(s_htd, 1)

            def aim_gather(t):
                after(dve, s_xr, 16 * t)
                dve.tensor_copy(at_x[:, :], token_of[:, bass.ds(t, 1)]).then_inc(s_ig, 1)

            def aim_scatter(t):
                after(dve, s_ys, 16 * t)
                dve.tensor_copy(at_y[:, :], place_of[:, bass.ds(t, 1)]).then_inc(s_is, 1)

            aim_gather(0)
            save_xt2(0)
            dve.wait_ge(s_b1, 16 * E)
            aim_gather(1)
            for t in range(2):
                hidden(t)
                save_xt2(t + 1)
                aim_gather(t + 2)
                if t > 0:
                    aim_scatter(t - 1)
                save_ht(t)
            with dve.Fori(2, NS - 2) as t:
                hidden(t)
                save_xt2(t + 1)
                aim_gather(t + 2)
                aim_scatter(t - 1)
                save_ht(t)
            for t in range(NS - 2, NS):
                hidden(t)
                if t + 1 < NS:
                    save_xt2(t + 1)
                aim_scatter(t - 1)
                save_ht(t)
            aim_scatter(NS - 1)

            def mix(u, p):
                for a in range(2):
                    n = 2 * u + a
                    dve.wait_ge(s_f1, n + 1)
                    dve.scalar_tensor_tensor(out=row(y1_all, n), in0=row(y2_all, n), scalar=w_2[:, bass.ds(n, 1)],
                                             in1=row(y1_all, n), op0=ALU.mult, op1=ALU.add).then_inc(s_fm, 1)

            def stats_mix(u, p):
                for a in range(2):
                    n = 2 * u + a
                    dve.wait_ge(s_fm, n + 1)
                    settle(dve, passed_dve)
                    dve.bn_stats(st_m[:, p, a, :], row(y1_all, n)).then_inc(s_fs, 1)

            def means_mix(u, p):
                after(dve, s_fb, u - 1)
                for a in range(2):
                    dve.wait_ge(s_fs, 2 * u + a + 1)
                    settle(dve, passed_dve)
                    dve.bn_aggr(mv_m[:, p, a, :], st_m[:, p, a, :]).then_inc(s_fg, 1)

            def invert_mix(u, p):
                dve.wait_ge(s_fd, u + 1)
                after(dve, s_fn, 2 * (u - 1))
                dve.reciprocal(rd_m[:, p, :, :], sd_m[:, p, :, :]).then_inc(s_fr, 1)

            def offset_mix(u, p):
                dve.wait_ge(s_fr, u + 1)
                dve.scalar_tensor_tensor(out=off_m[:, p, :, :], in0=mv_m[:, p, :, 0:1], scalar=-1.0, in1=rd_m[:, p, :, :],
                                         op0=ALU.mult, op1=ALU.mult).then_inc(s_fb, 1)

            steps(dve, NT // 2, [(1, mix), (3, invert_mix), (1, stats_mix), (3, offset_mix), (1, means_mix)])

        @block.scalar
        def _(act):
            act.wait_ge(s_const, 7)

            def deviation(n, p):
                act.wait_ge(s_stat, 2 * n + 2)
                after(act, s_rstd, n - 1)
                act.activation(std[p], mv[p][:, 1:2], ACT.Sqrt, bias=eps[:, 0:1]).then_inc(s_std, 1)

            def save_xt(n, p):
                act.wait_ge(s_xtp, n + 1)
                after(act, s_qkv, n - 1)
                act.activation(xn_t[p].rearrange("p k t -> p (k t)"), bank(p)[:, 0:C], ACT.Copy).then_inc(s_xt, 1)

            def high(n, p):
                act.wait_ge(s_rr, n + 1)
                after(act, s_pp, n - 1)
                act.activation(parts[p][:, 0, :], rr[p], ACT.Copy).then_inc(s_hi, 1)

            def middle(n, p):
                act.wait_ge(s_r1, n + 1)
                act.activation(parts[p][:, 1, :], r1[p], ACT.Copy).then_inc(s_mid, 1)

            def save_parts(n, p):
                act.wait_ge(s_pp, n + 1)
                src = bank(6).bitcast(BF16).rearrange("p (a t) -> p a t", t=P)
                act.wait_ge(s_pst, 16 * (n // 4 + 1))
                dst = staged[:, bass.ds((n // 4) % 2, 1), 0:8, bass.ds((n % 4) * P, P)].rearrange("p a c t -> p (a c) t")
                act.activation(dst, src, ACT.Copy).then_inc(s_pa, 1)

            steps(act, NT, [(7, middle), (3, save_xt), (6, high), (8, save_parts), (1, deviation)])

            def group(i, c):
                g, first = over(i, c, 1), c == 0
                for k in range(STEPS):
                    u, pair = k // 2, k % 2
                    act.wait_ge(s_sp, STEPS * g + k + 1)
                    if pair == 0 and not (first and u < 4):
                        act.wait_ge(s_pv, UNITS * g + u - 3)
                    act.activation(pt[u % 4][:, 2 * pair:2 * pair + 2, :].rearrange("p a t -> p (a t)"),
                                   bank(2 * pair, 2), ACT.Exp, scale=SC).then_inc(s_exp, 1)
                    if k == 1 and not first:
                        save_o(g - 1, 1)
                    if k == STEPS // 2 + 1:
                        save_o(g, 0)

            def save_o(g, half):
                act.wait_ge(s_pv, UNITS * g + ST * (half + 1))
                if half == 0:
                    after(act, s_ot, 16 * g)
                act.activation(o_stage[:, 512 * half:512 * (half + 1)], bank(7), ACT.Copy).then_inc(s_oe, 1)

            groups(act, group)
            save_o(NG - 1, 1)

            def save_ont(n, p):
                act.wait_ge(s_t2, n + 1)
                after(act, s_op, n - 1)
                act.activation(on_t[p].rearrange("p k t -> p (k t)"), bank(2)[:, 0:C], ACT.Copy).then_inc(s_ont, 1)

            def deviation_y(n, p):
                act.wait_ge(s_ya, 2 * n + 2)
                after(act, s_z, n - 1)
                act.activation(sd_a[:, p, :], mv_a[:, p, 1:2], ACT.Sqrt, bias=eps[:, 0:1]).then_inc(s_sda, 1)

            def norm_y(n, p):
                act.wait_ge(s_oa, n + 1)
                after(act, s_x2, n - 1)
                act.activation(yn[p], bank(3 + p)[:, 0:C], ACT.Identity, bias=off_a[:, p, :],
                               scale=rd_a[:, p, :]).then_inc(s_yn, 1)

            def deviation_x2(n, p):
                act.wait_ge(s_xs, 2 * n + 2)
                after(act, s_rdb, n - 1)
                act.activation(sd_b[:, p, :], mv_b[:, p, 1:2], ACT.Sqrt, bias=eps[:, 0:1]).then_inc(s_sdb, 1)

            def norm_x2(n, p):
                if isinstance(n, int) and n == 0:
                    act.wait_ge(s_yc, 16)
                act.wait_ge(s_ob, n + 1)
                after(act, s_keep[p], 8 * (n - p))
                after(act, s_sq, n - 1)
                after(act, s_t3, n - 1)
                act.activation(xn2[p][:, :], row(x2, n), ACT.Identity, bias=off_b[:, p, :],
                               scale=rd_b[:, p, :]).then_inc(s_xn2, 1)

            def squares(n, p):
                act.wait_ge(s_xn2, n + 1)
                after(act, s_sq, n)
                act.activation(square[:, :], xn2[p][:, :], ACT.Square, accum_out=sq[:, bass.ds(n, 1)]).then_inc(s_sq, 1)

            def save_xn2t(n, p):
                act.wait_ge(s_t3, n + 1)
                after(act, s_dot, n - 1)
                act.activation(xn2_t[p].rearrange("p k t -> p (k t)"), bank(5)[:, 0:C], ACT.Copy).then_inc(s_xn2t, 1)

            steps(act, NT, [(5, norm_y), (8, norm_x2), (4, deviation_y), (7, deviation_x2), (9, save_xn2t), (9, squares),
                            (2, save_ont)])

            act.wait_ge(s_dd, 1)
            act.activation(dist, tmp, ACT.Sqrt).then_inc(s_ds, 1)
            act.wait_ge(s_df, 1)
            act.activation(ratio, more, ACT.Exp).then_inc(s_ex, 1)

            act.wait_ge(s_rc, 14)
            for b in range(2 * NT // 4):
                act.wait_ge(s_bh, b + 1)
                act.activation(in_tile[:, b % 4, :, 0, :], in_tile[:, b % 4, :, 1, :], ACT.Copy, scale=number).then_inc(s_nt, 1)

            def gate(t):
                for c in range(2):
                    act.wait_ge(s_gb, 2 * t + c + 1)
                    act.activation(gates[c], gates[c], ACT.Silu).then_inc(s_si, 1)

            def save_y(t):
                act.wait_ge(s_yp, t + 1)
                after(act, s_ys, 16 * t)
                act.activation(y_row, bank(7)[:, 0:C], ACT.Copy).then_inc(s_yr, 1)

            def save_ht(t):
                act.wait_ge(s_ht, t + 1)
                after(act, s_yp, t)
                act.activation(h_t.rearrange("p k t -> p (k t)")[0:KP, 0:4 * P], bank(4)[0:KP, :], ACT.Copy).then_inc(s_hta, 1)

            gate(0)
            save_ht(0)
            gate(1)
            save_y(0)
            save_ht(1)
            with act.Fori(2, NS) as t:
                gate(t)
                save_y(t - 1)
                save_ht(t)
            save_y(NS - 1)

            def weigh_first(u, p):
                for a in range(2):
                    n = 2 * u + a
                    act.wait_ge(s_back, n + 1)
                    act.activation(row(y1_all, n), row(y1_all, n), ACT.Copy, scale=w_1[:, bass.ds(n, 1)]).then_inc(s_f1, 1)

            def deviation_mix(u, p):
                act.wait_ge(s_fg, 2 * u + 2)
                act.activation(sd_m[:, p, :, :], mv_m[:, p, :, 1:2], ACT.Sqrt, bias=eps[:, 0:1]).then_inc(s_fd, 1)

            def norm_mix(u, p):
                act.wait_ge(s_fb, u + 1)
                for a in range(2):
                    n = 2 * u + a
                    act.activation(row(y1_all, n), row(y1_all, n), ACT.Identity, bias=off_m[:, p, a, :],
                                   scale=rd_m[:, p, a, :]).then_inc(s_fn, 1)

            steps(act, NT // 2, [(2, deviation_mix), (0, weigh_first), (4, norm_mix)])

        @block.tensor
        def _(pe):
            pe.wait_ge(s_const, 7)
            pe.wait_ge(s_cload, 64)

            def turn_x(n, p):
                pe.wait_ge(s_xn, n + 1)
                after(pe, s_xt, n - 1)
                for k in range(KC):
                    last = pe.transpose(bank(p)[:, P * k:P * (k + 1)], xn[p][:, P * k:P * (k + 1)], ident[:, :])
                last.then_inc(s_xtp, 1)

            def project(n, p):
                pe.wait_ge(s_xt, n + 1)
                after(pe, s_qk, n - 1)
                after(pe, s_ra, 2 * (n - 1))
                for k in range(KC):
                    pe.matmul(bank(2 + p), xn_t[p][:, k, :], w_qkv[:, k, 0:2 * C], start=k == 0, stop=k == KC - 1)
                for k in range(KC):
                    last = pe.matmul(bank(4 + p)[:, 0:C], xn_t[p][:, k, :], w_qkv[:, k, 2 * C:3 * C],
                                     start=k == 0, stop=k == KC - 1)
                last.then_inc(s_qkv, 1)

            def turn_parts(n, p):
                pe.wait_ge(s_lo, n + 1)
                after(pe, s_pa, n)
                after(pe, s_pd, n)
                for a in range(12):
                    dst = bank(6, 2).bitcast(BF16)[:, P * a:P * (a + 1)]
                    last = pe.transpose(dst, parts[p].rearrange("p s c -> p (s c)")[:, P * a:P * (a + 1)], ident_bf[:, :])
                last.then_inc(s_pp, 1)

            steps(pe, NT, [(8, turn_parts), (3, turn_x), (4, project)])

            def max_scores(g, t3, k, half):
                j, t = k // ST, k % ST
                piece = 2 * k + half
                after(pe, s_max, 2 * STEPS * g + piece - 2)
                pe.matmul(bank(4 + (t3 + piece) % 3), qs[t3][0:QROWS, j, P * t:P * (t + 1)],
                          ks[t3][0:QROWS, j, 512 * half:512 * (half + 1)], start=True, stop=True).then_inc(s_mp, 1)

            def scores(g, t3, k):
                half, st, pair = k // UNITS, k // 2 % ST, k % 2
                after(pe, s_exp, STEPS * g + k - 1)
                for j in (2 * pair, 2 * pair + 1):
                    if k < 2:
                        pe.wait_ge(s_ml[j], 16 * (g + 1))
                    last = pe.matmul(bank(j), ks[t3][0:MROWS, j, P * st:P * (st + 1)],
                                     qs[t3][0:MROWS, j, 512 * half:512 * (half + 1)], start=True, stop=True)
                last.then_inc(s_sp, 1)

            def weigh(g, p, u):
                half, st = u // ST, u % ST
                pe.wait_ge(s_exp, STEPS * g + 2 * u + 2)
                if st == 0:
                    if half == 0:
                        pe.wait_ge(s_vg, g + 1)
                    after(pe, s_oe, 2 * g + half)
                for j in range(HG):
                    last = pe.matmul(bank(7)[32 * j:32 * (j + 1), :], vg[p][:, st, j, :],
                                     pt[u % 4][:, j, :], start=st == 0, stop=st == ST - 1,
                                     tile_position=(0, 32 * j))
                last.then_inc(s_pv, 1)

            def group(i, c):
                g, p, t3 = over(i, c, 1), c % 2, c % 3
                if c in (1, 2):
                    pe.wait_ge(s_ones, c + 1)
                for k in range(STEPS):
                    ahead, m = 1 + (k + LEAD) // STEPS, (k + LEAD) % STEPS
                    more = not (isinstance(g, int) and g + ahead >= NG)
                    if more:
                        if m == 0:
                            pe.wait_ge(s_stack[(c + ahead) % 3], STACK_DMAS * (over(i, c + ahead, 3) + 1))
                        max_scores(g + ahead, (c + ahead) % 3, m, 0)
                    scores(g, t3, k)
                    if more:
                        max_scores(g + ahead, (c + ahead) % 3, m, 1)
                    if k % 2 == 1 and k >= 3:
                        weigh(g, p, k // 2 - 1)
                    elif k == 1 and c > 0:
                        weigh(g - 1, 1 - p, UNITS - 1)

            pe.wait_ge(s_qk, NT)
            pe.wait_ge(s_ra, 2 * NT)
            pe.wait_ge(s_pa, NT)
            for g in range(2):
                pe.wait_ge(s_stack[g], STACK_DMAS)
                for k in range([STEPS, LEAD][g]):
                    for half in range(2):
                        max_scores(g, g, k, half)
            pe.wait_ge(s_pd, NT)
            pe.wait_ge(s_ones, 1)
            pe.wait_ge(s_pad, 2)
            groups(pe, group)
            weigh(NG - 1, 1, UNITS - 1)

            pe.wait_ge(s_wo, 48)
            pe.wait_ge(s_oe, 2 * NG)
            pe.wait_ge(s_exp, STEPS * NG)
            pe.wait_ge(s_max, 2 * STEPS * NG)

            def turn_ot(n, p):
                pe.wait_ge(s_otl[p], 8 * (n + (2 - p)))
                after(pe, s_on, n - 1)
                for k in range(HG):
                    last = pe.transpose(bank(p)[:, P * k:P * (k + 1)], ot[p][:, k, :], ident[:, :])
                last.then_inc(s_t1, 1)

            def turn_on(n, p):
                pe.wait_ge(s_on, n + 1)
                after(pe, s_ont, n)
                for k in range(KC):
                    last = pe.transpose(bank(2)[:, P * k:P * (k + 1)], on[p][:, P * k:P * (k + 1)], ident[:, :])
                last.then_inc(s_t2, 1)

            def project_o(n, p):
                pe.wait_ge(s_ont, n + 1)
                after(pe, s_yn, n - 1)
                pe.matmul(bank(3 + p)[:, 0:C], ones_f[0:1, :], b_o, start=True, stop=False)
                for k in range(KC):
                    last = pe.matmul(bank(3 + p)[:, 0:C], on_t[p][:, k, :], w_o[:, k, :], start=False, stop=k == KC - 1)
                last.then_inc(s_op, 1)

            def turn_xn2(n, p):
                pe.wait_ge(s_xn2, n + 1)
                after(pe, s_xn2t, n)
                for k in range(KC):
                    last = pe.transpose(bank(5)[:, P * k:P * (k + 1)], xn2[p][:, P * k:P * (k + 1)], ident[:, :])
                last.then_inc(s_t3, 1)

            def dots(n, p):
                pe.wait_ge(s_xn2t, n + 1)
                for k in range(KC):
                    last = pe.matmul(bank(6)[:, bass.ds(n * E, E)], xn2_t[p][:, k, :], cent_t[:, E * k:E * (k + 1)],
                                     start=k == 0, stop=k == KC - 1)
                last.then_inc(s_dot, 1)

            steps(pe, NT, [(10, dots), (9, turn_xn2), (2, turn_on), (0, turn_ot), (3, project_o)])

            pe.wait_ge(s_csq, 1)
            for k in range(KC):
                last = pe.matmul(bank(7)[:, 0:E], ones_f[:, :], ge[:, k, :], start=k == 0, stop=k == KC - 1)
            last.then_inc(s_c2, 1)
            pe.wait_ge(s_ch, 1)
            pe.matmul(bank(7)[:, 0:NT * E], upper, chosen, start=True, stop=True)
            pe.matmul(bank(5)[:, 0:NT * E], ones_bf, chosen, start=True, stop=True).then_inc(s_pos, 1)
            for b in range(2 * NT // 4):
                pe.wait_ge(s_oh, b + 1)
                pe.wait_ge(s_tn, b + 1)
                for n in range(4):
                    last = pe.matmul(bank(4)[:, 0:2 * NS], in_row[:, b % 4, n, :],
                                     in_tile[:, b % 4, n, :, :].rearrange("p a s -> p (a s)"),
                                     start=b + n == 0, stop=(b, n) == (2 * NT // 4 - 1, 3))
                last.then_inc(s_tb, 1)

            def turn_rows(t):
                pe.wait_ge(s_xr, 16 * (t + 1))
                after(pe, s_mx, t)
                for k in range(KC):
                    last = pe.transpose(bank(6)[:, P * k:P * (k + 1)], x_row[:, P * k:P * (k + 1)], ident[:, :])
                last.then_inc(s_mt, 1)

            def expert(t):
                return pe.value_load(tile_e[0:1, bass.ds(t, 1)], min_val=0, max_val=E - 1)

            def gate_up(t, e):
                pe.wait_ge(s_mx, t + 1)
                for c in range(4):
                    col = (c % 2) * HID + (c // 2) * CH
                    after(pe, (s_gb, s_ub)[c % 2], 2 * (t - 1) + c // 2 + 1)
                    dst = bank(c)[:, 0:CH]
                    for k in range(KC):
                        last = pe.matmul(dst, x_t[:, k, :],
                                         w1_sb[:, bass.ds(e, 1), k, col:col + CH].rearrange("p a n -> p (a n)"),
                                         start=k == 0, stop=k == KC - 1)
                    last.then_inc(s_gu, 1)

            def turn_hidden(t):
                pe.wait_ge(s_hid, 2 * t + 2)
                after(pe, s_hta, t)
                after(pe, s_htd, t)
                for k in range(KH):
                    last = pe.transpose(bank(4, 2)[0:KP, P * k:P * (k + 1)], hid[:, KP * k:KP * (k + 1)], ident[:, :])
                last.then_inc(s_ht, 1)

            def down(t, e):
                pe.wait_ge(s_hta, t + 1)
                pe.wait_ge(s_htd, t + 1)
                after(pe, s_yr, t)
                for k in range(KH):
                    rows = KP + 1 if k == 0 else KP
                    last = pe.matmul(bank(7)[:, 0:C], h_t[0:rows, k, :],
                                     w2_sb[0:rows, bass.ds(e, 1), k, :].rearrange("p a n -> p (a n)"),
                                     start=k == 0, stop=k == KH - 1)
                last.then_inc(s_yp, 1)

            pe.wait_ge(s_slot, 1)
            pe.wait_ge(s_w, 16 * E)
            pe.wait_ge(s_w2, 16 * (E + 1))
            turn_rows(0)
            gate_up(0, expert(0))
            turn_rows(1)
            turn_hidden(0)
            gate_up(1, expert(1))
            turn_rows(2)
            down(0, expert(0))
            turn_hidden(1)
            with pe.Fori(2, NS - 1) as t:
                gate_up(t, expert(t))
                turn_rows(t + 1)
                down(t - 1, expert(t - 1))
                turn_hidden(t)
            gate_up(NS - 1, expert(NS - 1))
            down(NS - 2, expert(NS - 2))
            turn_hidden(NS - 1)
            down(NS - 1, expert(NS - 1))


def layout(inputs):
    g = {k.replace("L0_", ""): np.asarray(v) for k, v in inputs.items()}
    half = np.arange(HALF, dtype=np.float32)
    theta = np.power(np.float32(10000.0), -half / np.float32(HALF)).astype(np.float32)
    freqs = np.arange(T, dtype=np.float32)[:, None] * theta[None, :]
    cos, sin = np.cos(freqs).astype(np.float32), np.sin(freqs).astype(np.float32)
    rope = np.stack([np.concatenate([cos, cos], 1), np.concatenate([-sin, sin], 1)])
    return {
        "x": g["attn_x"].reshape(NTOK, C),
        "wqkv": np.concatenate([g["attn_Wq"].T, g["attn_Wk"].T, g["attn_Wv"].T], axis=1),
        "bqkv": np.concatenate([g["attn_bq"], g["attn_bk"], g["attn_bv"]]),
        "wo": g["attn_Wo"].T,
        "bo": g["attn_bo"],
        "rope": rope,
        "cent": g["ffn_centroid"].T,
        "w1": np.concatenate([g["ffn_Wg"], g["ffn_W1"]], axis=2),
        "b1": np.concatenate([g["ffn_bg"], g["ffn_b1"]], axis=1),
        "w2": g["ffn_W2"],
        "b2": g["ffn_b2"],
    }


def kernel(**inputs):
    import concourse.bacc as bacc
    from concourse.bass_utils import run_bass_kernel_spmd

    nc = bacc.Bacc("TRN2", target_bir_lowering=False, num_devices=1,
                   dynamic_dma_scratch_size=8192)
    arrays, args = {}, []
    for name, a in layout(inputs).items():
        a = np.ascontiguousarray(a)
        arrays[f"in_{name}"] = a
        args.append(nc.dram_tensor(f"in_{name}", a.shape, mybir.dt.from_np(a.dtype), kind="ExternalInput").ap())
    args.append(nc.dram_tensor("out_x", (NTOK, C), F32, kind="ExternalOutput").ap())
    build(nc, *args)
    r = run_bass_kernel_spmd(nc, [arrays], core_ids=[0])
    return np.asarray(r.results[0]["out_x"]).reshape(B, T, C)
```
